# Optimizing a Trainium2 kernel written in Bass

```python
import numpy as np
import jax
import jax.numpy as jnp

def _softmax(x, axis=-1):
    return jax.nn.softmax(x, axis=axis)

def _gelu(x):
    return jax.nn.gelu(x, approximate=True)

def _silu(x):
    return jax.nn.silu(x)

def _sigmoid(x):
    return jax.nn.sigmoid(x)

def _layernorm(x, axis=-1, eps=1e-05):
    m = jnp.mean(x, axis=axis, keepdims=True)
    v = jnp.var(x, axis=axis, keepdims=True)
    return (x - m) / jnp.sqrt(v + eps)

def _scatter_add(tgt, idx, src, axis=0):
    return tgt.at[idx].add(src)

def _segment_sum(src, seg, n):
    return jax.ops.segment_sum(src, seg, n)
kernel_name = 'mk_flamingo_gated_d2_seqx_r8_8a2b3d'

def setup_inputs(seed: int=0):
    np.random.seed(seed)
    _w = jnp.asarray

    def _rec_inputs():
        import jax
        import jax.numpy as jnp
        _rk = jax.random.key(seed)
        x = 7.22e-05 + 1 * jax.random.normal(jax.random.fold_in(_rk, 1), (16, 64, 256), jnp.float32)
        _lenS = 64 - jax.random.randint(jax.random.fold_in(_rk, 7), (16,), 0, max(1, 64 // 4) + 1, jnp.int32)
        _lenS2 = 64 - jax.random.randint(jax.random.fold_in(_rk, 8), (16,), 0, max(1, 64 // 4) + 1, jnp.int32)
        _ctx_1024P = jax.random.normal(jax.random.fold_in(_rk, 11), (16, 16, 128), jnp.float32)
        _ctx_1024c = jax.random.dirichlet(jax.random.fold_in(_rk, 511), 0.3 * jnp.ones((16,), jnp.float32), (16, 64))
        _ctx_1024t = jnp.einsum('bsk,bkd->bsd', _ctx_1024c, _ctx_1024P)
        _ctx_1024t = _ctx_1024t * jax.lax.rsqrt(jnp.mean(jnp.square(_ctx_1024t)) + 1e-12) * 0.953939
        ctx_1024 = -0.000673644 + 1.00013 * (_ctx_1024t + 0.3 * jax.random.normal(jax.random.fold_in(_rk, 611), (16, 64, 128), jnp.float32))
        _validS = jnp.arange(64)[None, :] < _lenS[:, None]
        _validS2 = jnp.arange(64)[None, :] < _lenS2[:, None]
        _causal = jnp.tril(jnp.ones((64, 64), dtype=bool))
        mask_BxS2_bf1 = jnp.ones((16, 64), dtype=bool)
        _g = jax.random.normal(jax.random.fold_in(_rk, 9001), (2, 2), jnp.float32)
        _g = jnp.sign(_g) * jnp.maximum(jnp.abs(_g), 1.0) + (_g == 0) * 1.0
        g_xattn = _g[0]
        g_ffn = _g[1]
        return (x, ctx_1024, mask_BxS2_bf1, g_xattn, g_ffn)
    x, ctx_1024, mask_BxS2_bf1, g_xattn, g_ffn = _rec_inputs()

    def _L0_xattn_setup():
        import jax, jax.numpy as jnp
        import numpy as np
        B, S1, S2, DCA = (2, 256, 128, 16)
        QDIM, KDIM, H = (256, 128, 16)
        HD = QDIM // H
        SCALE = HD ** (-0.5)
        EPS = 1e-06
        DCA_WEIGHT = 1.0

        def _ln(t, w, b):
            m = jnp.mean(t, axis=-1, keepdims=True)
            v = jnp.var(t, axis=-1, keepdims=True)
            return (t - m) * jax.lax.rsqrt(v + EPS) * w + b

        def _attn(q, k, v):
            s = jnp.einsum('bhqd,bhkd->bhqk', q, k) * SCALE
            p = jax.nn.softmax(s, axis=-1)
            return jnp.einsum('bhqk,bhkd->bhqd', p, v)
        key = jax.random.key(seed)
        ks = jax.random.split(key, 8)
        w = lambda k, shape: jax.random.normal(k, shape, jnp.float32) * 0.02
        return {'x': jax.random.normal(ks[0], (B, S1, QDIM), jnp.float32), 'y': jax.random.normal(ks[1], (B, S2 + DCA, KDIM), jnp.float32), 'Wq': w(ks[2], (QDIM, QDIM)), 'bq': jnp.zeros((QDIM,), jnp.float32), 'Wk': w(ks[3], (KDIM, QDIM)), 'bk': jnp.zeros((QDIM,), jnp.float32), 'Wv': w(ks[4], (KDIM, QDIM)), 'bv': jnp.zeros((QDIM,), jnp.float32), 'Wkv_dca': w(ks[5], (KDIM, 2 * QDIM)), 'bkv_dca': jnp.zeros((2 * QDIM,), jnp.float32), 'qn_w': jnp.ones((HD,), jnp.float32), 'qn_b': jnp.zeros((HD,), jnp.float32), 'kn_w': jnp.ones((HD,), jnp.float32), 'kn_b': jnp.zeros((HD,), jnp.float32), 'kn_dca_w': jnp.ones((HD,), jnp.float32), 'kn_dca_b': jnp.zeros((HD,), jnp.float32), 'Wo': w(ks[6], (QDIM, QDIM)), 'bo': jnp.zeros((QDIM,), jnp.float32)}
    _L0_xattn_all = _L0_xattn_setup()
    _L0_xattn_in = {k: v for k, v in _L0_xattn_all.items() if k in ('Wq', 'bq', 'Wk', 'bk', 'Wv', 'bv', 'Wkv_dca', 'bkv_dca', 'qn_w', 'qn_b', 'kn_w', 'kn_b', 'kn_dca_w', 'kn_dca_b', 'Wo', 'bo')}
    del _L0_xattn_all

    def _L0_ffn_setup():
        import jax, jax.numpy as jnp
        import numpy as np
        B, S, D = (1, 256, 256)
        F = 64
        E = 16
        K = 4

        def _swiglu(x, wg, wu, wd):
            return jax.nn.silu(x @ wg) * (x @ wu) @ wd
        key = jax.random.key(seed)
        ks = jax.random.split(key, 10)
        s = 0.02
        return {'hidden_states': jax.random.normal(ks[0], (B, S, D), dtype=jnp.float32), 'gate_w': jax.random.normal(ks[1], (E, D), dtype=jnp.float32) * s, 'Wg': jax.random.normal(ks[2], (E, D, F), dtype=jnp.float32) * s, 'Wu': jax.random.normal(ks[3], (E, D, F), dtype=jnp.float32) * s, 'Wd': jax.random.normal(ks[4], (E, F, D), dtype=jnp.float32) * s, 'sWg': jax.random.normal(ks[5], (D, F), dtype=jnp.float32) * s, 'sWu': jax.random.normal(ks[6], (D, F), dtype=jnp.float32) * s, 'sWd': jax.random.normal(ks[7], (F, D), dtype=jnp.float32) * s, 'shared_gate_w': jax.random.normal(ks[8], (D, 1), dtype=jnp.float32) * s}
    _L0_ffn_all = _L0_ffn_setup()
    _L0_ffn_in = {k: v for k, v in _L0_ffn_all.items() if k in ('gate_w', 'Wg', 'Wu', 'Wd', 'sWg', 'sWu', 'sWd', 'shared_gate_w')}
    del _L0_ffn_all

    def _L1_xattn_setup():
        import jax, jax.numpy as jnp
        import numpy as np
        N_HEADS = 16
        N_KV_HEADS = 8
        HEAD_DIM = 128
        D_TEXT = 256
        D_VISION = 128
        GROUPS = N_HEADS // N_KV_HEADS
        key = jax.random.key(seed)
        ks = jax.random.split(key, 6)
        B, T_text, T_vis = (4, 256, 72)
        text_hidden = jax.random.normal(ks[0], (B, T_text, D_TEXT), dtype=jnp.float32)
        vision_tokens = jax.random.normal(ks[1], (B, T_vis, D_VISION), dtype=jnp.float32)
        vision_mask = jnp.ones((B, T_vis), dtype=bool)
        s = 0.02
        Wq = jax.random.normal(ks[2], (D_TEXT, N_HEADS * HEAD_DIM), dtype=jnp.float32) * s
        Wk = jax.random.normal(ks[3], (D_VISION, N_KV_HEADS * HEAD_DIM), dtype=jnp.float32) * s
        Wv = jax.random.normal(ks[4], (D_VISION, N_KV_HEADS * HEAD_DIM), dtype=jnp.float32) * s
        Wo = jax.random.normal(ks[5], (N_HEADS * HEAD_DIM, D_TEXT), dtype=jnp.float32) * s
        return {'text_hidden': text_hidden, 'vision_tokens': vision_tokens, 'vision_mask': vision_mask, 'Wq': Wq, 'Wk': Wk, 'Wv': Wv, 'Wo': Wo}
    _L1_xattn_all = _L1_xattn_setup()
    _L1_xattn_in = {k: v for k, v in _L1_xattn_all.items() if k in ('Wq', 'Wk', 'Wv', 'Wo')}
    del _L1_xattn_all

    def _L1_ffn_setup():
        import jax, jax.numpy as jnp
        import numpy as np
        HIDDEN = 256
        INTER = 688
        LUT_SIZE = 16

        def _ghost_linear(x, idx, lut):
            w = lut[idx]
            return jnp.einsum('bsh,oh->bso', x, w)
        key = jax.random.key(seed)
        k_x, k_lut, k_g, k_u, k_d = jax.random.split(key, 5)
        x = jax.random.normal(k_x, (2, 512, HIDDEN), dtype=jnp.float32)
        lut = jax.random.normal(k_lut, (LUT_SIZE,), dtype=jnp.float32) * 0.02
        gate_idx = jax.random.randint(k_g, (INTER, HIDDEN), 0, LUT_SIZE, dtype=jnp.int32)
        up_idx = jax.random.randint(k_u, (INTER, HIDDEN), 0, LUT_SIZE, dtype=jnp.int32)
        down_idx = jax.random.randint(k_d, (HIDDEN, INTER), 0, LUT_SIZE, dtype=jnp.int32)
        return {'x': x, 'lut': lut, 'gate_idx': gate_idx, 'up_idx': up_idx, 'down_idx': down_idx}
    _L1_ffn_all = _L1_ffn_setup()
    _L1_ffn_in = {k: v for k, v in _L1_ffn_all.items() if k in ('lut', 'gate_idx', 'up_idx', 'down_idx')}
    del _L1_ffn_all
    return {'x': x, 'ctx_1024': ctx_1024, 'mask_BxS2_bf1': mask_BxS2_bf1, 'g_xattn': g_xattn, 'g_ffn': g_ffn, 'L0_xattn_Wq': _L0_xattn_in['Wq'], 'L0_xattn_bq': _L0_xattn_in['bq'], 'L0_xattn_Wk': _L0_xattn_in['Wk'], 'L0_xattn_bk': _L0_xattn_in['bk'], 'L0_xattn_Wv': _L0_xattn_in['Wv'], 'L0_xattn_bv': _L0_xattn_in['bv'], 'L0_xattn_Wkv_dca': _L0_xattn_in['Wkv_dca'], 'L0_xattn_bkv_dca': _L0_xattn_in['bkv_dca'], 'L0_xattn_qn_w': _L0_xattn_in['qn_w'], 'L0_xattn_qn_b': _L0_xattn_in['qn_b'], 'L0_xattn_kn_w': _L0_xattn_in['kn_w'], 'L0_xattn_kn_b': _L0_xattn_in['kn_b'], 'L0_xattn_kn_dca_w': _L0_xattn_in['kn_dca_w'], 'L0_xattn_kn_dca_b': _L0_xattn_in['kn_dca_b'], 'L0_xattn_Wo': _L0_xattn_in['Wo'], 'L0_xattn_bo': _L0_xattn_in['bo'], 'L0_ffn_gate_w': _L0_ffn_in['gate_w'], 'L0_ffn_Wg': _L0_ffn_in['Wg'], 'L0_ffn_Wu': _L0_ffn_in['Wu'], 'L0_ffn_Wd': _L0_ffn_in['Wd'], 'L0_ffn_sWg': _L0_ffn_in['sWg'], 'L0_ffn_sWu': _L0_ffn_in['sWu'], 'L0_ffn_sWd': _L0_ffn_in['sWd'], 'L0_ffn_shared_gate_w': _L0_ffn_in['shared_gate_w'], 'L1_xattn_Wq': _L1_xattn_in['Wq'], 'L1_xattn_Wk': _L1_xattn_in['Wk'], 'L1_xattn_Wv': _L1_xattn_in['Wv'], 'L1_xattn_Wo': _L1_xattn_in['Wo'], 'L1_ffn_lut': _L1_ffn_in['lut'], 'L1_ffn_gate_idx': _L1_ffn_in['gate_idx'], 'L1_ffn_up_idx': _L1_ffn_in['up_idx'], 'L1_ffn_down_idx': _L1_ffn_in['down_idx']}

def reference(x, ctx_1024, mask_BxS2_bf1, g_xattn, g_ffn, L0_xattn_Wq, L0_xattn_bq, L0_xattn_Wk, L0_xattn_bk, L0_xattn_Wv, L0_xattn_bv, L0_xattn_Wkv_dca, L0_xattn_bkv_dca, L0_xattn_qn_w, L0_xattn_qn_b, L0_xattn_kn_w, L0_xattn_kn_b, L0_xattn_kn_dca_w, L0_xattn_kn_dca_b, L0_xattn_Wo, L0_xattn_bo, L0_ffn_gate_w, L0_ffn_Wg, L0_ffn_Wu, L0_ffn_Wd, L0_ffn_sWg, L0_ffn_sWu, L0_ffn_sWd, L0_ffn_shared_gate_w, L1_xattn_Wq, L1_xattn_Wk, L1_xattn_Wv, L1_xattn_Wo, L1_ffn_lut, L1_ffn_gate_idx, L1_ffn_up_idx, L1_ffn_down_idx):
    import jax
    import jax.numpy as jnp

    def _L0_xattn_ref(x, y, Wq, bq, Wk, bk, Wv, bv, Wkv_dca, bkv_dca, qn_w, qn_b, kn_w, kn_b, kn_dca_w, kn_dca_b, Wo, bo):
        import jax, jax.numpy as jnp
        import numpy as np
        B, S1, S2, DCA = (2, 256, 128, 16)
        QDIM, KDIM, H = (256, 128, 16)
        HD = QDIM // H
        SCALE = HD ** (-0.5)
        EPS = 1e-06
        DCA_WEIGHT = 1.0

        def _ln(t, w, b):
            m = jnp.mean(t, axis=-1, keepdims=True)
            v = jnp.var(t, axis=-1, keepdims=True)
            return (t - m) * jax.lax.rsqrt(v + EPS) * w + b

        def _attn(q, k, v):
            s = jnp.einsum('bhqd,bhkd->bhqk', q, k) * SCALE
            p = jax.nn.softmax(s, axis=-1)
            return jnp.einsum('bhqk,bhkd->bhqd', p, v)
        b, s1, _ = x.shape
        y_dca = y[:, -DCA:, :]
        y_main = y[:, :-DCA, :]
        kv_dca = (y_dca @ Wkv_dca + bkv_dca).reshape(b, DCA, 2, H, HD)
        k_dca = _ln(kv_dca[:, :, 0], kn_dca_w, kn_dca_b)
        v_dca = kv_dca[:, :, 1]
        s2 = y_main.shape[1]
        q = _ln((x @ Wq + bq).reshape(b, s1, H, HD), qn_w, qn_b)
        kv = jnp.concatenate([y_main @ Wk + bk, y_main @ Wv + bv], axis=-1)
        kv = kv.reshape(b, s2, H, 2 * HD)
        k = _ln(kv[..., :HD], kn_w, kn_b)
        v = kv[..., HD:]
        qT = q.transpose(0, 2, 1, 3)
        ctx = _attn(qT, k.transpose(0, 2, 1, 3), v.transpose(0, 2, 1, 3))
        ctx = ctx.transpose(0, 2, 1, 3).reshape(b, s1, QDIM)
        ctx_dca = _attn(qT, k_dca.transpose(0, 2, 1, 3), v_dca.transpose(0, 2, 1, 3))
        ctx_dca = ctx_dca.transpose(0, 2, 1, 3).reshape(b, s1, QDIM)
        ctx = ctx + DCA_WEIGHT * ctx_dca
        return ctx @ Wo + bo

    def _L0_ffn_ref(hidden_states, gate_w, Wg, Wu, Wd, sWg, sWu, sWd, shared_gate_w):
        import jax, jax.numpy as jnp
        import numpy as np
        B, S, D = (1, 256, 256)
        F = 64
        E = 16
        K = 4

        def _swiglu(x, wg, wu, wd):
            return jax.nn.silu(x @ wg) * (x @ wu) @ wd
        bsz, seq_len, dim = hidden_states.shape
        flat = hidden_states.reshape(-1, dim)
        T = flat.shape[0]
        router_logits = flat @ gate_w.T
        router_probs = jax.nn.softmax(router_logits.astype(jnp.float32), axis=-1)
        routing_weights, selected_experts = jax.lax.top_k(router_probs, K)
        routing_weights = routing_weights / routing_weights.sum(axis=-1, keepdims=True)
        routing_weights = routing_weights.astype(hidden_states.dtype)
        comb = jnp.sum(jax.nn.one_hot(selected_experts, E, dtype=flat.dtype) * routing_weights[..., None], axis=1)
        mixed = jnp.zeros_like(flat)
        for e in range(E):
            out_e = _swiglu(flat, Wg[e], Wu[e], Wd[e])
            mixed = mixed + comb[:, e:e + 1] * out_e
        shared = _swiglu(flat, sWg, sWu, sWd)
        shared_gate = jax.nn.sigmoid(flat @ shared_gate_w)
        return (mixed + shared * shared_gate).reshape(bsz, seq_len, dim)

    def _L1_xattn_ref(text_hidden, vision_tokens, vision_mask, Wq, Wk, Wv, Wo):
        import jax, jax.numpy as jnp
        import numpy as np
        N_HEADS = 16
        N_KV_HEADS = 8
        HEAD_DIM = 128
        D_TEXT = 256
        D_VISION = 128
        GROUPS = N_HEADS // N_KV_HEADS
        B, T_text, _ = text_hidden.shape
        T_vis = vision_tokens.shape[1]
        scale = jnp.float32(np.sqrt(HEAD_DIM))
        q = (text_hidden @ Wq).reshape(B, T_text, N_HEADS, HEAD_DIM).transpose(0, 2, 1, 3)
        k = (vision_tokens @ Wk).reshape(B, T_vis, N_KV_HEADS, HEAD_DIM).transpose(0, 2, 1, 3)
        v = (vision_tokens @ Wv).reshape(B, T_vis, N_KV_HEADS, HEAD_DIM).transpose(0, 2, 1, 3)
        k = jnp.repeat(k, GROUPS, axis=1)
        v = jnp.repeat(v, GROUPS, axis=1)
        scores = jnp.einsum('bhtd,bhsd->bhts', q, k) / scale
        mask = vision_mask[:, None, None, :]
        scores = jnp.where(mask, scores, -jnp.inf)
        attn = jax.nn.softmax(scores, axis=-1)
        attn = jnp.nan_to_num(attn, nan=0.0)
        out = jnp.einsum('bhts,bhsd->bhtd', attn, v)
        out = out.transpose(0, 2, 1, 3).reshape(B, T_text, N_HEADS * HEAD_DIM)
        return out @ Wo

    def _L1_ffn_ref(x, lut, gate_idx, up_idx, down_idx):
        import jax, jax.numpy as jnp
        import numpy as np
        HIDDEN = 256
        INTER = 688
        LUT_SIZE = 16

        def _ghost_linear(x, idx, lut):
            w = lut[idx]
            return jnp.einsum('bsh,oh->bso', x, w)
        gate = _ghost_linear(x, gate_idx, lut)
        up = _ghost_linear(x, up_idx, lut)
        h = jax.nn.silu(gate) * up
        return _ghost_linear(h, down_idx, lut)
    x = x + jnp.tanh(g_xattn[0]) * _L0_xattn_ref(_layernorm(x, axis=-1), ctx_1024, L0_xattn_Wq, L0_xattn_bq, L0_xattn_Wk, L0_xattn_bk, L0_xattn_Wv, L0_xattn_bv, L0_xattn_Wkv_dca, L0_xattn_bkv_dca, L0_xattn_qn_w, L0_xattn_qn_b, L0_xattn_kn_w, L0_xattn_kn_b, L0_xattn_kn_dca_w, L0_xattn_kn_dca_b, L0_xattn_Wo, L0_xattn_bo)
    x = x + jnp.tanh(g_ffn[0]) * _L0_ffn_ref(_layernorm(x, axis=-1), L0_ffn_gate_w, L0_ffn_Wg, L0_ffn_Wu, L0_ffn_Wd, L0_ffn_sWg, L0_ffn_sWu, L0_ffn_sWd, L0_ffn_shared_gate_w)
    x = x + jnp.tanh(g_xattn[1]) * _L1_xattn_ref(_layernorm(x, axis=-1), ctx_1024, mask_BxS2_bf1, L1_xattn_Wq, L1_xattn_Wk, L1_xattn_Wv, L1_xattn_Wo)
    x = x + jnp.tanh(g_ffn[1]) * _L1_ffn_ref(_layernorm(x, axis=-1), L1_ffn_lut, L1_ffn_gate_idx, L1_ffn_up_idx, L1_ffn_down_idx)
    return x

_drawn_inputs = setup_inputs


def setup_inputs(seed=0):
    import zlib

    import numpy as np

    out = dict(_drawn_inputs(seed))
    spreads = {'g_ffn': (-1.0, 0.6),
     'L0_xattn_bq': (0.0, 0.8),
     'L0_xattn_bk': (0.0, 0.527),
     'L0_xattn_bv': (0.0, 0.435),
     'L0_xattn_bkv_dca': (0.0, 0.321),
     'L0_xattn_qn_w': (1.0, 0.6),
     'L0_xattn_qn_b': (0.0, 0.8),
     'L0_xattn_kn_w': (1.0, 0.6),
     'L0_xattn_kn_b': (0.0, 2.0),
     'L0_xattn_kn_dca_w': (1.0, 0.6),
     'L0_xattn_kn_dca_b': (0.0, 2.0),
     'L0_xattn_bo': (0.0, 0.1)}
    factors = {'L0_xattn_Wq': 3.197,
     'L0_xattn_Wv': 2.689,
     'L0_ffn_gate_w': 8.0,
     'L0_ffn_Wg': 8.0,
     'L0_ffn_Wu': 8.0,
     'L0_ffn_Wd': 8.0,
     'L0_ffn_sWg': 8.0,
     'L0_ffn_sWu': 8.0,
     'L0_ffn_sWd': 8.0,
     'L0_ffn_shared_gate_w': 8.0,
     'L1_xattn_Wq': 8.0,
     'L1_xattn_Wk': 8.0,
     'L1_ffn_lut': 5.847}
    for name, (base, spread) in spreads.items():
        noise = np.random.default_rng([zlib.crc32(name.encode()), seed]).standard_normal(out[name].shape)
        drawn = base * np.exp(spread * noise) if base else spread * noise
        out[name] = jnp.asarray(drawn.astype(out[name].dtype))
    for name, factor in factors.items():
        out[name] = (out[name] * factor).astype(out[name].dtype)
    return out
```

```python
from contextlib import ExitStack

import numpy as np

import concourse.bass as bass
from concourse import mybir

ALU = mybir.AluOpType
ACT = mybir.ActivationFunctionType
F32 = mybir.dt.float32
F32R = mybir.dt.float32r
BF16 = mybir.dt.bfloat16
I32 = mybir.dt.int32
U32 = mybir.dt.uint32
U8 = mybir.dt.uint8
AX = mybir.AxisListType.X

P = 128
B, S, D = 16, 64, 256
DV = 128
GROUPS = 4
TG = B * S // GROUPS
BG = TG // S
TILES = TG // P
DC = D // P
H0, HD0 = 16, 16
DCA = 16
MAIN = S - DCA
PARTS = ((0, MAIN), (MAIN, S))
PAIRS0 = 4
E, F, TOPK = 16, 64, 4
EC = E * F // P
NL = E + 2
H1, HD1, KV1 = 16, 128, 8
HALF = H1 // 2
PAIRS1 = HALF // 2
HG = H1 // GROUPS
INTER, LUT = 688, 16
FC = -(-INTER // P)
FLAST = INTER - (FC - 1) * P
IG = INTER // GROUPS
DG = D // GROUPS
ROUNDS = (DC * IG, DC * IG, FC * DG)
RMAX = max(ROUNDS)
MASKED = 1e30

NVEC = D + D + 2 * HD0
NVK = 2 * D + 2 * HD0
NWA = 2 * DC * D + 4 * D
GB = 2 * DC * 4 * F + 2 * D
NWS = DC * 2 * F + D + DC * NL
GCW = HG * D + HG // 2 * 2 * DV + HG * D
NCONST = P + 2 + E
NSEL = (EC + 1) * P


class Signal:

    def __init__(self, sem, per_group):
        self.sem, self.per_group, self.n = sem, per_group, 0

    def up(self):
        self.n += 1
        return self.sem, 1

    def at(self, g, n):
        return self.sem, g * self.per_group + n

    def last(self, g):
        return self.at(g, self.n)


def build(nc, a):
    ctx = ExitStack()
    with ctx:
        def sb(name, shape, dt=F32):
            return ctx.enter_context(nc.sbuf_tensor(name, shape, dt))[:]

        def sem(name):
            return ctx.enter_context(nc.semaphore(name))

        def signals(phase, **per_group):
            return {k: Signal(sem(f"{phase}_{k}"), n) for k, n in per_group.items()}

        ps = ctx.enter_context(nc.psum_tensor("ps", [P, 8, 512], F32))[:]

        x = sb("x", [P, GROUPS * TILES, D])
        ctx_T = sb("ctx_T", [P, B * S])
        ctx_n = sb("ctx_n", [P, TILES, DV])
        const = sb("const", [P, NCONST])
        ident, parity = const[:, 0:P], const[:, P:P + 2]
        iota = const[:, P + 2:P + 2 + E]
        gates = sb("gates", [P, 4])
        tg = sb("tg", [P, 4])
        expo = sb("expo", [P, TILES])
        lut = sb("lut", [P, LUT])
        lut_step = sb("lut_step", [P, LUT // 2])
        mask_row8 = sb("mask_row8", [1, B * S], U8)
        mask_rows = sb("mask_rows", [1, 2, TG], BF16)
        ones_row = sb("ones_row", [1, P], BF16)
        mask_n8 = sb("mask_n8", [P, GROUPS * TILES], U8)
        mask_n = sb("mask_n", [P, GROUPS * TILES])
        xn = sb("xn", [P, TILES, D])
        stats = sb("stats", [P, TILES, 6])
        mv = sb("mv", [P, TILES, 2])
        ve = sb("ve", [P, TILES])
        rstd = sb("rstd", [P, TILES])
        xT_hi = sb("xT_hi", [P, DC, TG], F32R)
        xT_lo = sb("xT_lo", [P, DC, TG], F32R)
        shared_r = sb("shared_r", [P, 2 * NWA], F32R)
        wB_hi = sb("wB_hi", [P, GROUPS * GB], F32R)
        wB_lo = sb("wB_lo", [P, GROUPS * GB], F32R)
        wS_hi = sb("wS_hi", [P, NWS], F32R)
        wS_lo = sb("wS_lo", [P, NWS], F32R)
        wM_hi = sb("wM_hi", [P, H1, D], F32R)
        wM_lo = sb("wM_lo", [P, H1, D], F32R)
        wN_hi = sb("wN_hi", [P, H1, D], F32R)
        wN_lo = sb("wN_lo", [P, H1, D], F32R)
        stage = sb("stage", [P, GCW])
        work = sb("work", [P, 8000])
        workr = sb("workr", [P, 1536 + (EC + 1) * P], F32R)

        def carver(pool):
            at = [0]

            def carve(n):
                at[0] += n
                assert at[0] <= pool.shape[1], at
                return pool[:, at[0] - n:at[0]]
            return carve

        def split_tokens(v):
            return v.rearrange("p c n -> p (c n)")

        def bc_last(v, n):
            return v.unsqueeze(2).broadcast_to([v.shape[0], v.shape[1], n])

        def bc_mid(v, n):
            return v.unsqueeze(1).broadcast_to([v.shape[0], n, v.shape[1]])

        def wA(w):
            return (w[:, 0:DC * D].rearrange("p (c n) -> p c n", c=DC), w[:, DC * D:DC * D + 2 * D],
                    w[:, DC * D + 2 * D:DC * D + 4 * D], w[:, DC * D + 4 * D:NWA].rearrange("p (c n) -> p c n", c=DC))

        wA_hi, wA_lo = shared_r[:, 0:NWA], shared_r[:, NWA:2 * NWA]
        wq_hi, wkv_hi, wkvd_hi, wo_hi = wA(wA_hi)
        wq_lo, wkv_lo, wkvd_lo, wo_lo = wA(wA_lo)

        def wB(w):
            v, n = w.rearrange("p (g n) -> p g n", g=GROUPS), DC * 4 * F
            return (v[:, :, 0:n].rearrange("p g (c n) -> p g c n", c=DC),
                    v[:, :, n:2 * n].rearrange("p g (c n) -> p g c n", c=DC),
                    v[:, :, 2 * n:].rearrange("p g (k n) -> p g k n", k=2))

        eg_hi, eu_hi, ed_hi = wB(wB_hi)
        eg_lo, eu_lo, ed_lo = wB(wB_lo)

        def wS(w):
            n = DC * 2 * F
            return (w[:, 0:n].rearrange("p (c n) -> p c n", c=DC), w[0:F, n:n + D],
                    w[:, n + D:].rearrange("p (c n) -> p c n", c=DC))

        sgu_hi, sd_hi, wr_hi = wS(wS_hi)
        sgu_lo, sd_lo, wr_lo = wS(wS_lo)

        def wF(w):
            n = DC * FC * P
            return (w[:, 0:n].rearrange("p (c n) -> p c n", c=DC), w[:, n:2 * n].rearrange("p (c n) -> p c n", c=DC),
                    w[:, 2 * n:2 * n + FC * D].rearrange("p (c n) -> p c n", c=FC))

        fg_hi, fu_hi, fd_hi = wF(wB_hi)
        fg_lo, fu_lo, fd_lo = wF(wB_lo)

        waited = sem("waited")
        const_in, gates_in, x_in, ctxT_in, vec_in, lut_in, mask_in = (
            sem(n) for n in ("const_in", "gates_in", "x_in", "ctxT_in", "vec_in", "lut_in", "mask_in"))
        wA_in, wS_in, sel_in, setup_pool, setup_act, setup_dve, out_done = (
            sem(n) for n in ("wA_in", "wS_in", "sel_in", "setup_pool", "setup_act", "setup_dve", "out_done"))

        common = dict(stat=4, var_ready=1, rstd_ready=1, xn_ready=2, xT_done=1, hi_ready=1, lo_ready=1)
        A = signals("A", **common, dve=6, act=1, pool=2, ctx_hi=2, ctx_lo=2, kv_done=2, q_done=1, qkv_ready=5,
                    centred=1, squared=1, grp_var=1, grp_guess=1, scaled=1, qk_ready=2, qT_done=2, kT_ready=1,
                    qx_ready=2, scores_done=PAIRS0, maxed=2 * PAIRS0, shifted=2 * PAIRS0, exp_ready=PAIRS0,
                    summed=2 * PAIRS0, recip_ready=PAIRS0, probs_ready=2 * PAIRS0, pT_done=PAIRS0,
                    pT_ready=PAIRS0, pv_done=1, an_ready=4, anT_done=1, an_hi=1, an_lo=1, o_done=1, o_biased=1,
                    x_done=1, prep_hi=1, prep_lo=1)
        A_prep_in = sem("A_prep_in")
        CH = EC + 1
        Bp = signals("B", **common, dve=12, logits_done=1, shifted=1, exp_ready=1, gate_ready=1, comb_ready=2,
                     combT_done=1, combT_hi=1, combT_lo=1, gu_done=CH, tanh_ready=CH, h1=CH, h2=CH, bc_done=CH,
                     h3=CH, h_hi=CH, h_lo=CH, out_done=1, x_done=TILES, join_done=4, join_hi=4, join_lo=4)
        B_prep_in = sem("B_prep_in")
        C = signals("C", **common, mask_ready=2, ctx_masked=TILES, cx_hi=1, cx_lo=1, q_done=2 * PAIRS1, q_ready=2 * PAIRS1,
                    scores_done=4, maxed=4, shifted=4, exp_ready=4, summed=4, recip_ready=4, probs_ready=4,
                    pT_done=4, pT_hi=4, pT_lo=4, z_done=2 * BG, z_hi=2 * BG, z_lo=2 * BG, out_done=2, x_done=2,
                    bits=4 * 3, level1=8 * 3, chosen=3 * 3, dec_hi=3, dec_lo=3)
        C_nat_in, C_idx_in = sem("C_nat_in"), sem("C_idx_in")
        Dp = signals("D", **common, gu_done=FC, tanh_ready=FC, h1=FC, h3=FC, h_hi=FC, h_lo=FC, out_done=1,
                     x_done=TILES)

        def normalise(dve, g, ph):
            for t in range(TILES):
                nc.vector.bn_stats(stats[:, t, :], x[:, g * TILES + t, :]).then_inc(*ph["stat"].up())
            for t in range(TILES):
                dve.wait_ge(*ph["stat"].at(g, t + 1))
                dve.sem_inc(waited, 1)
                nc.vector.bn_aggr(mv[:, t, :], stats[:, t, :]).then_inc(*ph["stat"].up())
            dve.wait_ge(*ph["stat"].last(g))
            nc.vector.tensor_scalar(ve, mv[:, :, 1], 1e-5, None, ALU.add).then_inc(*ph["var_ready"].up())
            dve.wait_ge(*ph["rstd_ready"].at(g, 1))
            for t in range(TILES):
                nc.vector.tensor_scalar(xn[:, t, :], x[:, g * TILES + t, :], mv[:, t, 0:1], rstd[:, t:t + 1],
                                        ALU.subtract, ALU.mult).then_inc(*ph["xn_ready"].up())

        def inverse_root(pool, g, ph):
            pool.wait_ge(*ph["var_ready"].at(g, 1))
            nc.gpsimd.tensor_tensor(rstd, ve, expo, ALU.pow).then_inc(*ph["rstd_ready"].up())

        def turn(src, to):
            for c in range(DC):
                for t in range(TILES):
                    last = nc.tensor.transpose(ps[:, to, c * TG + t * P:c * TG + (t + 1) * P],
                                               src[:, t, c * P:(c + 1) * P], ident)
            return last

        def turn_x(pe, g, ph):
            pe.wait_ge(*ph["xn_ready"].at(g, TILES))
            turn(xn, 0).then_inc(*ph["xT_done"].up())

        def upper_x(act, g, ph):
            act.wait_ge(*ph["xT_done"].at(g, 1))
            nc.scalar.copy(split_tokens(xT_hi), ps[:, 0, :]).then_inc(*ph["hi_ready"].up())

        def lower_x(dve, g, ph):
            dve.wait_ge(*ph["hi_ready"].at(g, 1))
            nc.vector.tensor_tensor(split_tokens(xT_lo), ps[:, 0, :], split_tokens(xT_hi).bitcast(F32),
                                    ALU.subtract).then_inc(*ph["lo_ready"].up())

        def x_split(pe, g, ph):
            pe.wait_ge(*ph["hi_ready"].at(g, 1))
            pe.wait_ge(*ph["lo_ready"].at(g, 1))

        def mm3(out, l_hi, l_lo, r_hi, r_lo, start, stop, loose=False):
            for i, (l, r) in enumerate(((l_hi, r_hi), (l_hi, r_lo), (l_lo, r_hi))):
                last = nc.tensor.matmul(out, l, r, start=start and i == 0, stop=stop and i == 2)
            return last

        take = carver(work)
        r1, r2 = take(2048), take(2048)
        qk = r2[:, 0:TILES * 2 * D]
        qk4 = qk.rearrange("p (t k n) -> p t k n", t=TILES, k=2)
        sq = r1[:, 0:TILES * 2 * D]
        probs = r1.rearrange("p (b k n) -> p b k n", b=PAIRS0, k=8)
        pT = r2.rearrange("p (b k n) -> p b k n", b=PAIRS0, k=4)
        vsb = take(TILES * D).rearrange("p (t n) -> p t n", t=TILES)
        vec, veck = take(NVEC), take(NVK)
        bq, bo, qn_w, qn_b = vec[:, 0:D], vec[:, D:2 * D], vec[:, 2 * D:2 * D + HD0], vec[:, 2 * D + HD0:]
        bkv, kn_w, kn_b = veck[:, 0:2 * D], veck[:, 2 * D:2 * D + HD0], veck[:, 2 * D + HD0:]
        kT_flat = take(DC * TG)
        kT = kT_flat.rearrange("p (c n) -> p c n", c=DC)
        an = kT_flat.rearrange("p (t n) -> p t n", t=TILES)
        qx = take(2 * DC * TG).rearrange("p (k h n) -> p k h n", h=2, n=S)
        gsum, gmean, gssq, gvar, gln, guess, gsq, gfix, grs = (take(64) for _ in range(9))
        mxA, smA, rcA = (take(64).rearrange("p (b n) -> p b n", b=PAIRS0) for _ in range(3))
        take_r = carver(workr)
        ctxm = [take_r(TG).rearrange("p (b n) -> p b n", b=BG) for _ in range(4)]
        heads = qk.rearrange("p (h n) -> p h n", n=HD0)

        def ctx_rows(g, lo, hi):
            return ctx_T[:, bass.ds(g * TG, TG)].rearrange("p (b n) -> p b n", b=BG)[:, :, lo:hi]

        def pe_A(pe, g):
            turn_x(pe, g, A)
            pe.wait_ge(*A["ctx_hi"].at(g, 2))
            pe.wait_ge(*A["ctx_lo"].at(g, 2))
            for t in range(TILES):
                m = [c.rearrange("p b n -> p (b n)")[:, t * P:(t + 1) * P] for c in ctxm]
                mm3(ps[:, 2 + t, :], m[0], m[1], wkv_hi, wkv_lo, True, False)
                mm3(ps[:, 2 + t, :], m[2], m[3], wkvd_hi, wkvd_lo, False, True).then_inc(*A["kv_done"].up())
            x_split(pe, g, A)
            for t in range(TILES):
                for c in range(DC):
                    last = mm3(ps[:, 1, t * D:(t + 1) * D], xT_hi[:, c, t * P:(t + 1) * P],
                               xT_lo[:, c, t * P:(t + 1) * P], wq_hi[:, c, :], wq_lo[:, c, :], c == 0, c == DC - 1)
            last.then_inc(*A["q_done"].up())
            pe.wait_ge(*A["qk_ready"].at(g, 2))
            for k in range(2):
                for c in range(DC):
                    for t in range(TILES):
                        last = nc.tensor.transpose(ps[:, 4 + k, c * TG + t * P:c * TG + (t + 1) * P],
                                                   qk4[:, t, k, c * P:(c + 1) * P], ident)
                last.then_inc(*A["qT_done"].up())
            pe.wait_ge(*A["kT_ready"].at(g, 1))
            pe.wait_ge(*A["qx_ready"].at(g, 2))
            for t in range(TILES):
                for c in range(DC):
                    for b in range(2):
                        tok, k = t * P + b * S, (t * DC + c) * 2 + b
                        for p in range(PAIRS0):
                            last = nc.tensor.matmul(ps[:, p, k * S:(k + 1) * S],
                                                    qx[32 * p:32 * p + 32, c * BG + 2 * t + b].rearrange("p h n -> p (h n)"),
                                                    kT[32 * p:32 * p + 32, c, tok:tok + S], start=True, stop=True)
                            if k == 7:
                                last.then_inc(*A["scores_done"].up())
            for p in range(PAIRS0):
                pe.wait_ge(*A["probs_ready"].at(g, 2 * p + 2))
                for k in range(4):
                    last = nc.tensor.transpose(ps[:, 4 + p, k * P:(k + 1) * P],
                                               probs[:, p, 2 * k:2 * k + 2, :].rearrange("p a b -> p (a b)"), ident)
                last.then_inc(*A["pT_done"].up())
            for p in range(PAIRS0):
                pe.wait_ge(*A["pT_ready"].at(g, p + 1))
                for k in range(4):
                    t, c = divmod(k, DC)
                    for b in range(2):
                        o, d = (t * 8 + c * 4 + p) * 32, (c * 8 + 2 * p) * HD0
                        last = nc.tensor.matmul(ps[:, b, o:o + 32], pT[S * b:S * b + S, p, k, :],
                                                vsb[S * b:S * b + S, t, d:d + 32], start=True, stop=True)
            last.then_inc(*A["pv_done"].up())
            pe.wait_ge(*A["an_ready"].at(g, 4))
            turn(an, 2).then_inc(*A["anT_done"].up())
            pe.wait_ge(*A["an_hi"].at(g, 1))
            pe.wait_ge(*A["an_lo"].at(g, 1))
            for t in range(TILES):
                for c in range(DC):
                    last = mm3(ps[:, 3, t * D:(t + 1) * D], xT_hi[:, c, t * P:(t + 1) * P],
                               xT_lo[:, c, t * P:(t + 1) * P], wo_hi[:, c, :], wo_lo[:, c, :], c == 0, c == DC - 1)
            last.then_inc(*A["o_done"].up())
            pe.wait_ge(*A["x_done"].at(g, 1))

        def act_A(act, g):
            for i, (lo, hi) in enumerate(PARTS):
                nc.scalar.copy(ctxm[2 * i][:, :, lo:hi], ctx_rows(g, lo, hi)).then_inc(*A["ctx_hi"].up())
            upper_x(act, g, A)
            act.wait_ge(A_prep_in, g * 16 + 16)
            nc.scalar.copy(wB_hi[:, bass.ds(g * GB, GB)], stage[:, 0:GB]).then_inc(*A["prep_hi"].up())
            act.wait_ge(*A["centred"].at(g, 1))
            nc.scalar.activation(sq, qk, ACT.Square).then_inc(*A["squared"].up())
            act.wait_ge(*A["grp_var"].at(g, 1))
            nc.scalar.activation(gln, gvar, ACT.Ln).then_inc(*A["act"].up())
            act.wait_ge(*A["act"].last(g))
            nc.scalar.activation(guess, gln, ACT.Exp, scale=-0.5).then_inc(*A["grp_guess"].up())
            act.wait_ge(*A["qT_done"].at(g, 1))
            for h in range(2):
                nc.scalar.activation(qx[:, :, h, :], ps[:, 4, :].rearrange("p (k n) -> p k n", n=S), ACT.Identity,
                                     scale=parity[:, h:h + 1]).then_inc(*A["qx_ready"].up())
            act.wait_ge(*A["qT_done"].at(g, 2))
            nc.scalar.copy(kT_flat, ps[:, 5, :]).then_inc(*A["kT_ready"].up())
            for p in range(PAIRS0):
                act.wait_ge(*A["shifted"].at(g, 2 * p + 2))
                v = split_tokens(probs[:, p])
                nc.scalar.activation(v, v, ACT.Exp, scale=HD0 ** -0.5).then_inc(*A["exp_ready"].up())
            for p in range(PAIRS0):
                act.wait_ge(*A["pT_done"].at(g, p + 1))
                nc.scalar.copy(split_tokens(pT[:, p]), ps[:, 4 + p, :]).then_inc(*A["pT_ready"].up())
            act.wait_ge(*A["pv_done"].at(g, 1))
            for b in range(2):
                for h in range(2):
                    src = ps[S * h:S * h + S, b, :].rearrange("p (k h n) -> p k h n", k=16, h=2)[:, :, h, :]
                    dst = an[S * b:S * b + S].rearrange("p t (k h n) -> p (t k) h n", k=8, h=2)[:, :, h, :]
                    nc.scalar.copy(dst, src).then_inc(*A["an_ready"].up())
            act.wait_ge(*A["anT_done"].at(g, 1))
            nc.scalar.copy(split_tokens(xT_hi), ps[:, 2, :]).then_inc(*A["an_hi"].up())
            act.wait_ge(*A["x_done"].at(g, 1))

        def dve_A(dve, g):
            normalise(dve, g, A)
            for i, (lo, hi) in enumerate(PARTS):
                dve.wait_ge(*A["ctx_hi"].at(g, i + 1))
                nc.vector.tensor_tensor(ctxm[2 * i + 1][:, :, lo:hi], ctx_rows(g, lo, hi),
                                        ctxm[2 * i][:, :, lo:hi].bitcast(F32), ALU.subtract).then_inc(*A["ctx_lo"].up())
            lower_x(dve, g, A)
            for t in range(TILES):
                dve.wait_ge(*A["kv_done"].at(g, t + 1))
                nc.vector.tensor_tensor(qk4[:, t, 1, :], ps[:, 2 + t, 0:D], bkv[:, 0:D],
                                        ALU.add).then_inc(*A["qkv_ready"].up())
                nc.vector.tensor_tensor(vsb[:, t, :], ps[:, 2 + t, D:2 * D], bkv[:, D:2 * D],
                                        ALU.add).then_inc(*A["qkv_ready"].up())
            dve.wait_ge(*A["q_done"].at(g, 1))
            nc.vector.tensor_tensor(qk4[:, :, 0, :], ps[:, 1, :].rearrange("p (t n) -> p t n", t=TILES),
                                    bc_mid(bq, TILES), ALU.add).then_inc(*A["qkv_ready"].up())
            dve.wait_ge(*A["qkv_ready"].last(g))
            nc.vector.tensor_reduce(gsum, heads, AX, ALU.add).then_inc(*A["dve"].up())
            dve.wait_ge(*A["dve"].last(g))
            nc.vector.tensor_scalar(gmean, gsum, 1.0 / HD0, None, ALU.mult).then_inc(*A["dve"].up())
            dve.wait_ge(*A["dve"].last(g))
            nc.vector.tensor_tensor(heads, heads, bc_last(gmean, HD0), ALU.subtract).then_inc(*A["centred"].up())
            dve.wait_ge(*A["squared"].at(g, 1))
            nc.vector.tensor_reduce(gssq, sq.rearrange("p (h n) -> p h n", n=HD0), AX, ALU.add).then_inc(*A["dve"].up())
            dve.wait_ge(*A["dve"].last(g))
            nc.vector.tensor_scalar(gvar, gssq, 1.0 / HD0, 1e-6, ALU.mult, ALU.add).then_inc(*A["grp_var"].up())
            dve.wait_ge(*A["grp_guess"].at(g, 1))
            nc.vector.tensor_tensor(gsq, guess, guess, ALU.mult).then_inc(*A["dve"].up())
            dve.wait_ge(*A["dve"].last(g))
            nc.vector.scalar_tensor_tensor(out=gfix, in0=gsq, scalar=-0.5, in1=gvar, op0=ALU.mult,
                                           op1=ALU.mult).then_inc(*A["dve"].up())
            dve.wait_ge(*A["dve"].last(g))
            nc.vector.scalar_tensor_tensor(out=grs, in0=gfix, scalar=1.5, in1=guess, op0=ALU.add,
                                           op1=ALU.mult).then_inc(*A["dve"].up())
            dve.wait_ge(*A["dve"].last(g))
            nc.vector.tensor_tensor(heads, heads, bc_last(grs, HD0), ALU.mult).then_inc(*A["scaled"].up())
            for p in range(PAIRS0):
                dve.wait_ge(*A["scores_done"].at(g, p + 1))
                s = ps[:, p, :].rearrange("p (k n) -> p k n", k=8)
                for i, (lo, hi) in enumerate(PARTS):
                    nc.vector.tensor_reduce(mxA[:, p, 8 * i:8 * i + 8], s[:, :, lo:hi], AX,
                                            ALU.max).then_inc(*A["maxed"].up())
                for i, (lo, hi) in enumerate(PARTS):
                    dve.wait_ge(*A["maxed"].at(g, 2 * p + i + 1))
                    nc.vector.tensor_tensor(probs[:, p, :, lo:hi], s[:, :, lo:hi],
                                            bc_last(mxA[:, p, 8 * i:8 * i + 8], hi - lo),
                                            ALU.subtract).then_inc(*A["shifted"].up())
            for p in range(PAIRS0):
                dve.wait_ge(*A["exp_ready"].at(g, p + 1))
                for i, (lo, hi) in enumerate(PARTS):
                    nc.vector.tensor_reduce(smA[:, p, 8 * i:8 * i + 8], probs[:, p, :, lo:hi], AX,
                                            ALU.add).then_inc(*A["summed"].up())
                dve.wait_ge(*A["summed"].last(g))
                nc.vector.reciprocal(rcA[:, p, :], smA[:, p, :]).then_inc(*A["recip_ready"].up())
            dve.wait_ge(*A["an_hi"].at(g, 1))
            nc.vector.tensor_tensor(split_tokens(xT_lo), ps[:, 2, :], split_tokens(xT_hi).bitcast(F32),
                                    ALU.subtract).then_inc(*A["an_lo"].up())
            dve.wait_ge(*A["o_done"].at(g, 1))
            nc.vector.tensor_tensor(xn, ps[:, 3, :].rearrange("p (t n) -> p t n", t=TILES), bc_mid(bo, TILES),
                                    ALU.add).then_inc(*A["o_biased"].up())
            dve.wait_ge(*A["o_biased"].at(g, 1))
            dve.wait_ge(*A["prep_lo"].at(g, 1))
            xg = x[:, bass.ds(g * TILES, TILES), :]
            nc.vector.scalar_tensor_tensor(out=xg, in0=xn, scalar=tg[:, 0:1], in1=xg, op0=ALU.mult,
                                           op1=ALU.add).then_inc(*A["x_done"].up())
            dve.wait_ge(*A["x_done"].at(g, 1))

        def pool_A(pool, g):
            inverse_root(pool, g, A)
            pool.wait_ge(*A["prep_hi"].at(g, 1))
            nc.gpsimd.tensor_tensor(wB_lo[:, bass.ds(g * GB, GB)], stage[:, 0:GB],
                                    wB_hi[:, bass.ds(g * GB, GB)].bitcast(F32), ALU.subtract).then_inc(*A["prep_lo"].up())
            pool.wait_ge(*A["scaled"].at(g, 1))
            for k, w in enumerate((qn_w, kn_w)):
                v = qk4[:, :, k, :].rearrange("p t (h n) -> p t h n", n=HD0)
                wb = w.unsqueeze(1).unsqueeze(1).broadcast_to([P, TILES, H0, HD0])
                nc.gpsimd.tensor_tensor(v, v, wb, ALU.mult).then_inc(*A["pool"].up())
            for k, w in enumerate((qn_b, kn_b)):
                v = qk4[:, :, k, :].rearrange("p t (h n) -> p t h n", n=HD0)
                wb = w.unsqueeze(1).unsqueeze(1).broadcast_to([P, TILES, H0, HD0])
                pool.wait_ge(*A["pool"].at(g, k + 1))
                nc.gpsimd.tensor_tensor(v, v, wb, ALU.add).then_inc(*A["qk_ready"].up())
            for p in range(PAIRS0):
                pool.wait_ge(*A["recip_ready"].at(g, p + 1))
                for i, (lo, hi) in enumerate(PARTS):
                    v = probs[:, p, :, lo:hi]
                    nc.gpsimd.tensor_tensor(v, v, bc_last(rcA[:, p, 8 * i:8 * i + 8], hi - lo),
                                            ALU.mult).then_inc(*A["probs_ready"].up())
            pool.wait_ge(*A["x_done"].at(g, 1))

        def sp_A(sp, g):
            sp.dma_start(stage[:, 0:GB], a["wB"][bass.ds(g, 1)].rearrange("o p n -> p (o n)")).then_inc(A_prep_in, 16)
            sp.wait_ge(A_prep_in, g * 16 + 16)
            sp.sem_inc(waited, 1)
            sp.wait_ge(*A["x_done"].at(g, 1))
            sp.sem_inc(waited, 1)

        take = carver(work)
        lgs = take(TILES * NL).rearrange("p (t n) -> p t n", t=TILES)
        m8, ixf = (take(TILES * 8).rearrange("p (t n) -> p t n", t=TILES) for _ in range(2))
        ix = take(TILES * 8).bitcast(U32).rearrange("p (t n) -> p t n", t=TILES)
        ex, chosen, wsel = (take(TILES * E).rearrange("p (t n) -> p t n", t=TILES) for _ in range(3))
        comb = take(TILES * (E + 1)).rearrange("p (t n) -> p t n", t=TILES)
        eq = take(TILES * E * TOPK).rearrange("p (t n k) -> p t n k", t=TILES, k=TOPK)
        wsum, wrec, whalf, sgate = (take(TILES) for _ in range(4))
        th, h1, h2, h3 = ([take(TG), take(TG)] for _ in range(4))
        take_r = carver(workr)
        h_hi, h_lo = ([take_r(TG), take_r(TG)] for _ in range(2))
        combT_hi, combT_lo = (take_r(TG)[0:E + 1] for _ in range(2))
        sel = take_r((EC + 1) * P)[0:E + 1].rearrange("p (k n) -> p k n", k=EC + 1)
        BC_BANK = (5, 1)
        wqT, wkT = stage[:, 0:HG * D].rearrange("p (h n) -> p h n", h=HG), \
            stage[:, HG * D:HG * D + HG // 2 * DV].rearrange("p (h n) -> p h n", h=HG // 2)
        wvT = stage[:, HG * D + HG // 2 * DV:HG * D + HG * DV].rearrange("p (h n) -> p h n", h=HG // 2)
        wo1 = stage[:, HG * D + HG * DV:GCW].rearrange("p (h n) -> p h n", h=HG)
        JOIN = ((wM_hi, wM_lo), (wM_hi, wM_lo), (wN_hi, wN_lo), (wN_hi, wN_lo))

        def rows_B(k):
            return P if k < EC else F

        def up_B(k):
            return ps[:, 3 + k % 2, TG:2 * TG] if k < EC else ps[F:2 * F, 3 + k % 2, 0:TG]

        def pe_B(pe, g):
            turn_x(pe, g, Bp)
            x_split(pe, g, Bp)
            for t in range(TILES):
                for c in range(DC):
                    last = mm3(ps[:, 1, t * NL:(t + 1) * NL], xT_hi[:, c, t * P:(t + 1) * P],
                               xT_lo[:, c, t * P:(t + 1) * P], wr_hi[:, c, :], wr_lo[:, c, :], c == 0, c == DC - 1)
            last.then_inc(*Bp["logits_done"].up())

            def gate_up(k):
                if k >= 2:
                    pe.wait_ge(*Bp["h2"].at(g, k - 1))
                if k < EC:
                    col = slice(k % 2 * P, k % 2 * P + P)
                    for i, (w_hi, w_lo) in enumerate(((eg_hi, eg_lo), (eu_hi, eu_lo))):
                        for c in range(DC):
                            last = mm3(ps[:, 3 + k % 2, i * TG:(i + 1) * TG], w_hi[:, k // 2, c, col],
                                       w_lo[:, k // 2, c, col], xT_hi[:, c, :], xT_lo[:, c, :], c == 0, c == DC - 1)
                else:
                    for c in range(DC):
                        last = mm3(ps[:, 3 + k % 2, 0:TG], sgu_hi[:, c, :], sgu_lo[:, c, :], xT_hi[:, c, :],
                                   xT_lo[:, c, :], c == 0, c == DC - 1)
                last.then_inc(*Bp["gu_done"].up())

            def spread(k):
                if k >= 2:
                    pe.wait_ge(*Bp["h3"].at(g, k - 1))
                o = ps[:, BC_BANK[k % 2], 0:TG]
                nc.tensor.matmul(o, sel[:, k, :], combT_hi, start=True, stop=False)
                nc.tensor.matmul(o, sel[:, k, :], combT_lo, start=False, stop=True).then_inc(*Bp["bc_done"].up())

            def down(k):
                pe.wait_ge(*Bp["h_hi"].at(g, k + 1))
                pe.wait_ge(*Bp["h_lo"].at(g, k + 1))
                n = rows_B(k)
                d_hi, d_lo = (ed_hi[:, k // 2, k % 2, :], ed_lo[:, k // 2, k % 2, :]) if k < EC else (sd_hi, sd_lo)
                for t in range(TILES):
                    last = mm3(ps[:, 6 + t, 0:D], h_hi[k % 2][0:n, t * P:(t + 1) * P],
                               h_lo[k % 2][0:n, t * P:(t + 1) * P], d_hi, d_lo, k == 0, k == EC)
                return last

            def join(r):
                if r == 0:
                    pe.wait_ge(B_prep_in, g * 16 + 16)
                if r >= 2:
                    pe.wait_ge(*Bp["join_lo"].at(g, r - 1))
                for i in range(2):
                    h = 2 * (r % 2) + i
                    for c in range(DC) if r < 2 else ():
                        last = nc.tensor.matmul(ps[:, 2 * (r % 2), i * D + c * DV:i * D + (c + 1) * DV],
                                                wqT[:, h, c * P:(c + 1) * P], wkT[:, h // 2, :], start=True, stop=True)
                    if r >= 2:
                        last = nc.tensor.matmul(ps[:, 2 * (r % 2), i * D:(i + 1) * D], wvT[:, h // 2, :],
                                                wo1[:, h, :], start=True, stop=True)
                last.then_inc(*Bp["join_done"].up())

            gate_up(0)
            gate_up(1)
            join(0)
            pe.wait_ge(*Bp["comb_ready"].at(g, 2))
            for t in range(TILES):
                last = nc.tensor.transpose(ps[0:E + 1, 2, t * P:(t + 1) * P], comb[:, t, :], ident)
            last.then_inc(*Bp["combT_done"].up())
            pe.wait_ge(*Bp["combT_hi"].at(g, 1))
            pe.wait_ge(*Bp["combT_lo"].at(g, 1))
            spread(0)
            spread(1)
            down(0)
            for k in range(2, EC + 1):
                gate_up(k)
                spread(k)
                if k in (2, 4, 6):
                    join(k // 2)
                down(k - 1)
            down(EC).then_inc(*Bp["out_done"].up())
            pe.wait_ge(*Bp["x_done"].at(g, TILES))

        def act_B(act, g):
            upper_x(act, g, Bp)

            def tanh(k):
                act.wait_ge(*Bp["gu_done"].at(g, k + 1))
                n = rows_B(k)
                nc.scalar.activation(th[k % 2][0:n], ps[0:n, 3 + k % 2, 0:TG], ACT.Tanh,
                                     scale=0.5).then_inc(*Bp["tanh_ready"].up())

            def upper(k):
                act.wait_ge(*Bp["h3"].at(g, k + 1))
                n = rows_B(k)
                nc.scalar.copy(h_hi[k % 2][0:n], h3[k % 2][0:n]).then_inc(*Bp["h_hi"].up())

            def join(r):
                act.wait_ge(*Bp["join_done"].at(g, r + 1))
                w = JOIN[r][0][:, bass.ds(g * HG + 2 * (r % 2), 2), :]
                nc.scalar.copy(w, ps[:, 2 * (r % 2), :].rearrange("p (h n) -> p h n", h=2)).then_inc(*Bp["join_hi"].up())

            tanh(0)
            tanh(1)
            join(0)
            act.wait_ge(*Bp["shifted"].at(g, 1))
            nc.scalar.activation(ex, ex, ACT.Exp).then_inc(*Bp["exp_ready"].up())
            nc.scalar.activation(sgate, lgs[:, :, E], ACT.Tanh, scale=0.5).then_inc(*Bp["gate_ready"].up())
            act.wait_ge(*Bp["combT_done"].at(g, 1))
            nc.scalar.copy(combT_hi, ps[0:E + 1, 2, 0:TG]).then_inc(*Bp["combT_hi"].up())
            upper(0)
            for k in range(2, EC + 1):
                tanh(k)
                if k in (2, 4, 6):
                    join(k // 2)
                upper(k - 1)
            upper(EC)
            act.wait_ge(*Bp["x_done"].at(g, TILES))

        def dve_B(dve, g):
            normalise(dve, g, Bp)
            lower_x(dve, g, Bp)

            def gated(k):
                n = rows_B(k)
                dve.wait_ge(*Bp["tanh_ready"].at(g, k + 1))
                nc.vector.scalar_tensor_tensor(out=h1[k % 2][0:n], in0=th[k % 2][0:n], scalar=1.0,
                                               in1=ps[0:n, 3 + k % 2, 0:TG], op0=ALU.add,
                                               op1=ALU.mult).then_inc(*Bp["h1"].up())
                dve.wait_ge(*Bp["h1"].at(g, k + 1))
                nc.vector.tensor_tensor(h2[k % 2][0:n], h1[k % 2][0:n], up_B(k), ALU.mult).then_inc(*Bp["h2"].up())

            def weighted(k):
                n = rows_B(k)
                dve.wait_ge(*Bp["h2"].at(g, k + 1))
                dve.wait_ge(*Bp["bc_done"].at(g, k + 1))
                nc.vector.tensor_tensor(h3[k % 2][0:n], h2[k % 2][0:n], ps[0:n, BC_BANK[k % 2], 0:TG],
                                        ALU.mult).then_inc(*Bp["h3"].up())

            def join(r):
                dve.wait_ge(*Bp["join_hi"].at(g, r + 1))
                hi, lo = (w[:, bass.ds(g * HG + 2 * (r % 2), 2), :] for w in JOIN[r])
                nc.vector.tensor_tensor(lo, ps[:, 2 * (r % 2), :].rearrange("p (h n) -> p h n", h=2),
                                        hi.bitcast(F32), ALU.subtract).then_inc(*Bp["join_lo"].up())

            dve.wait_ge(*Bp["logits_done"].at(g, 1))
            nc.vector.tensor_copy(lgs, ps[:, 1, 0:TILES * NL].rearrange("p (t n) -> p t n", t=TILES)
                                  ).then_inc(*Bp["dve"].up())
            dve.wait_ge(*Bp["dve"].last(g))
            dve.sem_inc(waited, 1)
            for t in range(TILES):
                nc.vector.max(m8[:, t, :], lgs[:, t, 0:E]).then_inc(*Bp["dve"].up())
            dve.wait_ge(*Bp["dve"].last(g))
            nc.vector.tensor_tensor(ex, lgs[:, :, 0:E], m8[:, :, 0:1].broadcast_to([P, TILES, E]),
                                    ALU.subtract).then_inc(*Bp["shifted"].up())
            for t in range(TILES):
                nc.vector.max_index(ix[:, t, :], m8[:, t, :], lgs[:, t, 0:E]).then_inc(*Bp["dve"].up())
            dve.wait_ge(*Bp["dve"].last(g))
            nc.vector.tensor_copy(ixf, ix).then_inc(*Bp["dve"].up())
            dve.wait_ge(*Bp["dve"].last(g))
            nc.vector.tensor_tensor(eq, iota.unsqueeze(1).unsqueeze(3).broadcast_to([P, TILES, E, TOPK]),
                                    ixf[:, :, 0:TOPK].unsqueeze(2).broadcast_to([P, TILES, E, TOPK]),
                                    ALU.is_equal).then_inc(*Bp["dve"].up())
            dve.wait_ge(*Bp["dve"].last(g))
            nc.vector.tensor_reduce(chosen, eq, AX, ALU.add).then_inc(*Bp["dve"].up())
            dve.wait_ge(*Bp["dve"].last(g))
            dve.wait_ge(*Bp["exp_ready"].at(g, 1))
            nc.vector.tensor_tensor(wsel, ex, chosen, ALU.mult).then_inc(*Bp["dve"].up())
            dve.wait_ge(*Bp["dve"].last(g))
            nc.vector.tensor_reduce(wsum, wsel, AX, ALU.add).then_inc(*Bp["dve"].up())
            dve.wait_ge(*Bp["dve"].last(g))
            nc.vector.reciprocal(wrec, wsum).then_inc(*Bp["dve"].up())
            dve.wait_ge(*Bp["dve"].last(g))
            nc.vector.tensor_scalar(whalf, wrec, 0.5, None, ALU.mult).then_inc(*Bp["dve"].up())
            dve.wait_ge(*Bp["dve"].last(g))
            nc.vector.tensor_tensor(comb[:, :, 0:E], wsel, bc_last(whalf, E), ALU.mult).then_inc(*Bp["comb_ready"].up())
            dve.wait_ge(*Bp["gate_ready"].at(g, 1))
            nc.vector.tensor_scalar(comb[:, :, E], sgate, 0.25, 0.25, ALU.mult, ALU.add).then_inc(*Bp["comb_ready"].up())
            gated(0)
            gated(1)
            join(0)
            dve.wait_ge(*Bp["combT_hi"].at(g, 1))
            nc.vector.tensor_tensor(combT_lo, ps[0:E + 1, 2, 0:TG], combT_hi.bitcast(F32),
                                    ALU.subtract).then_inc(*Bp["combT_lo"].up())
            weighted(0)
            weighted(1)
            for k in range(2, EC + 1):
                gated(k)
                if k in (2, 4, 6):
                    join(k // 2)
                weighted(k)
            dve.wait_ge(*Bp["out_done"].at(g, 1))
            for t in range(TILES):
                xt = x[:, g * TILES + t, :]
                nc.vector.scalar_tensor_tensor(out=xt, in0=ps[:, 6 + t, 0:D], scalar=tg[:, 1:2], in1=xt,
                                               op0=ALU.mult, op1=ALU.add).then_inc(*Bp["x_done"].up())
            dve.wait_ge(*Bp["x_done"].at(g, TILES))

        def pool_B(pool, g):
            inverse_root(pool, g, Bp)
            for k in range(EC + 1):
                n = rows_B(k)
                pool.wait_ge(*Bp["h_hi"].at(g, k + 1))
                nc.gpsimd.tensor_tensor(h_lo[k % 2][0:n], h3[k % 2][0:n], h_hi[k % 2][0:n].bitcast(F32),
                                        ALU.subtract).then_inc(*Bp["h_lo"].up())
            pool.wait_ge(*Bp["x_done"].at(g, TILES))

        def sp_B(sp, g):
            sp.dma_start(stage, a["wC"][bass.ds(g, 1)].rearrange("o p n -> p (o n)")).then_inc(B_prep_in, 16)
            sp.wait_ge(B_prep_in, g * 16 + 16)
            sp.sem_inc(waited, 1)
            sp.wait_ge(*Bp["x_done"].at(g, TILES))
            sp.sem_inc(waited, 1)

        take = carver(work)
        qt = take(PAIRS1 * 2 * TG).rearrange("p (j b h n) -> p j b h n", j=PAIRS1, b=BG, h=2)
        pC = take(2 * 512).rearrange("p (s k n) -> p s k n", s=2, k=8)
        mxC, smC, rcC = (take(4 * 8).rearrange("p (s n) -> p s n", s=4) for _ in range(3))
        bits = take(4 * RMAX).bitcast(I32).rearrange("p (b n) -> p b n", b=4)
        lev = take(8 * RMAX).rearrange("p (j n) -> p j n", j=8)
        take_r = carver(workr)
        pT_hi, pT_lo = (take_r(TILES * 512).rearrange("p (t n) -> p t n", t=TILES) for _ in range(2))
        cx_hi, cx_lo = (take_r(TILES * DV).rearrange("p (t n) -> p t n", t=TILES) for _ in range(2))
        z_hi, z_lo = (shared_r[:, i * HALF * TG:(i + 1) * HALF * TG].rearrange("p (h n) -> p h n", h=HALF)
                      for i in range(2))
        idx = stage[:, 0:sum(ROUNDS)].bitcast(I32)

        def decoded(w, g, r):
            if r < 2:
                return w[r][:, :, bass.ds(g * IG, IG)]
            return w[2][:, :, bass.ds(g * DG, DG)]

        def shape_r(v, r):
            return v.rearrange("p (c n) -> p c n", c=DC if r < 2 else FC)

        def pe_C(pe, g):
            turn_x(pe, g, C)
            x_split(pe, g, C)

            def queries(u):
                for j in range(PAIRS1):
                    n = u * PAIRS1 + j
                    if n >= 2:
                        pe.wait_ge(*C["q_ready"].at(g, n - 1))
                    for h in range(2):
                        hh = 2 * n + h
                        for c in range(DC):
                            last = mm3(ps[:, 1 + n % 2, h * TG:(h + 1) * TG], wM_hi[:, hh, c * DV:(c + 1) * DV],
                                       wM_lo[:, hh, c * DV:(c + 1) * DV], xT_hi[:, c, :], xT_lo[:, c, :],
                                       c == 0, c == DC - 1)
                    last.then_inc(*C["q_done"].up())

            def scores(u):
                pe.wait_ge(*C["mask_ready"].at(g, 2))
                for s in range(2):
                    if u:
                        pe.wait_ge(*C["shifted"].at(g, s + 1))
                    nc.tensor.matmul(ps[:, 3 + s, :], ones_row, mask_rows.rearrange("p a n -> p (a n)"),
                                     start=True, stop=False)
                    pe.wait_ge(*C["q_ready"].at(g, u * PAIRS1 + 2 * s + 2))
                    for jj in range(2):
                        for b in range(BG):
                            k = jj * BG + b
                            last = nc.tensor.matmul(ps[:, 3 + s, k * S:(k + 1) * S],
                                                    qt[:, 2 * s + jj, b].rearrange("p h n -> p (h n)"),
                                                    ctx_g[:, b * S:(b + 1) * S], start=False, stop=k == 7)
                    last.then_inc(*C["scores_done"].up())

            def mix(u):
                for s in range(2):
                    n = 2 * u + s
                    pe.wait_ge(*C["probs_ready"].at(g, n + 1))
                    if n:
                        pe.wait_ge(*C["pT_lo"].at(g, n))
                    for k in range(4):
                        last = nc.tensor.transpose(ps[:, 5, k * P:(k + 1) * P],
                                                   pC[:, s, 2 * k:2 * k + 2, :].rearrange("p a b -> p (a b)"), ident)
                    last.then_inc(*C["pT_done"].up())
                pe.wait_ge(*C["cx_lo"].at(g, 1))
                pe.wait_ge(*C["pT_lo"].at(g, 2 * u + 2))
                for t in range(TILES):
                    for b in range(2):
                        n = u * BG + 2 * t + b
                        if n >= 2:
                            pe.wait_ge(*C["z_lo"].at(g, n - 1))
                        r = slice(S * b, S * b + S)
                        mm3(ps[:, 6 + b, :], cx_hi[r, t, :], cx_lo[r, t, :], pT_hi[r, t, :], pT_lo[r, t, :],
                            True, True).then_inc(*C["z_done"].up())

            def output(u):
                pe.wait_ge(*C["z_lo"].at(g, (u + 1) * BG))
                if u:
                    pe.wait_ge(*C["x_done"].at(g, 1))
                for t in range(TILES):
                    for h in range(HALF):
                        hh = u * HALF + h
                        last = mm3(ps[:, 0, t * D:(t + 1) * D], z_hi[:, h, t * P:(t + 1) * P],
                                   z_lo[:, h, t * P:(t + 1) * P], wN_hi[:, hh, :], wN_lo[:, hh, :],
                                   h == 0, h == HALF - 1)
                last.then_inc(*C["out_done"].up())

            queries(0)
            scores(0)
            queries(1)
            mix(0)
            scores(1)
            output(0)
            mix(1)
            output(1)
            pe.wait_ge(*C["x_done"].at(g, 2))

        ctx_g = sb("ctx_g", [P, TG])

        def act_C(act, g):
            upper_x(act, g, C)

            def queries(u):
                for j in range(PAIRS1):
                    n = u * PAIRS1 + j
                    act.wait_ge(*C["q_done"].at(g, n + 1))
                    if u:
                        act.wait_ge(*C["scores_done"].at(g, j // 2 + 1))
                    nc.scalar.copy(qt[:, j].rearrange("p b h n -> p h b n"),
                                   ps[:, 1 + n % 2, :].rearrange("p (h b n) -> p h b n", h=2, b=BG)
                                   ).then_inc(*C["q_ready"].up())

            def exps(u):
                for s in range(2):
                    act.wait_ge(*C["shifted"].at(g, 2 * u + s + 1))
                    v = split_tokens(pC[:, s])
                    nc.scalar.activation(v, v, ACT.Exp, scale=HD1 ** -0.5).then_inc(*C["exp_ready"].up())

            def upper_probs(u):
                for s in range(2):
                    act.wait_ge(*C["pT_done"].at(g, 2 * u + s + 1))
                    dst = pT_hi.rearrange("p t (j n) -> p t j n", j=PAIRS1)[:, :, 2 * s:2 * s + 2, :]
                    nc.scalar.copy(dst.rearrange("p t j n -> p j t n"),
                                   ps[:, 5, :].rearrange("p (j t n) -> p j t n", j=2, t=2)).then_inc(*C["pT_hi"].up())

            def upper_z(u):
                for k in range(BG):
                    act.wait_ge(*C["z_done"].at(g, u * BG + k + 1))
                    if u and k == 0:
                        act.wait_ge(*C["out_done"].at(g, 1))
                    nc.scalar.copy(z_hi[:, :, k * S:(k + 1) * S],
                                   ps[:, 6 + k % 2, :].rearrange("p (h n) -> p h n", h=HALF)).then_inc(*C["z_hi"].up())

            queries(0)
            act.wait_ge(*C["ctx_masked"].at(g, TILES))
            nc.scalar.copy(split_tokens(cx_hi), split_tokens(ctx_n)).then_inc(*C["cx_hi"].up())
            exps(0)
            queries(1)
            upper_probs(0)
            upper_z(0)
            exps(1)
            for r in range(3):
                act.wait_ge(*C["chosen"].at(g, 3 * r + 3))
                nc.scalar.copy(decoded((fg_hi, fu_hi, fd_hi), g, r), shape_r(lev[:, 0, 0:ROUNDS[r]], r)
                               ).then_inc(*C["dec_hi"].up())
            upper_probs(1)
            upper_z(1)
            act.wait_ge(*C["x_done"].at(g, 2))

        def dve_C(dve, g):
            normalise(dve, g, C)
            nc.vector.tensor_scalar(mask_rows, mask_row8[:, bass.ds(g * TG, TG)].unsqueeze(1)
                                    .broadcast_to([1, 2, TG]), -1.0, MASKED, ALU.add, ALU.mult
                                    ).then_inc(*C["mask_ready"].up())
            nc.vector.tensor_copy(ctx_g, ctx_T[:, bass.ds(g * TG, TG)]).then_inc(*C["mask_ready"].up())
            lower_x(dve, g, C)
            dve.wait_ge(C_nat_in, g * 16 + 16)
            for t in range(TILES):
                nc.vector.tensor_scalar(ctx_n[:, t, :], ctx_n[:, t, :], mask_n[:, bass.ds(g * TILES + t, 1)], None,
                                        ALU.mult).then_inc(*C["ctx_masked"].up())

            def shift(u):
                for s in range(2):
                    n = 2 * u + s
                    dve.wait_ge(*C["scores_done"].at(g, n + 1))
                    sc = ps[:, 3 + s, :].rearrange("p (k n) -> p k n", k=8)
                    nc.vector.tensor_reduce(mxC[:, n, :], sc, AX, ALU.max).then_inc(*C["maxed"].up())
                    dve.wait_ge(*C["maxed"].at(g, n + 1))
                    if u:
                        dve.wait_ge(*C["pT_done"].at(g, s + 1))
                    nc.vector.tensor_tensor(pC[:, s], sc, bc_last(mxC[:, n, :], S),
                                            ALU.subtract).then_inc(*C["shifted"].up())

            def sums(u):
                for s in range(2):
                    n = 2 * u + s
                    dve.wait_ge(*C["exp_ready"].at(g, n + 1))
                    nc.vector.tensor_reduce(smC[:, n, :], pC[:, s], AX, ALU.add).then_inc(*C["summed"].up())
                    dve.wait_ge(*C["summed"].at(g, n + 1))
                    nc.vector.reciprocal(rcC[:, n, :], smC[:, n, :]).then_inc(*C["recip_ready"].up())

            def lower_probs(u):
                for s in range(2):
                    dve.wait_ge(*C["pT_hi"].at(g, 2 * u + s + 1))
                    lo, hi = (v.rearrange("p t (j n) -> p t j n", j=PAIRS1)[:, :, 2 * s:2 * s + 2, :]
                              .rearrange("p t j n -> p j t n") for v in (pT_lo, pT_hi))
                    nc.vector.tensor_tensor(lo, ps[:, 5, :].rearrange("p (j t n) -> p j t n", j=2, t=2),
                                            hi.bitcast(F32), ALU.subtract).then_inc(*C["pT_lo"].up())

            def lower_z(u):
                for k in range(BG):
                    dve.wait_ge(*C["z_hi"].at(g, u * BG + k + 1))
                    nc.vector.tensor_tensor(z_lo[:, :, k * S:(k + 1) * S],
                                            ps[:, 6 + k % 2, :].rearrange("p (h n) -> p h n", h=HALF),
                                            z_hi[:, :, k * S:(k + 1) * S].bitcast(F32),
                                            ALU.subtract).then_inc(*C["z_lo"].up())

            def add(u):
                dve.wait_ge(*C["out_done"].at(g, u + 1))
                if u:
                    dve.wait_ge(*C["x_done"].at(g, 1))
                xg = x[:, bass.ds(g * TILES, TILES), :]
                nc.vector.scalar_tensor_tensor(out=xg, in0=ps[:, 0, :].rearrange("p (t n) -> p t n", t=TILES),
                                               scalar=tg[:, 2:3], in1=xg, op0=ALU.mult,
                                               op1=ALU.add).then_inc(*C["x_done"].up())

            def decode(r):
                n, o = ROUNDS[r], sum(ROUNDS[:r])
                if r == 0:
                    dve.wait_ge(C_idx_in, g * 16 + 16)
                else:
                    dve.wait_ge(*C["level1"].at(g, 8 * r))
                    dve.wait_ge(*C["chosen"].last(g))
                for bit in range(4):
                    nc.vector.tensor_scalar(bits[:, bit, 0:n], idx[:, o:o + n], 1 << bit, None,
                                            ALU.bitwise_and).then_inc(*C["bits"].up())
                dve.wait_ge(*C["level1"].at(g, 8 * r + 8))
                for i, step in enumerate((1, 2, 4)):
                    left, right = (lev[:, k::2 * step, 0:n] for k in (0, step))
                    m = bits[:, i + 1:i + 2, 0:n].broadcast_to([P, 4 // step, n])
                    if i:
                        dve.wait_ge(*C["chosen"].last(g))
                    else:
                        dve.wait_ge(*C["bits"].at(g, 4 * r + 4))
                    dve.sem_inc(waited, 1)
                    nc.vector.copy_predicated(left, m, right).then_inc(*C["chosen"].up())

            shift(0)
            dve.wait_ge(*C["cx_hi"].at(g, 1))
            nc.vector.tensor_tensor(split_tokens(cx_lo), split_tokens(ctx_n), split_tokens(cx_hi).bitcast(F32),
                                    ALU.subtract).then_inc(*C["cx_lo"].up())
            sums(0)
            decode(0)
            lower_probs(0)
            lower_z(0)
            shift(1)
            sums(1)
            decode(1)
            decode(2)
            lower_probs(1)
            add(0)
            lower_z(1)
            dve.wait_ge(*C["dec_lo"].at(g, 3))
            add(1)
            dve.wait_ge(*C["x_done"].at(g, 2))

        def pool_C(pool, g):
            inverse_root(pool, g, C)

            def scale(u):
                for s in range(2):
                    n = 2 * u + s
                    pool.wait_ge(*C["recip_ready"].at(g, n + 1))
                    nc.gpsimd.tensor_tensor(pC[:, s], pC[:, s], bc_last(rcC[:, n, :], S),
                                            ALU.mult).then_inc(*C["probs_ready"].up())

            def level1(r):
                n = ROUNDS[r]
                pool.wait_ge(*C["bits"].at(g, 4 * r + 1))
                if r:
                    pool.wait_ge(*C["dec_lo"].at(g, r))
                pool.sem_inc(waited, 1)
                for j in range(8):
                    nc.gpsimd.tensor_scalar(lev[:, j, 0:n], bits[:, 0, 0:n], lut_step[:, j:j + 1],
                                            lut[:, 2 * j:2 * j + 1], ALU.mult, ALU.add).then_inc(*C["level1"].up())

            def lower(r):
                pool.wait_ge(*C["dec_hi"].at(g, r + 1))
                nc.gpsimd.tensor_tensor(decoded((fg_lo, fu_lo, fd_lo), g, r), shape_r(lev[:, 0, 0:ROUNDS[r]], r),
                                        decoded((fg_hi, fu_hi, fd_hi), g, r).bitcast(F32),
                                        ALU.subtract).then_inc(*C["dec_lo"].up())

            scale(0)
            level1(0)
            scale(1)
            lower(0)
            level1(1)
            lower(1)
            level1(2)
            lower(2)
            pool.wait_ge(*C["x_done"].at(g, 2))

        def sp_C(sp, g):
            sp.dma_start(ctx_n, a["ctx_n"][bass.ds(g * TILES, TILES)].rearrange("t p n -> p t n")).then_inc(C_nat_in, 16)
            sp.dma_start(idx, a["idx"][bass.ds(g, 1)].rearrange("o p n -> p (o n)")).then_inc(C_idx_in, 16)
            sp.wait_ge(C_nat_in, g * 16 + 16)
            sp.sem_inc(waited, 1)
            sp.wait_ge(C_idx_in, g * 16 + 16)
            sp.sem_inc(waited, 1)
            sp.wait_ge(*C["x_done"].at(g, 2))
            sp.sem_inc(waited, 1)

        take = carver(work)
        fth, fh1, fh3 = ([take(TG), take(TG)] for _ in range(3))
        take_r = carver(workr)
        fh_hi, fh_lo = ([take_r(TG), take_r(TG)] for _ in range(2))

        def rows_D(k):
            return P if k < FC - 1 else FLAST

        def pe_D(pe, g):
            turn_x(pe, g, Dp)
            x_split(pe, g, Dp)

            def gate_up(k):
                if k >= 2:
                    pe.wait_ge(*Dp["h3"].at(g, k - 1))
                for i, (w_hi, w_lo) in enumerate(((fg_hi, fg_lo), (fu_hi, fu_lo))):
                    for c in range(DC):
                        last = mm3(ps[:, 3 + k % 2, i * TG:(i + 1) * TG], w_hi[:, c, k * P:(k + 1) * P],
                                   w_lo[:, c, k * P:(k + 1) * P], xT_hi[:, c, :], xT_lo[:, c, :], c == 0, c == DC - 1)
                last.then_inc(*Dp["gu_done"].up())

            def down(k):
                n = rows_D(k)
                pe.wait_ge(*Dp["h_hi"].at(g, k + 1))
                pe.wait_ge(*Dp["h_lo"].at(g, k + 1))
                for t in range(TILES):
                    last = mm3(ps[:, 6 + t, 0:D], fh_hi[k % 2][0:n, t * P:(t + 1) * P],
                               fh_lo[k % 2][0:n, t * P:(t + 1) * P], fd_hi[0:n, k, :], fd_lo[0:n, k, :],
                               k == 0, k == FC - 1)
                return last

            gate_up(0)
            gate_up(1)
            down(0)
            for k in range(2, FC):
                gate_up(k)
                down(k - 1)
            down(FC - 1).then_inc(*Dp["out_done"].up())
            pe.wait_ge(*Dp["x_done"].at(g, TILES))

        def act_D(act, g):
            upper_x(act, g, Dp)

            def tanh(k):
                n = rows_D(k)
                act.wait_ge(*Dp["gu_done"].at(g, k + 1))
                nc.scalar.activation(fth[k % 2][0:n], ps[0:n, 3 + k % 2, 0:TG], ACT.Tanh,
                                     scale=0.5).then_inc(*Dp["tanh_ready"].up())

            def upper(k):
                n = rows_D(k)
                act.wait_ge(*Dp["h3"].at(g, k + 1))
                nc.scalar.copy(fh_hi[k % 2][0:n], fh3[k % 2][0:n]).then_inc(*Dp["h_hi"].up())

            tanh(0)
            tanh(1)
            upper(0)
            for k in range(2, FC):
                tanh(k)
                upper(k - 1)
            upper(FC - 1)
            act.wait_ge(*Dp["x_done"].at(g, TILES))

        def dve_D(dve, g):
            normalise(dve, g, Dp)
            lower_x(dve, g, Dp)
            for k in range(FC):
                n = rows_D(k)
                dve.wait_ge(*Dp["tanh_ready"].at(g, k + 1))
                nc.vector.scalar_tensor_tensor(out=fh1[k % 2][0:n], in0=fth[k % 2][0:n], scalar=1.0,
                                               in1=ps[0:n, 3 + k % 2, 0:TG], op0=ALU.add,
                                               op1=ALU.mult).then_inc(*Dp["h1"].up())
                dve.wait_ge(*Dp["h1"].at(g, k + 1))
                nc.vector.scalar_tensor_tensor(out=fh3[k % 2][0:n], in0=fh1[k % 2][0:n], scalar=0.5,
                                               in1=ps[0:n, 3 + k % 2, TG:2 * TG], op0=ALU.mult,
                                               op1=ALU.mult).then_inc(*Dp["h3"].up())
            dve.wait_ge(*Dp["out_done"].at(g, 1))
            for t in range(TILES):
                xt = x[:, g * TILES + t, :]
                nc.vector.scalar_tensor_tensor(out=xt, in0=ps[:, 6 + t, 0:D], scalar=tg[:, 3:4], in1=xt,
                                               op0=ALU.mult, op1=ALU.add).then_inc(*Dp["x_done"].up())
            dve.wait_ge(*Dp["x_done"].at(g, TILES))

        def pool_D(pool, g):
            inverse_root(pool, g, Dp)
            for k in range(FC):
                n = rows_D(k)
                pool.wait_ge(*Dp["h_hi"].at(g, k + 1))
                nc.gpsimd.tensor_tensor(fh_lo[k % 2][0:n], fh3[k % 2][0:n], fh_hi[k % 2][0:n].bitcast(F32),
                                        ALU.subtract).then_inc(*Dp["h_lo"].up())
            pool.wait_ge(*Dp["x_done"].at(g, TILES))

        def sp_D(sp, g):
            sp.wait_ge(*Dp["x_done"].at(g, TILES))
            sp.dma_start(a["out"][bass.ds(g * TILES, TILES)].rearrange("t p n -> p t n"),
                         x[:, bass.ds(g * TILES, TILES), :]).then_inc(out_done, 16)

        block = ctx.enter_context(nc.Block())

        @block.sync
        def _(sp):
            sp.dma_start(x, a["x"].rearrange("t p n -> p t n")).then_inc(x_in, 16)
            sp.dma_start(stage[:, 0:NWA], a["wA"]).then_inc(wA_in, 16)
            sp.dma_start(ctx_T, a["ctx_T"]).then_inc(ctxT_in, 16)
            sp.dma_start(const, a["const"]).then_inc(const_in, 16)
            sp.dma_start(vec, a["vec"].partition_broadcast(P)).then_inc(vec_in, 16)
            for b in range(2):
                for (lo, hi), v in zip(PARTS, (a["vec_main"], a["vec_last"])):
                    sp.dma_start(veck[b * S + lo:b * S + hi, :], v.partition_broadcast(hi - lo)).then_inc(vec_in, 16)
            sp.dma_start(gates, a["gates"].partition_broadcast(P)).then_inc(gates_in, 16)
            sp.dma_start(lut, a["lut"].partition_broadcast(P)).then_inc(lut_in, 16)
            sp.dma_start(mask_row8, a["mask_row"]).then_inc(mask_in, 16)
            sp.dma_start(mask_n8, a["mask_n"]).then_inc(mask_in, 16)
            sp.wait_ge(setup_dve, 2)
            sp.dma_start(stage[:, GB:GB + NWS], a["wS"]).then_inc(wS_in, 16)
            sp.dma_start(stage[0:E + 1, 0:NSEL], a["sel"]).then_inc(sel_in, 16)
            sp.wait_ge(setup_act, 4)
            with sp.Fori(0, GROUPS) as g:
                sp_A(sp, g)
            sp.wait_ge(setup_dve, 5)
            with sp.Fori(0, GROUPS) as g:
                sp_B(sp, g)
            with sp.Fori(0, GROUPS) as g:
                sp_C(sp, g)
            with sp.Fori(0, GROUPS) as g:
                sp_D(sp, g)
            sp.wait_ge(out_done, 16 * GROUPS)

        @block.tensor
        def _(pe):
            pe.wait_ge(const_in, 16)
            pe.wait_ge(setup_dve, 2)
            with pe.Fori(0, GROUPS) as g:
                pe_A(pe, g)
            pe.wait_ge(setup_dve, 5)
            pe.wait_ge(setup_act, 4)
            with pe.Fori(0, GROUPS) as g:
                pe_B(pe, g)
            with pe.Fori(0, GROUPS) as g:
                pe_C(pe, g)
            with pe.Fori(0, GROUPS) as g:
                pe_D(pe, g)

        @block.scalar
        def _(act):
            act.wait_ge(wA_in, 16)
            nc.scalar.copy(wA_hi, stage[:, 0:NWA]).then_inc(setup_act, 1)
            act.wait_ge(gates_in, 16)
            nc.scalar.activation(tg, gates, ACT.Tanh).then_inc(setup_act, 1)
            act.wait_ge(wS_in, 16)
            nc.scalar.copy(wS_hi, stage[:, GB:GB + NWS]).then_inc(setup_act, 1)
            act.wait_ge(sel_in, 16)
            nc.scalar.copy(sel.rearrange("p k n -> p (k n)"), stage[0:E + 1, 0:NSEL]).then_inc(setup_act, 1)
            act.wait_ge(ctxT_in, 16)
            act.wait_ge(const_in, 16)
            act.wait_ge(setup_pool, 3)
            with act.Fori(0, GROUPS) as g:
                act_A(act, g)
            with act.Fori(0, GROUPS) as g:
                act_B(act, g)
            with act.Fori(0, GROUPS) as g:
                act_C(act, g)
            with act.Fori(0, GROUPS) as g:
                act_D(act, g)

        @block.vector
        def _(dve):
            dve.wait_ge(setup_act, 1)
            nc.vector.tensor_tensor(wA_lo, stage[:, 0:NWA], wA_hi.bitcast(F32), ALU.subtract).then_inc(setup_dve, 1)
            dve.wait_ge(lut_in, 16)
            lp = lut.rearrange("p (j b) -> p j b", b=2)
            nc.vector.tensor_tensor(lut_step, lp[:, :, 1], lp[:, :, 0], ALU.subtract).then_inc(setup_dve, 1)
            dve.wait_ge(mask_in, 32)
            nc.vector.tensor_copy(mask_n, mask_n8).then_inc(setup_dve, 1)
            nc.vector.memset(ones_row, 1.0).then_inc(setup_dve, 1)
            dve.wait_ge(setup_act, 3)
            nc.vector.tensor_tensor(wS_lo, stage[:, GB:GB + NWS], wS_hi.bitcast(F32),
                                    ALU.subtract).then_inc(setup_dve, 1)
            dve.wait_ge(x_in, 16)
            dve.wait_ge(ctxT_in, 16)
            dve.wait_ge(vec_in, 16 * 5)
            with dve.Fori(0, GROUPS) as g:
                dve_A(dve, g)
            dve.wait_ge(const_in, 16)
            with dve.Fori(0, GROUPS) as g:
                dve_B(dve, g)
            pad = [w[:, :, INTER:FC * P].bitcast(F32) for w in (fg_hi, fg_lo, fu_hi, fu_lo)]
            for w in pad:
                nc.vector.memset(w, 0.0).then_inc(setup_dve, 1)
            with dve.Fori(0, GROUPS) as g:
                dve_C(dve, g)
            with dve.Fori(0, GROUPS) as g:
                dve_D(dve, g)

        @block.gpsimd
        def _(pool):
            for c in range(3):
                v = (workr[:, 0:4 * TG].bitcast(F32), expo, None)[c]
                if c < 2:
                    nc.gpsimd.memset(v, (0.0, -0.5)[c]).then_inc(setup_pool, 1)
            pool.wait_ge(setup_pool, 2)
            nc.gpsimd.memset(xn[:, :, 0:1], 0.0).then_inc(setup_pool, 1)
            pool.wait_ge(vec_in, 16 * 5)
            with pool.Fori(0, GROUPS) as g:
                pool_A(pool, g)
            with pool.Fori(0, GROUPS) as g:
                pool_B(pool, g)
            pool.wait_ge(setup_dve, 2)
            with pool.Fori(0, GROUPS) as g:
                pool_C(pool, g)
            with pool.Fori(0, GROUPS) as g:
                pool_D(pool, g)

        for name, phase in (("A", A), ("B", Bp), ("C", C), ("D", Dp)):
            for key, s in phase.items():
                assert s.n == s.per_group, (name, key, s.n, s.per_group)


def laid_out(i):
    f = {}
    f["x"] = i["x"].reshape(GROUPS * TILES, P, D)
    c = i["ctx_1024"].reshape(B * S, DV)
    f["ctx_T"] = c.T
    f["ctx_n"] = c.reshape(GROUPS * TILES, P, DV)

    def chunks(w):
        return w.reshape(-1, P, w.shape[1]).transpose(1, 0, 2).reshape(P, -1)

    def by_head(w):
        return w.reshape(w.shape[:-1] + (H0, 2, HD0)).swapaxes(-3, -2).reshape(w.shape)

    wkv = by_head(np.concatenate([i["L0_xattn_Wk"], i["L0_xattn_Wv"]], axis=1))
    f["wA"] = np.concatenate([chunks(i["L0_xattn_Wq"]), wkv, i["L0_xattn_Wkv_dca"], chunks(i["L0_xattn_Wo"])], axis=1)
    f["vec"] = np.concatenate([i["L0_xattn_bq"], i["L0_xattn_bo"], i["L0_xattn_qn_w"], i["L0_xattn_qn_b"]])
    bkv = by_head(np.concatenate([i["L0_xattn_bk"], i["L0_xattn_bv"]]))
    f["vec_main"] = np.concatenate([bkv, i["L0_xattn_kn_w"], i["L0_xattn_kn_b"]])
    f["vec_last"] = np.concatenate([i["L0_xattn_bkv_dca"], i["L0_xattn_kn_dca_w"], i["L0_xattn_kn_dca_b"]])
    f["gates"] = np.stack([i["g_xattn"], i["g_ffn"]], axis=1).reshape(-1)
    parts = []
    for w in (i["L0_ffn_Wg"], i["L0_ffn_Wu"]):
        parts.append(w.reshape(GROUPS, 4, DC, P, F).transpose(0, 3, 2, 1, 4).reshape(GROUPS, P, -1))
    parts.append(i["L0_ffn_Wd"].reshape(GROUPS, 2, P, D).transpose(0, 2, 1, 3).reshape(GROUPS, P, -1))
    f["wB"] = np.concatenate(parts, axis=2)
    sgu = chunks(np.concatenate([i["L0_ffn_sWg"], i["L0_ffn_sWu"]], axis=1))
    sd = np.concatenate([i["L0_ffn_sWd"], np.zeros_like(i["L0_ffn_sWd"])])
    router = np.concatenate([i["L0_ffn_gate_w"].T, i["L0_ffn_shared_gate_w"],
                             np.zeros_like(i["L0_ffn_shared_gate_w"])], axis=1)
    f["wS"] = np.concatenate([sgu, sd, chunks(router)], axis=1)
    q = i["L1_xattn_Wq"].reshape(D, GROUPS, HG, HD1).transpose(1, 3, 2, 0).reshape(GROUPS, P, -1)
    k, v = (i[n].reshape(DV, GROUPS, HG // 2, HD1).transpose(1, 3, 2, 0).reshape(GROUPS, P, -1)
            for n in ("L1_xattn_Wk", "L1_xattn_Wv"))
    o = i["L1_xattn_Wo"].reshape(GROUPS, HG, HD1, D).transpose(0, 2, 1, 3).reshape(GROUPS, P, -1)
    f["wC"] = np.concatenate([q, k, v, o], axis=2)
    up = [i[n].T.reshape(DC, P, GROUPS, IG).transpose(2, 1, 0, 3).reshape(GROUPS, P, -1)
          for n in ("L1_ffn_gate_idx", "L1_ffn_up_idx")]
    d = i["L1_ffn_down_idx"].T
    d = np.concatenate([d, np.zeros((FC * P - INTER, D), d.dtype)]).reshape(FC, P, GROUPS, DG)
    f["idx"] = np.concatenate(up + [d.transpose(2, 1, 0, 3).reshape(GROUPS, P, -1)], axis=2)
    f["lut"] = i["L1_ffn_lut"]
    m = i["mask_BxS2_bf1"].view(np.uint8)
    f["mask_row"] = m.reshape(1, B * S)
    f["mask_n"] = m.reshape(GROUPS * TILES, P).T
    const = np.zeros((P, NCONST), np.float32)
    const[:, 0:P] = np.eye(P)
    const[:, P] = np.arange(P) // HD0 % 2 == 0
    const[:, P + 1] = np.arange(P) // HD0 % 2 == 1
    const[:, P + 2:P + 2 + E] = np.arange(E)
    f["const"] = const
    sel = np.zeros((E + 1, EC + 1, P), np.float32)
    for k_ in range(EC):
        for e in range(2):
            sel[2 * k_ + e, k_, e * F:(e + 1) * F] = 1
    sel[E, EC, :] = 1
    f["sel"] = sel.reshape(E + 1, NSEL)
    return {k_: np.ascontiguousarray(v_) for k_, v_ in f.items()}


def kernel(**inputs):
    import concourse.bacc as bacc
    from concourse.bass_utils import run_bass_kernel_spmd

    arrays = laid_out({k: np.asarray(v) for k, v in inputs.items()})
    nc = bacc.Bacc("TRN2", target_bir_lowering=False, num_devices=1)
    a = {k: nc.dram_tensor(f"in_{k}", v.shape, mybir.dt.from_np(v.dtype), kind="ExternalInput").ap()
         for k, v in arrays.items()}
    a["out"] = nc.dram_tensor("out", (GROUPS * TILES, P, D), F32, kind="ExternalOutput").ap()
    build(nc, a)
    r = run_bass_kernel_spmd(nc, [{f"in_{k}": v for k, v in arrays.items()}], core_ids=[0])
    return r.results[0]["out"].reshape(B, S, D)
```

```python
from contextlib import ExitStack

import numpy as np

import concourse.bass as bass
from concourse import mybir

ALU = mybir.AluOpType
ACT = mybir.ActivationFunctionType
F32 = mybir.dt.float32
F32R = mybir.dt.float32r
BF16 = mybir.dt.bfloat16
I32 = mybir.dt.int32
U32 = mybir.dt.uint32
U8 = mybir.dt.uint8
AX = mybir.AxisListType.X

P = 128
B, S, D = 16, 64, 256
DV = 128
GROUPS = 4
TG = B * S // GROUPS
BG = TG // S
TILES = TG // P
DC = D // P
H0, HD0 = 16, 16
DCA = 16
MAIN = S - DCA
PARTS = ((0, MAIN), (MAIN, S))
PAIRS0 = 4
E, F, TOPK = 16, 64, 4
EC = E * F // P
NL = E + 2
H1, HD1, KV1 = 16, 128, 8
HALF = H1 // 2
PAIRS1 = HALF // 2
HG = H1 // GROUPS
INTER, LUT = 688, 16
FC = -(-INTER // P)
FLAST = INTER - (FC - 1) * P
IG = INTER // GROUPS
DG = D // GROUPS
ROUNDS = (DC * IG, DC * IG, FC * DG)
RMAX = max(ROUNDS)
MASKED = 1e30

NVEC = D + D + 2 * HD0
NVK = 2 * D + 2 * HD0
NWA = 2 * DC * D + 4 * D
GB = 2 * DC * 4 * F + 2 * D
NWS = DC * 2 * F + D + DC * NL
GCW = HG * D + HG // 2 * 2 * DV + HG * D
NCONST = P + 2 + E
NSEL = (EC + 1) * P


class Signal:

    def __init__(self, sem, per_group):
        self.sem, self.per_group, self.n = sem, per_group, 0

    def up(self):
        self.n += 1
        return self.sem, 1

    def at(self, g, n):
        return self.sem, g * self.per_group + n

    def last(self, g):
        return self.at(g, self.n)


def build(nc, a):
    ctx = ExitStack()
    with ctx:
        def sb(name, shape, dt=F32):
            return ctx.enter_context(nc.sbuf_tensor(name, shape, dt))[:]

        def sem(name):
            return ctx.enter_context(nc.semaphore(name))

        def signals(phase, **per_group):
            return {k: Signal(sem(f"{phase}_{k}"), n) for k, n in per_group.items()}

        ps = ctx.enter_context(nc.psum_tensor("ps", [P, 8, 512], F32))[:]

        x = sb("x", [P, GROUPS * TILES, D])
        ctx_T = sb("ctx_T", [P, B * S])
        ctx_n = sb("ctx_n", [P, TILES, DV])
        const = sb("const", [P, NCONST])
        ident, parity = const[:, 0:P], const[:, P:P + 2]
        iota = const[:, P + 2:P + 2 + E]
        gates = sb("gates", [P, 4])
        tg = sb("tg", [P, 4])
        expo = sb("expo", [P, TILES])
        lut = sb("lut", [P, LUT])
        lut_step = sb("lut_step", [P, LUT // 2])
        mask_row8 = sb("mask_row8", [1, B * S], U8)
        mask_rows = sb("mask_rows", [1, 2, TG], BF16)
        ones_row = sb("ones_row", [1, P], BF16)
        mask_n8 = sb("mask_n8", [P, GROUPS * TILES], U8)
        mask_n = sb("mask_n", [P, GROUPS * TILES])
        xn = sb("xn", [P, TILES, D])
        stats = sb("stats", [P, TILES, 6])
        mv = sb("mv", [P, TILES, 2])
        ve = sb("ve", [P, TILES])
        rstd = sb("rstd", [P, TILES])
        xT_hi = sb("xT_hi", [P, DC, TG], F32R)
        xT_lo = sb("xT_lo", [P, DC, TG], F32R)
        shared_r = sb("shared_r", [P, 2 * NWA], F32R)
        wB_hi = sb("wB_hi", [P, GROUPS * GB], F32R)
        wB_lo = sb("wB_lo", [P, GROUPS * GB], F32R)
        wS_hi = sb("wS_hi", [P, NWS], F32R)
        wS_lo = sb("wS_lo", [P, NWS], F32R)
        stage = sb("stage", [P, GCW])
        with nc.sbuf_tensor("workA", [P, 13248], F32) as early, \
                nc.sbuf_tensor("workAr", [P, 4 * TG + 2 * DC * TG], F32R) as early_r:
            workA, workAr = early[:], early_r[:]
        wM_hi = sb("wM_hi", [P, H1, D], F32R)
        wM_lo = sb("wM_lo", [P, H1, D], F32R)
        wN_hi = sb("wN_hi", [P, H1, D], F32R)
        wN_lo = sb("wN_lo", [P, H1, D], F32R)
        work = sb("work", [P, 7800])
        workr = sb("workr", [P, 8 * TG + NSEL], F32R)

        def carver(pool):
            at = [0]

            def carve(n):
                at[0] += n
                assert at[0] <= pool.shape[1], at
                return pool[:, at[0] - n:at[0]]
            return carve

        def split_tokens(v):
            return v.rearrange("p c n -> p (c n)")

        def bc_last(v, n):
            return v.unsqueeze(2).broadcast_to([v.shape[0], v.shape[1], n])

        def bc_mid(v, n):
            return v.unsqueeze(1).broadcast_to([v.shape[0], n, v.shape[1]])

        def wA(w):
            return (w[:, 0:DC * D].rearrange("p (c n) -> p c n", c=DC), w[:, DC * D:DC * D + 2 * D],
                    w[:, DC * D + 2 * D:DC * D + 4 * D], w[:, DC * D + 4 * D:NWA].rearrange("p (c n) -> p c n", c=DC))

        wA_hi, wA_lo = shared_r[:, 0:NWA], shared_r[:, NWA:2 * NWA]
        wq_hi, wkv_hi, wkvd_hi, wo_hi = wA(wA_hi)
        wq_lo, wkv_lo, wkvd_lo, wo_lo = wA(wA_lo)

        def wB(w):
            v, n = w.rearrange("p (g n) -> p g n", g=GROUPS), DC * 4 * F
            return (v[:, :, 0:n].rearrange("p g (c n) -> p g c n", c=DC),
                    v[:, :, n:2 * n].rearrange("p g (c n) -> p g c n", c=DC),
                    v[:, :, 2 * n:].rearrange("p g (k n) -> p g k n", k=2))

        eg_hi, eu_hi, ed_hi = wB(wB_hi)
        eg_lo, eu_lo, ed_lo = wB(wB_lo)

        def wS(w):
            n = DC * 2 * F
            return (w[:, 0:n].rearrange("p (c n) -> p c n", c=DC), w[0:F, n:n + D],
                    w[:, n + D:].rearrange("p (c n) -> p c n", c=DC))

        sgu_hi, sd_hi, wr_hi = wS(wS_hi)
        sgu_lo, sd_lo, wr_lo = wS(wS_lo)

        def wF(w):
            n = DC * FC * P
            return (w[:, 0:n].rearrange("p (c n) -> p c n", c=DC), w[:, n:2 * n].rearrange("p (c n) -> p c n", c=DC),
                    w[:, 2 * n:2 * n + FC * D].rearrange("p (c n) -> p c n", c=FC))

        fg_hi, fu_hi, fd_hi = wF(wB_hi)
        fg_lo, fu_lo, fd_lo = wF(wB_lo)

        waited = sem("waited")
        const_in, gates_in, x_in, ctxT_in, vec_in, lut_in, mask_in = (
            sem(n) for n in ("const_in", "gates_in", "x_in", "ctxT_in", "vec_in", "lut_in", "mask_in"))
        wA_in, wS_in, sel_in, setup_pool, setup_act, setup_dve, out_done = (
            sem(n) for n in ("wA_in", "wS_in", "sel_in", "setup_pool", "setup_act", "setup_dve", "out_done"))

        front = signals("front", stat=4, var_ready=1, rstd_ready=1, xn_ready=2, xT_done=1, hi_ready=1, lo_ready=1)
        A = signals("A", dve=6, act=1, pool=2, ctx_hi=2, ctx_lo=2, kv_done=2, q_done=1, kv_ready=6, q_ready=1,
                    centred=1, squared=1, grp_var=1, grp_guess=1, scaled=1, qk_ready=2, qT_done=2, kT_ready=PAIRS0,
                    qx_ready=2, scores_done=2, maxed=4, shifted=4, exp_ready=2, summed=4, recip_ready=2,
                    probs_ready=4, pT_done=2, pT_ready=2, pv_done=1, an_ready=4, anT_done=1, an_hi=1, an_lo=1,
                    o_done=1, o_biased=1, x_done=1, prep_hi=1, prep_lo=1)
        A_prep_in = sem("A_prep_in")
        CH = EC + 1
        Bp = signals("B", dve=12, logits_done=1, shifted=1, exp_ready=1, gate_ready=1, comb_ready=2,
                     combT_done=1, combT_hi=1, combT_lo=1, gu_done=CH, tanh_ready=CH, h1=CH, h2=CH, bc_done=CH,
                     h3=CH, h_hi=CH, h_lo=CH, out_done=1, x_done=TILES, join_done=4, join_hi=4, join_lo=4)
        B_prep_in = sem("B_prep_in")
        C = signals("C", mask_ready=2, ctx_masked=TILES, cx_hi=1, cx_lo=1, q_done=2 * PAIRS1, q_ready=2 * PAIRS1,
                    scores_done=4, maxed=4, shifted=4, exp_ready=4, summed=4, recip_ready=4, probs_ready=4,
                    pT_done=4, pT_hi=4, pT_lo=4, z_done=2 * BG, z_hi=2 * BG, z_lo=2 * BG, out_done=2, x_done=2,
                    bits=4 * 3, level1=8 * 3, chosen=3 * 3, dec_hi=3, dec_lo=3)
        C_nat_in, C_idx_in = sem("C_nat_in"), sem("C_idx_in")
        Dp = signals("D", gu_done=FC, tanh_ready=FC, h1=FC, h3=FC, h_hi=FC, h_lo=FC, out_done=1,
                     x_done=TILES)

        def front_stats(dve, f, g):
            for t in range(TILES):
                nc.vector.bn_stats(stats[:, t, :], x[:, g * TILES + t, :]).then_inc(*front["stat"].up())
            for t in range(TILES):
                dve.wait_ge(*front["stat"].at(f, t + 1))
                dve.sem_inc(waited, 1)
                nc.vector.bn_aggr(mv[:, t, :], stats[:, t, :]).then_inc(*front["stat"].up())
            dve.wait_ge(*front["stat"].at(f, 4))
            nc.vector.tensor_scalar(ve, mv[:, :, 1], 1e-5, None, ALU.add).then_inc(*front["var_ready"].up())

        def front_norm(dve, f, g):
            dve.wait_ge(*front["rstd_ready"].at(f, 1))
            for t in range(TILES):
                nc.vector.tensor_scalar(xn[:, t, :], x[:, g * TILES + t, :], mv[:, t, 0:1], rstd[:, t:t + 1],
                                        ALU.subtract, ALU.mult).then_inc(*front["xn_ready"].up())

        def front_dve(dve, f, g):
            front_stats(dve, f, g)
            front_norm(dve, f, g)

        def front_pool(pool, f):
            pool.wait_ge(*front["var_ready"].at(f, 1))
            nc.gpsimd.tensor_tensor(rstd, ve, expo, ALU.pow).then_inc(*front["rstd_ready"].up())

        def turn(src, to):
            for c in range(DC):
                for t in range(TILES):
                    last = nc.tensor.transpose(ps[:, to, c * TG + t * P:c * TG + (t + 1) * P],
                                               src[:, t, c * P:(c + 1) * P], ident)
            return last

        def front_pe(pe, f, to):
            pe.wait_ge(*front["xn_ready"].at(f, TILES))
            turn(xn, to).then_inc(*front["xT_done"].up())

        def front_upper(act, f, to):
            act.wait_ge(*front["xT_done"].at(f, 1))
            nc.scalar.copy(split_tokens(xT_hi), ps[:, to, :]).then_inc(*front["hi_ready"].up())

        def front_lower(dve, f, to):
            dve.wait_ge(*front["hi_ready"].at(f, 1))
            nc.vector.tensor_tensor(split_tokens(xT_lo), ps[:, to, :], split_tokens(xT_hi).bitcast(F32),
                                    ALU.subtract).then_inc(*front["lo_ready"].up())

        def x_split(pe, f):
            pe.wait_ge(*front["hi_ready"].at(f, 1))
            pe.wait_ge(*front["lo_ready"].at(f, 1))

        def after(g):
            return (g + 1) % GROUPS

        def mm3(out, l_hi, l_lo, r_hi, r_lo, start, stop, loose=False):
            for i, (l, r) in enumerate(((l_hi, r_hi), (l_hi, r_lo), (l_lo, r_hi))):
                last = nc.tensor.matmul(out, l, r, start=start and i == 0, stop=stop and i == 2)
            return last

        take = carver(workA)
        qk = take(TILES * 2 * D)
        qk4 = qk.rearrange("p (t k n) -> p t k n", t=TILES, k=2)
        heads = qk.rearrange("p (h n) -> p h n", n=HD0)
        sq = take(TILES * 2 * D)
        probs = take(TILES * 1024).rearrange("p (t k n) -> p t k n", t=TILES, n=S)
        pT = take(TILES * 1024).rearrange("p (t k n) -> p t k n", t=TILES, n=P)
        vz = take(TILES * 8 * 2 * 32).rearrange("p (t k b n) -> p t k b n", t=TILES, k=8, b=2)
        vec, veck = take(NVEC), take(NVK)
        bq, bo, qn_w, qn_b = vec[:, 0:D], vec[:, D:2 * D], vec[:, 2 * D:2 * D + HD0], vec[:, 2 * D + HD0:]
        bkv, kn_w, kn_b = veck[:, 0:2 * D], veck[:, 2 * D:2 * D + HD0], veck[:, 2 * D + HD0:]
        vnext = take(TILES * D).rearrange("p (t n) -> p t n", t=TILES)
        kx = take(DC * BG * PAIRS0 * S).rearrange("p (k a n) -> p k a n", a=PAIRS0, n=S)
        qx = take(2 * DC * TG).rearrange("p (k h n) -> p k h n", h=2, n=S)
        an = take(TILES * D).rearrange("p (t n) -> p t n", t=TILES)
        gsum, gmean, gssq, gvar, gln, guess, gsq, gfix, grs = (take(64) for _ in range(9))
        mxA, smA, rcA = (take(64).rearrange("p (t n) -> p t n", t=TILES) for _ in range(3))
        take_r = carver(workAr)
        ctxm = [take_r(TG).rearrange("p (b n) -> p b n", b=BG) for _ in range(4)]
        aT_hi, aT_lo = (take_r(DC * TG).rearrange("p (c n) -> p c n", c=DC) for _ in range(2))

        def ctx_rows(g, lo, hi):
            return ctx_T[:, bass.ds(g * TG, TG)].rearrange("p (b n) -> p b n", b=BG)[:, :, lo:hi]

        def pe_A_kv(pe, n):
            pe.wait_ge(*A["ctx_hi"].at(n, 2))
            pe.wait_ge(*A["ctx_lo"].at(n, 2))
            for t in range(TILES):
                m = [c.rearrange("p b n -> p (b n)")[:, t * P:(t + 1) * P] for c in ctxm]
                mm3(ps[:, 4 + t, :], m[0], m[1], wkv_hi, wkv_lo, True, False)
                mm3(ps[:, 4 + t, :], m[2], m[3], wkvd_hi, wkvd_lo, False, True).then_inc(*A["kv_done"].up())

        def pe_A_q(pe, n):
            x_split(pe, n)
            pe.wait_ge(*A["kv_ready"].at(n, 2))
            for t in range(TILES):
                for c in range(DC):
                    last = mm3(ps[:, 4, t * D:(t + 1) * D], xT_hi[:, c, t * P:(t + 1) * P],
                               xT_lo[:, c, t * P:(t + 1) * P], wq_hi[:, c, :], wq_lo[:, c, :], c == 0, c == DC - 1)
            last.then_inc(*A["q_done"].up())

        def pe_A_turn(pe, n):
            pe.wait_ge(*A["qk_ready"].at(n, 2))
            for k in range(2):
                for c in range(DC):
                    for t in range(TILES):
                        last = nc.tensor.transpose(ps[:, 4 + k, c * TG + t * P:c * TG + (t + 1) * P],
                                                   qk4[:, t, k, c * P:(c + 1) * P], ident)
                last.then_inc(*A["qT_done"].up())

        def act_A_ctx(act, n):
            for i, (lo, hi) in enumerate(PARTS):
                nc.scalar.copy(ctxm[2 * i][:, :, lo:hi], ctx_rows(n, lo, hi)).then_inc(*A["ctx_hi"].up())

        def act_A_square(act, n):
            act.wait_ge(*A["centred"].at(n, 1))
            nc.scalar.activation(sq, qk, ACT.Square).then_inc(*A["squared"].up())

        def act_A_guess(act, n):
            act.wait_ge(*A["grp_var"].at(n, 1))
            nc.scalar.activation(gln, gvar, ACT.Ln).then_inc(*A["act"].up())
            act.wait_ge(*A["act"].at(n, 1))
            nc.scalar.activation(guess, gln, ACT.Exp, scale=-0.5).then_inc(*A["grp_guess"].up())

        def act_A_qk(act, n):
            act.wait_ge(*A["qT_done"].at(n, 1))
            for h in range(2):
                nc.scalar.activation(qx[:, :, h, :], ps[:, 4, :].rearrange("p (k n) -> p k n", n=S), ACT.Identity,
                                     scale=parity[:, h:h + 1]).then_inc(*A["qx_ready"].up())
            act.wait_ge(*A["qT_done"].at(n, 2))
            for p in range(PAIRS0):
                r = slice(32 * p, 32 * p + 32)
                nc.scalar.copy(kx[r, :, p, :], ps[r, 5, :].rearrange("p (k n) -> p k n", n=S)
                               ).then_inc(*A["kT_ready"].up())

        def dve_A_ctx(dve, n):
            for i, (lo, hi) in enumerate(PARTS):
                dve.wait_ge(*A["ctx_hi"].at(n, i + 1))
                nc.vector.tensor_tensor(ctxm[2 * i + 1][:, :, lo:hi], ctx_rows(n, lo, hi),
                                        ctxm[2 * i][:, :, lo:hi].bitcast(F32), ALU.subtract
                                        ).then_inc(*A["ctx_lo"].up())

        def dve_A_kv(dve, n):
            for t in range(TILES):
                dve.wait_ge(*A["kv_done"].at(n, t + 1))
                nc.vector.tensor_tensor(qk4[:, t, 1, :], ps[:, 4 + t, 0:D], bkv[:, 0:D],
                                        ALU.add).then_inc(*A["kv_ready"].up())
                nc.vector.tensor_tensor(vnext[:, t, :], ps[:, 4 + t, D:2 * D], bkv[:, D:2 * D],
                                        ALU.add).then_inc(*A["kv_ready"].up())

        def dve_A_q(dve, n):
            dve.wait_ge(*A["q_done"].at(n, 1))
            nc.vector.tensor_tensor(qk4[:, :, 0, :], ps[:, 4, :].rearrange("p (t n) -> p t n", t=TILES),
                                    bc_mid(bq, TILES), ALU.add).then_inc(*A["q_ready"].up())

        def dve_A_mean(dve, n):
            dve.wait_ge(*A["kv_ready"].at(n, 4))
            dve.wait_ge(*A["q_ready"].at(n, 1))
            nc.vector.tensor_reduce(gsum, heads, AX, ALU.add).then_inc(*A["dve"].up())
            dve.wait_ge(*A["dve"].at(n, 1))
            nc.vector.tensor_scalar(gmean, gsum, 1.0 / HD0, None, ALU.mult).then_inc(*A["dve"].up())
            dve.wait_ge(*A["dve"].at(n, 2))
            nc.vector.tensor_tensor(heads, heads, bc_last(gmean, HD0), ALU.subtract).then_inc(*A["centred"].up())

        def dve_A_var(dve, n):
            dve.wait_ge(*A["squared"].at(n, 1))
            nc.vector.tensor_reduce(gssq, sq.rearrange("p (h n) -> p h n", n=HD0), AX, ALU.add
                                    ).then_inc(*A["dve"].up())
            dve.wait_ge(*A["dve"].at(n, 3))
            nc.vector.tensor_scalar(gvar, gssq, 1.0 / HD0, 1e-6, ALU.mult, ALU.add).then_inc(*A["grp_var"].up())

        def dve_A_scale(dve, n):
            dve.wait_ge(*A["grp_guess"].at(n, 1))
            nc.vector.tensor_tensor(gsq, guess, guess, ALU.mult).then_inc(*A["dve"].up())
            dve.wait_ge(*A["dve"].at(n, 4))
            nc.vector.scalar_tensor_tensor(out=gfix, in0=gsq, scalar=-0.5, in1=gvar, op0=ALU.mult,
                                           op1=ALU.mult).then_inc(*A["dve"].up())
            dve.wait_ge(*A["dve"].at(n, 5))
            nc.vector.scalar_tensor_tensor(out=grs, in0=gfix, scalar=1.5, in1=guess, op0=ALU.add,
                                           op1=ALU.mult).then_inc(*A["dve"].up())
            dve.wait_ge(*A["dve"].at(n, 6))
            nc.vector.tensor_tensor(heads, heads, bc_last(grs, HD0), ALU.mult).then_inc(*A["scaled"].up())

        def dve_A_values(dve, n):
            dve.wait_ge(*A["kv_ready"].at(n, 4))
            for b in range(2):
                r = slice(S * b, S * b + S)
                nc.vector.tensor_copy(vz[r, :, :, b, :], vnext[r].rearrange("p t (k n) -> p t k n", n=32)
                                      ).then_inc(*A["kv_ready"].up())

        def pool_A_affine(pool, n):
            pool.wait_ge(*A["scaled"].at(n, 1))
            for i, ws in enumerate(((qn_w, kn_w), (qn_b, kn_b))):
                for k, w in enumerate(ws):
                    v = qk4[:, :, k, :].rearrange("p t (h n) -> p t h n", n=HD0)
                    wb = w.unsqueeze(1).unsqueeze(1).broadcast_to([P, TILES, H0, HD0])
                    if i == 0:
                        nc.gpsimd.tensor_tensor(v, v, wb, ALU.mult).then_inc(*A["pool"].up())
                    else:
                        pool.wait_ge(*A["pool"].at(n, k + 1))
                        nc.gpsimd.tensor_tensor(v, v, wb, ALU.add).then_inc(*A["qk_ready"].up())

        def pe_A_scores(pe, g):
            pe.wait_ge(*A["kT_ready"].at(g, PAIRS0))
            pe.wait_ge(*A["qx_ready"].at(g, 2))
            for t in range(TILES):
                for c in range(DC):
                    o = ps[:, 2 * t + c, :].rearrange("p (a b n) -> p a b n", a=PAIRS0, b=2)
                    for b in range(2):
                        k = c * BG + 2 * t + b
                        last = nc.tensor.matmul(o[:, :, b, :], qx[:, k].rearrange("p h n -> p (h n)"),
                                                kx[:, k], start=True, stop=True)
                last.then_inc(*A["scores_done"].up())

        def pe_A_probs(pe, g, t):
            pe.wait_ge(*A["probs_ready"].at(g, 2 * t + 2))
            for k in range(8):
                last = nc.tensor.transpose(ps[:, 2 * t + k // 4, k % 4 * P:(k % 4 + 1) * P],
                                           probs[:, t, 2 * k:2 * k + 2, :].rearrange("p a b -> p (a b)"), ident)
            last.then_inc(*A["pT_done"].up())

        def pe_A_values(pe, g, t):
            pe.wait_ge(*A["pT_ready"].at(g, t + 1))
            if t == 0:
                pe.wait_ge(*A["kv_ready"].at(g, 6))
            for k in range(8):
                last = nc.tensor.matmul(ps[:, 6 + t, k * 64:(k + 1) * 64], pT[:, t, k, :],
                                        vz[:, t, k].rearrange("p b n -> p (b n)"), start=True, stop=True)
            if t == TILES - 1:
                last.then_inc(*A["pv_done"].up())

        def pe_A_turn_out(pe, g):
            pe.wait_ge(*A["an_ready"].at(g, 4))
            turn(an, 0).then_inc(*A["anT_done"].up())

        def pe_A_out(pe, g):
            pe.wait_ge(*A["an_hi"].at(g, 1))
            pe.wait_ge(*A["an_lo"].at(g, 1))
            for t in range(TILES):
                for c in range(DC):
                    last = mm3(ps[:, 1, t * D:(t + 1) * D], aT_hi[:, c, t * P:(t + 1) * P],
                               aT_lo[:, c, t * P:(t + 1) * P], wo_hi[:, c, :], wo_lo[:, c, :], c == 0, c == DC - 1)
            last.then_inc(*A["o_done"].up())

        def act_A_exp(act, g, t):
            act.wait_ge(*A["shifted"].at(g, 2 * t + 2))
            v = split_tokens(probs[:, t])
            nc.scalar.activation(v, v, ACT.Exp, scale=HD0 ** -0.5).then_inc(*A["exp_ready"].up())

        def act_A_probs(act, g, t):
            act.wait_ge(*A["pT_done"].at(g, t + 1))
            nc.scalar.copy(split_tokens(pT[:, t]), split_tokens(ps[:, 2 * t:2 * t + 2, :])
                           ).then_inc(*A["pT_ready"].up())

        def act_A_an(act, g):
            act.wait_ge(*A["pv_done"].at(g, 1))
            for b in range(2):
                for h in range(2):
                    src = ps[S * h:S * h + S, 6:8, :].rearrange("p t (k b h n) -> p (t k) b h n", b=2, h=2, n=HD0)
                    dst = an[S * b:S * b + S].rearrange("p t (k h n) -> p (t k) h n", k=8, h=2)
                    nc.scalar.copy(dst[:, :, h, :], src[:, :, b, h, :]).then_inc(*A["an_ready"].up())

        def act_A_upper(act, g):
            act.wait_ge(*A["anT_done"].at(g, 1))
            nc.scalar.copy(split_tokens(aT_hi), ps[:, 0, :]).then_inc(*A["an_hi"].up())

        def act_A_prep(act, g):
            act.wait_ge(A_prep_in, g * 16 + 16)
            nc.scalar.copy(wB_hi[:, bass.ds(g * GB, GB)], stage[:, 0:GB]).then_inc(*A["prep_hi"].up())

        def dve_A_shift(dve, g, t):
            dve.wait_ge(*A["scores_done"].at(g, t + 1))
            s = split_tokens(ps[:, 2 * t:2 * t + 2, :]).rearrange("p (k n) -> p k n", n=S)
            for i, (lo, hi) in enumerate(PARTS):
                nc.vector.tensor_reduce(mxA[:, t, 16 * i:16 * i + 16], s[:, :, lo:hi], AX,
                                        ALU.max).then_inc(*A["maxed"].up())
            for i, (lo, hi) in enumerate(PARTS):
                dve.wait_ge(*A["maxed"].at(g, 2 * t + i + 1))
                nc.vector.tensor_tensor(probs[:, t, :, lo:hi], s[:, :, lo:hi],
                                        bc_last(mxA[:, t, 16 * i:16 * i + 16], hi - lo),
                                        ALU.subtract).then_inc(*A["shifted"].up())

        def dve_A_sum(dve, g, t):
            dve.wait_ge(*A["exp_ready"].at(g, t + 1))
            for i, (lo, hi) in enumerate(PARTS):
                nc.vector.tensor_reduce(smA[:, t, 16 * i:16 * i + 16], probs[:, t, :, lo:hi], AX,
                                        ALU.add).then_inc(*A["summed"].up())
            dve.wait_ge(*A["summed"].at(g, 2 * t + 2))
            nc.vector.reciprocal(rcA[:, t, :], smA[:, t, :]).then_inc(*A["recip_ready"].up())

        def dve_A_lower(dve, g):
            dve.wait_ge(*A["an_hi"].at(g, 1))
            nc.vector.tensor_tensor(split_tokens(aT_lo), ps[:, 0, :], split_tokens(aT_hi).bitcast(F32),
                                    ALU.subtract).then_inc(*A["an_lo"].up())

        def dve_A_add(dve, g):
            dve.wait_ge(*A["o_done"].at(g, 1))
            nc.vector.tensor_tensor(an, ps[:, 1, :].rearrange("p (t n) -> p t n", t=TILES), bc_mid(bo, TILES),
                                    ALU.add).then_inc(*A["o_biased"].up())
            dve.wait_ge(*A["o_biased"].at(g, 1))
            xg = x[:, bass.ds(g * TILES, TILES), :] if not isinstance(g, int) else x[:, g * TILES:(g + 1) * TILES, :]
            nc.vector.scalar_tensor_tensor(out=xg, in0=an, scalar=tg[:, 0:1], in1=xg, op0=ALU.mult,
                                           op1=ALU.add).then_inc(*A["x_done"].up())

        def pool_A_scale(pool, g, t):
            pool.wait_ge(*A["recip_ready"].at(g, t + 1))
            for i, (lo, hi) in enumerate(PARTS):
                v = probs[:, t, :, lo:hi]
                nc.gpsimd.tensor_tensor(v, v, bc_last(rcA[:, t, 16 * i:16 * i + 16], hi - lo),
                                        ALU.mult).then_inc(*A["probs_ready"].up())

        def pool_A_prep(pool, g):
            pool.wait_ge(*A["prep_hi"].at(g, 1))
            nc.gpsimd.tensor_tensor(wB_lo[:, bass.ds(g * GB, GB)], stage[:, 0:GB],
                                    wB_hi[:, bass.ds(g * GB, GB)].bitcast(F32), ALU.subtract
                                    ).then_inc(*A["prep_lo"].up())

        def pe_A_start(pe):
            front_pe(pe, 0, 6)
            pe_A_kv(pe, 0)
            pe_A_q(pe, 0)
            pe_A_turn(pe, 0)

        def pe_A(pe, g, more):
            n = g + 1
            pe_A_scores(pe, g)
            if more:
                front_pe(pe, n, 6)
                pe_A_kv(pe, n)
                pe_A_q(pe, n)
            pe_A_probs(pe, g, 0)
            if more:
                pe.wait_ge(*front["lo_ready"].at(n, 1))
            pe_A_values(pe, g, 0)
            pe_A_probs(pe, g, 1)
            pe_A_values(pe, g, 1)
            pe_A_turn_out(pe, g)
            if more:
                pe.wait_ge(*A["q_ready"].at(n, 1))
                pe_A_turn(pe, n)
            pe_A_out(pe, g)
            if not more:
                front_pe(pe, n, 7)
            pe.wait_ge(*A["x_done"].at(g, 1))

        def act_A_start(act):
            act_A_ctx(act, 0)
            front_upper(act, 0, 6)
            act_A_square(act, 0)
            act_A_guess(act, 0)
            act_A_qk(act, 0)

        def act_A(act, g, more):
            n = g + 1
            if more:
                act_A_ctx(act, n)
            act_A_prep(act, g)
            if more:
                front_upper(act, n, 6)
            act_A_exp(act, g, 0)
            act_A_exp(act, g, 1)
            act_A_probs(act, g, 0)
            if more:
                act_A_square(act, n)
                act_A_guess(act, n)
            act_A_probs(act, g, 1)
            act_A_an(act, g)
            act_A_upper(act, g)
            if more:
                act_A_qk(act, n)
            else:
                front_upper(act, n, 7)
            act.wait_ge(*A["x_done"].at(g, 1))

        def dve_A_start(dve):
            front_dve(dve, 0, 0)
            dve_A_ctx(dve, 0)
            front_lower(dve, 0, 6)
            dve_A_kv(dve, 0)
            dve_A_values(dve, 0)
            dve_A_q(dve, 0)
            dve_A_mean(dve, 0)
            dve_A_var(dve, 0)
            dve_A_scale(dve, 0)

        def dve_A(dve, g, more):
            n = g + 1
            if more:
                front_dve(dve, n, n)
                dve_A_ctx(dve, n)
            dve_A_shift(dve, g, 0)
            if more:
                front_lower(dve, n, 6)
            dve_A_sum(dve, g, 0)
            dve_A_shift(dve, g, 1)
            if more:
                dve_A_kv(dve, n)
            dve_A_sum(dve, g, 1)
            if more:
                dve_A_q(dve, n)
                dve_A_mean(dve, n)
                dve_A_var(dve, n)
                dve_A_scale(dve, n)
            dve_A_lower(dve, g)
            dve_A_add(dve, g)
            if more:
                dve_A_values(dve, n)
            else:
                dve.wait_ge(*A["x_done"].at(g, 1))
                front_dve(dve, n, 0)
                front_lower(dve, n, 7)
            dve.wait_ge(*A["x_done"].at(g, 1))

        def pool_A_start(pool):
            front_pool(pool, 0)
            pool_A_affine(pool, 0)

        def pool_A(pool, g, more):
            n = g + 1
            if more:
                front_pool(pool, n)
            pool_A_prep(pool, g)
            pool_A_scale(pool, g, 0)
            pool_A_scale(pool, g, 1)
            if more:
                pool_A_affine(pool, n)
            else:
                front_pool(pool, n)
            pool.wait_ge(*A["x_done"].at(g, 1))

        def sp_A(sp, g):
            sp.dma_start(stage[:, 0:GB], a["wB"][bass.ds(g, 1)].rearrange("o p n -> p (o n)")).then_inc(A_prep_in, 16)
            sp.wait_ge(A_prep_in, g * 16 + 16)
            sp.sem_inc(waited, 1)
            sp.wait_ge(*A["prep_lo"].at(g, 1))
            sp.sem_inc(waited, 1)

        take = carver(work)
        lgs = take(TILES * NL).rearrange("p (t n) -> p t n", t=TILES)
        m8, ixf = (take(TILES * 8).rearrange("p (t n) -> p t n", t=TILES) for _ in range(2))
        ix = take(TILES * 8).bitcast(U32).rearrange("p (t n) -> p t n", t=TILES)
        ex, chosen, wsel = (take(TILES * E).rearrange("p (t n) -> p t n", t=TILES) for _ in range(3))
        comb = take(TILES * (E + 1)).rearrange("p (t n) -> p t n", t=TILES)
        eq = take(TILES * E * TOPK).rearrange("p (t n k) -> p t n k", t=TILES, k=TOPK)
        wsum, wrec, whalf, sgate = (take(TILES) for _ in range(4))
        th, h1, h2, h3 = ([take(TG) for _ in range(3)] for _ in range(4))
        take_r = carver(workr)
        h_hi, h_lo = ([take_r(TG) for _ in range(3)] for _ in range(2))
        combT_hi, combT_lo = (take_r(TG)[0:E + 1] for _ in range(2))
        sel = take_r((EC + 1) * P)[0:E + 1].rearrange("p (k n) -> p k n", k=EC + 1)
        logits = ps[:, 7, TG:TG + TILES * NL]
        combT = ps[0:E + 1, 6, TG:2 * TG]
        wqT, wkT = stage[:, 0:HG * D].rearrange("p (h n) -> p h n", h=HG), \
            stage[:, HG * D:HG * D + HG // 2 * DV].rearrange("p (h n) -> p h n", h=HG // 2)
        wvT = stage[:, HG * D + HG // 2 * DV:HG * D + HG * DV].rearrange("p (h n) -> p h n", h=HG // 2)
        wo1 = stage[:, HG * D + HG * DV:GCW].rearrange("p (h n) -> p h n", h=HG)
        JOIN = ((wM_hi, wM_lo), (wM_hi, wM_lo), (wN_hi, wN_lo), (wN_hi, wN_lo))

        def rows_B(k):
            return P if k < EC else F

        def gate_of(k):
            return ps[:, (3, 4, 1)[k % 3], 0:TG]

        def up_of(k):
            return ps[:, (3, 4, 1)[k % 3], TG:2 * TG]

        def up_B(k):
            return up_of(k) if k < EC else gate_of(k)[F:2 * F]

        def spread_of(k):
            return ps[:, (5, 2)[k % 2], 0:TG]

        def pe_B(pe, g):
            x_split(pe, 4 + g)
            for t in range(TILES):
                for c in range(DC):
                    last = mm3(logits[:, t * NL:(t + 1) * NL], xT_hi[:, c, t * P:(t + 1) * P],
                               xT_lo[:, c, t * P:(t + 1) * P], wr_hi[:, c, :], wr_lo[:, c, :], c == 0, c == DC - 1)
            last.then_inc(*Bp["logits_done"].up())

            def gate_up(k):
                if k >= 3:
                    pe.wait_ge(*Bp["h2"].at(g, k - 2))
                if k < EC:
                    col = slice(k % 2 * P, k % 2 * P + P)
                    for o, w_hi, w_lo in ((gate_of(k), eg_hi, eg_lo), (up_of(k), eu_hi, eu_lo)):
                        for c in range(DC):
                            last = mm3(o, w_hi[:, k // 2, c, col],
                                       w_lo[:, k // 2, c, col], xT_hi[:, c, :], xT_lo[:, c, :], c == 0, c == DC - 1)
                else:
                    for c in range(DC):
                        last = mm3(gate_of(k), sgu_hi[:, c, :], sgu_lo[:, c, :], xT_hi[:, c, :],
                                   xT_lo[:, c, :], c == 0, c == DC - 1)
                last.then_inc(*Bp["gu_done"].up())

            def spread(k):
                if k >= 2:
                    pe.wait_ge(*Bp["h3"].at(g, k - 1))
                o = spread_of(k)
                nc.tensor.matmul(o, sel[:, k, :], combT_hi, start=True, stop=False)
                nc.tensor.matmul(o, sel[:, k, :], combT_lo, start=False, stop=True).then_inc(*Bp["bc_done"].up())

            def down(k):
                pe.wait_ge(*Bp["h_hi"].at(g, k + 1))
                pe.wait_ge(*Bp["h_lo"].at(g, k + 1))
                n = rows_B(k)
                d_hi, d_lo = (ed_hi[:, k // 2, k % 2, :], ed_lo[:, k // 2, k % 2, :]) if k < EC else (sd_hi, sd_lo)
                for t in range(TILES):
                    last = mm3(ps[:, 6 + t, 0:D], h_hi[k % 3][0:n, t * P:(t + 1) * P],
                               h_lo[k % 3][0:n, t * P:(t + 1) * P], d_hi, d_lo, k == 0, k == EC)
                return last

            def join(r):
                if r == 0:
                    pe.wait_ge(B_prep_in, g * 16 + 16)
                if r:
                    pe.wait_ge(*Bp["join_lo"].at(g, r))
                for i in range(2):
                    h = 2 * (r % 2) + i
                    for c in range(DC) if r < 2 else ():
                        last = nc.tensor.matmul(ps[:, 0, i * D + c * DV:i * D + (c + 1) * DV],
                                                wqT[:, h, c * P:(c + 1) * P], wkT[:, h // 2, :], start=True, stop=True)
                    if r >= 2:
                        last = nc.tensor.matmul(ps[:, 0, i * D:(i + 1) * D], wvT[:, h // 2, :],
                                                wo1[:, h, :], start=True, stop=True)
                last.then_inc(*Bp["join_done"].up())

            gate_up(0)
            gate_up(1)
            join(0)
            gate_up(2)
            pe.wait_ge(*Bp["comb_ready"].at(g, 2))
            for t in range(TILES):
                last = nc.tensor.transpose(combT[:, t * P:(t + 1) * P], comb[:, t, :], ident)
            last.then_inc(*Bp["combT_done"].up())
            pe.wait_ge(*Bp["combT_hi"].at(g, 1))
            pe.wait_ge(*Bp["combT_lo"].at(g, 1))
            spread(0)
            spread(1)
            for k in range(3, EC + 1):
                gate_up(k)
                down(k - 3)
                spread(k - 1)
                if k in (3, 5, 7):
                    join(k // 2)
            down(EC - 2)
            spread(EC)
            pe.wait_ge(*Bp["join_lo"].at(g, 4))
            front_pe(pe, 5 + g, 0)
            down(EC - 1)
            down(EC).then_inc(*Bp["out_done"].up())
            pe.wait_ge(*Bp["x_done"].at(g, TILES))

        def act_B(act, g):

            def tanh(k):
                act.wait_ge(*Bp["gu_done"].at(g, k + 1))
                n = rows_B(k)
                nc.scalar.activation(th[k % 3][0:n], gate_of(k)[0:n], ACT.Tanh,
                                     scale=0.5).then_inc(*Bp["tanh_ready"].up())

            def upper(k):
                act.wait_ge(*Bp["h3"].at(g, k + 1))
                n = rows_B(k)
                nc.scalar.copy(h_hi[k % 3][0:n], h3[k % 3][0:n]).then_inc(*Bp["h_hi"].up())

            def join(r):
                act.wait_ge(*Bp["join_done"].at(g, r + 1))
                w = JOIN[r][0][:, bass.ds(g * HG + 2 * (r % 2), 2), :]
                nc.scalar.copy(w, ps[:, 0, :].rearrange("p (h n) -> p h n", h=2)).then_inc(*Bp["join_hi"].up())

            tanh(0)
            act.wait_ge(*Bp["shifted"].at(g, 1))
            nc.scalar.activation(ex, ex, ACT.Exp).then_inc(*Bp["exp_ready"].up())
            nc.scalar.activation(sgate, lgs[:, :, E], ACT.Tanh, scale=0.5).then_inc(*Bp["gate_ready"].up())
            tanh(1)
            join(0)
            tanh(2)
            act.wait_ge(*Bp["combT_done"].at(g, 1))
            nc.scalar.copy(combT_hi, combT).then_inc(*Bp["combT_hi"].up())
            upper(0)
            for k in range(3, EC + 1):
                tanh(k)
                upper(k - 2)
                if k in (3, 5, 7):
                    join(k // 2)
            upper(EC - 1)
            front_upper(act, 5 + g, 0)
            upper(EC)
            act.wait_ge(*Bp["x_done"].at(g, TILES))

        def dve_B(dve, g):
            front_stats(dve, 5 + g, after(g))

            def gated(k):
                n = rows_B(k)
                dve.wait_ge(*Bp["tanh_ready"].at(g, k + 1))
                nc.vector.scalar_tensor_tensor(out=h1[k % 3][0:n], in0=th[k % 3][0:n], scalar=1.0,
                                               in1=gate_of(k)[0:n], op0=ALU.add,
                                               op1=ALU.mult).then_inc(*Bp["h1"].up())
                dve.wait_ge(*Bp["h1"].at(g, k + 1))
                nc.vector.tensor_tensor(h2[k % 3][0:n], h1[k % 3][0:n], up_B(k), ALU.mult).then_inc(*Bp["h2"].up())

            def weighted(k):
                n = rows_B(k)
                dve.wait_ge(*Bp["h2"].at(g, k + 1))
                dve.wait_ge(*Bp["bc_done"].at(g, k + 1))
                nc.vector.tensor_tensor(h3[k % 3][0:n], h2[k % 3][0:n], spread_of(k)[0:n],
                                        ALU.mult).then_inc(*Bp["h3"].up())

            def join(r):
                dve.wait_ge(*Bp["join_hi"].at(g, r + 1))
                hi, lo = (w[:, bass.ds(g * HG + 2 * (r % 2), 2), :] for w in JOIN[r])
                nc.vector.tensor_tensor(lo, ps[:, 0, :].rearrange("p (h n) -> p h n", h=2),
                                        hi.bitcast(F32), ALU.subtract).then_inc(*Bp["join_lo"].up())

            dve.wait_ge(*Bp["logits_done"].at(g, 1))
            nc.vector.tensor_copy(lgs, logits.rearrange("p (t n) -> p t n", t=TILES)
                                  ).then_inc(*Bp["dve"].up())
            dve.wait_ge(*Bp["dve"].last(g))
            dve.sem_inc(waited, 1)
            for t in range(TILES):
                nc.vector.max(m8[:, t, :], lgs[:, t, 0:E]).then_inc(*Bp["dve"].up())
            dve.wait_ge(*Bp["dve"].last(g))
            nc.vector.tensor_tensor(ex, lgs[:, :, 0:E], m8[:, :, 0:1].broadcast_to([P, TILES, E]),
                                    ALU.subtract).then_inc(*Bp["shifted"].up())
            for t in range(TILES):
                nc.vector.max_index(ix[:, t, :], m8[:, t, :], lgs[:, t, 0:E]).then_inc(*Bp["dve"].up())
            dve.wait_ge(*Bp["dve"].last(g))
            nc.vector.tensor_copy(ixf, ix).then_inc(*Bp["dve"].up())
            dve.wait_ge(*Bp["dve"].last(g))
            nc.vector.tensor_tensor(eq, iota.unsqueeze(1).unsqueeze(3).broadcast_to([P, TILES, E, TOPK]),
                                    ixf[:, :, 0:TOPK].unsqueeze(2).broadcast_to([P, TILES, E, TOPK]),
                                    ALU.is_equal).then_inc(*Bp["dve"].up())
            dve.wait_ge(*Bp["dve"].last(g))
            nc.vector.tensor_reduce(chosen, eq, AX, ALU.add).then_inc(*Bp["dve"].up())
            dve.wait_ge(*Bp["dve"].last(g))
            dve.wait_ge(*Bp["exp_ready"].at(g, 1))
            nc.vector.tensor_tensor(wsel, ex, chosen, ALU.mult).then_inc(*Bp["dve"].up())
            dve.wait_ge(*Bp["dve"].last(g))
            nc.vector.tensor_reduce(wsum, wsel, AX, ALU.add).then_inc(*Bp["dve"].up())
            dve.wait_ge(*Bp["dve"].last(g))
            nc.vector.reciprocal(wrec, wsum).then_inc(*Bp["dve"].up())
            dve.wait_ge(*Bp["dve"].last(g))
            nc.vector.tensor_scalar(whalf, wrec, 0.5, None, ALU.mult).then_inc(*Bp["dve"].up())
            dve.wait_ge(*Bp["dve"].last(g))
            nc.vector.tensor_tensor(comb[:, :, 0:E], wsel, bc_last(whalf, E), ALU.mult).then_inc(*Bp["comb_ready"].up())
            dve.wait_ge(*Bp["gate_ready"].at(g, 1))
            nc.vector.tensor_scalar(comb[:, :, E], sgate, 0.25, 0.25, ALU.mult, ALU.add).then_inc(*Bp["comb_ready"].up())
            gated(0)
            gated(1)
            join(0)
            dve.wait_ge(*Bp["combT_hi"].at(g, 1))
            nc.vector.tensor_tensor(combT_lo, combT, combT_hi.bitcast(F32),
                                    ALU.subtract).then_inc(*Bp["combT_lo"].up())
            gated(2)
            weighted(0)
            front_norm(dve, 5 + g, after(g))
            for k in range(3, EC + 1):
                weighted(k - 2)
                gated(k)
                if k in (3, 5, 7):
                    join(k // 2)
            weighted(EC - 1)
            weighted(EC)
            front_lower(dve, 5 + g, 0)
            dve.wait_ge(*Bp["out_done"].at(g, 1))
            for t in range(TILES):
                xt = x[:, g * TILES + t, :]
                nc.vector.scalar_tensor_tensor(out=xt, in0=ps[:, 6 + t, 0:D], scalar=tg[:, 1:2], in1=xt,
                                               op0=ALU.mult, op1=ALU.add).then_inc(*Bp["x_done"].up())
            dve.wait_ge(*Bp["x_done"].at(g, TILES))

        def pool_B(pool, g):
            front_pool(pool, 5 + g)
            for k in range(EC + 1):
                n = rows_B(k)
                pool.wait_ge(*Bp["h_hi"].at(g, k + 1))
                nc.gpsimd.tensor_tensor(h_lo[k % 3][0:n], h3[k % 3][0:n], h_hi[k % 3][0:n].bitcast(F32),
                                        ALU.subtract).then_inc(*Bp["h_lo"].up())
            pool.wait_ge(*Bp["x_done"].at(g, TILES))

        def sp_B(sp, g):
            sp.dma_start(stage, a["wC"][bass.ds(g, 1)].rearrange("o p n -> p (o n)")).then_inc(B_prep_in, 16)
            sp.wait_ge(B_prep_in, g * 16 + 16)
            sp.sem_inc(waited, 1)
            sp.wait_ge(*Bp["join_done"].at(g, 4))
            sp.sem_inc(waited, 1)

        take = carver(work)
        qt = take(PAIRS1 * 2 * TG).rearrange("p (j b h n) -> p j b h n", j=PAIRS1, b=BG, h=2)
        pC = take(2 * 512).rearrange("p (s k n) -> p s k n", s=2, k=8)
        mxC, smC, rcC = (take(4 * 8).rearrange("p (s n) -> p s n", s=4) for _ in range(3))
        bits = take(4 * RMAX).bitcast(I32).rearrange("p (b n) -> p b n", b=4)
        lev = take(8 * RMAX).rearrange("p (j n) -> p j n", j=8)
        take_r = carver(workr)
        pT_hi, pT_lo = (take_r(TILES * 512).rearrange("p (t n) -> p t n", t=TILES) for _ in range(2))
        cx_hi, cx_lo = (take_r(TILES * DV).rearrange("p (t n) -> p t n", t=TILES) for _ in range(2))
        z_hi, z_lo = (shared_r[:, i * HALF * TG:(i + 1) * HALF * TG].rearrange("p (h n) -> p h n", h=HALF)
                      for i in range(2))
        idx = stage[:, 0:sum(ROUNDS)].bitcast(I32)
        TURNED = (5, 0)

        POOL_LEVEL1 = 5

        def z_of(n):
            return ps[:, (6, 7, 1)[n % 3], :]

        ctx_g = stage[:, sum(ROUNDS):sum(ROUNDS) + TG]

        def decoded(w, g, r):
            if r < 2:
                return w[r][:, :, bass.ds(g * IG, IG)]
            return w[2][:, :, bass.ds(g * DG, DG)]

        def shape_r(v, r):
            return v.rearrange("p (c n) -> p c n", c=DC if r < 2 else FC)

        def pe_C(pe, g):
            x_split(pe, 8 + g)

            def queries(u):
                for j in range(PAIRS1):
                    n = u * PAIRS1 + j
                    if n >= 2:
                        pe.wait_ge(*C["q_ready"].at(g, n - 1))
                    for h in range(2):
                        hh = 2 * n + h
                        for c in range(DC):
                            last = mm3(ps[:, 1 + n % 2, h * TG:(h + 1) * TG], wM_hi[:, hh, c * DV:(c + 1) * DV],
                                       wM_lo[:, hh, c * DV:(c + 1) * DV], xT_hi[:, c, :], xT_lo[:, c, :],
                                       c == 0, c == DC - 1)
                    last.then_inc(*C["q_done"].up())

            def scores(u):
                if u == 0:
                    pe.wait_ge(*C["mask_ready"].at(g, 2))
                for s in range(2):
                    if u:
                        pe.wait_ge(*C["shifted"].at(g, s + 1))
                    nc.tensor.matmul(ps[:, 3 + s, :], ones_row, mask_rows.rearrange("p a n -> p (a n)"),
                                     start=True, stop=False)
                    pe.wait_ge(*C["q_ready"].at(g, u * PAIRS1 + 2 * s + 2))
                    for jj in range(2):
                        for b in range(BG):
                            k = jj * BG + b
                            last = nc.tensor.matmul(ps[:, 3 + s, k * S:(k + 1) * S],
                                                    qt[:, 2 * s + jj, b].rearrange("p h n -> p (h n)"),
                                                    ctx_g[:, b * S:(b + 1) * S], start=False, stop=k == 7)
                    last.then_inc(*C["scores_done"].up())

            def turn_probs(u, s):
                n = 2 * u + s
                pe.wait_ge(*C["probs_ready"].at(g, n + 1))
                if n >= 2:
                    pe.wait_ge(*C["pT_lo"].at(g, n - 1))
                for k in range(4):
                    last = nc.tensor.transpose(ps[:, TURNED[s], k * P:(k + 1) * P],
                                               pC[:, s, 2 * k:2 * k + 2, :].rearrange("p a b -> p (a b)"), ident)
                last.then_inc(*C["pT_done"].up())

            def mix(u):
                if u == 0:
                    pe.wait_ge(*C["cx_lo"].at(g, 1))
                    pe.wait_ge(*C["q_ready"].last(g))
                pe.wait_ge(*C["pT_lo"].at(g, 2 * u + 2))
                for t in range(TILES):
                    for b in range(2):
                        n = u * BG + 2 * t + b
                        if n >= 3:
                            pe.wait_ge(*C["z_lo"].at(g, n - 2))
                        r = slice(S * b, S * b + S)
                        mm3(z_of(n), cx_hi[r, t, :], cx_lo[r, t, :], pT_hi[r, t, :], pT_lo[r, t, :],
                            True, True).then_inc(*C["z_done"].up())

            def output(u, t):
                pe.wait_ge(*C["z_lo"].at(g, u * BG + 2 * t + 2))
                if u and t == 0:
                    pe.wait_ge(*C["x_done"].at(g, 1))
                for h in range(HALF):
                    hh = u * HALF + h
                    last = mm3(ps[:, 2, t * D:(t + 1) * D], z_hi[:, h, t * P:(t + 1) * P],
                               z_lo[:, h, t * P:(t + 1) * P], wN_hi[:, hh, :], wN_lo[:, hh, :],
                               h == 0, h == HALF - 1)
                if t == TILES - 1:
                    last.then_inc(*C["out_done"].up())

            queries(0)
            scores(0)
            queries(1)
            turn_probs(0, 0)
            turn_probs(0, 1)
            scores(1)
            mix(0)
            output(0, 0)
            turn_probs(1, 0)
            turn_probs(1, 1)
            output(0, 1)
            front_pe(pe, 9 + g, 3)
            mix(1)
            output(1, 0)
            output(1, 1)
            pe.wait_ge(*C["x_done"].at(g, 2))

        def act_C(act, g):

            def queries(u):
                for j in range(PAIRS1):
                    n = u * PAIRS1 + j
                    act.wait_ge(*C["q_done"].at(g, n + 1))
                    if u:
                        act.wait_ge(*C["scores_done"].at(g, j // 2 + 1))
                    nc.scalar.copy(qt[:, j].rearrange("p b h n -> p h b n"),
                                   ps[:, 1 + n % 2, :].rearrange("p (h b n) -> p h b n", h=2, b=BG)
                                   ).then_inc(*C["q_ready"].up())

            def exps(u):
                for s in range(2):
                    act.wait_ge(*C["shifted"].at(g, 2 * u + s + 1))
                    v = split_tokens(pC[:, s])
                    nc.scalar.activation(v, v, ACT.Exp, scale=HD1 ** -0.5).then_inc(*C["exp_ready"].up())

            def upper_probs(u):
                for s in range(2):
                    act.wait_ge(*C["pT_done"].at(g, 2 * u + s + 1))
                    dst = pT_hi.rearrange("p t (j n) -> p t j n", j=PAIRS1)[:, :, 2 * s:2 * s + 2, :]
                    nc.scalar.copy(dst.rearrange("p t j n -> p j t n"),
                                   ps[:, TURNED[s], :].rearrange("p (j t n) -> p j t n", j=2, t=2)
                                   ).then_inc(*C["pT_hi"].up())

            def upper_z(u):
                for k in range(BG):
                    act.wait_ge(*C["z_done"].at(g, u * BG + k + 1))
                    if u and k == 0:
                        act.wait_ge(*C["out_done"].at(g, 1))
                    nc.scalar.copy(z_hi[:, :, k * S:(k + 1) * S],
                                   z_of(u * BG + k).rearrange("p (h n) -> p h n", h=HALF)).then_inc(*C["z_hi"].up())

            def level1(r):
                n = ROUNDS[r]
                act.wait_ge(*C["bits"].at(g, 4 * r + 1))
                for j in range(POOL_LEVEL1, 8):
                    nc.scalar.activation(lev[:, j, 0:n], bits[:, 0, 0:n], ACT.Identity, scale=lut_step[:, j:j + 1],
                                         bias=lut[:, 2 * j:2 * j + 1]).then_inc(*C["level1"].up())

            def upper_decoded(r):
                act.wait_ge(*C["chosen"].at(g, 3 * r + 3))
                nc.scalar.copy(decoded((fg_hi, fu_hi, fd_hi), g, r), shape_r(lev[:, 0, 0:ROUNDS[r]], r)
                               ).then_inc(*C["dec_hi"].up())

            act.wait_ge(*C["ctx_masked"].at(g, TILES))
            nc.scalar.copy(split_tokens(cx_hi), split_tokens(ctx_n)).then_inc(*C["cx_hi"].up())
            queries(0)
            level1(0)
            exps(0)
            queries(1)
            upper_decoded(0)
            level1(1)
            upper_probs(0)
            exps(1)
            upper_z(0)
            upper_decoded(1)
            level1(2)
            upper_probs(1)
            front_upper(act, 9 + g, 3)
            upper_z(1)
            upper_decoded(2)
            act.wait_ge(*C["x_done"].at(g, 2))

        def dve_C(dve, g):
            front_stats(dve, 9 + g, after(g))
            nc.vector.tensor_scalar(mask_rows, mask_row8[:, bass.ds(g * TG, TG)].unsqueeze(1)
                                    .broadcast_to([1, 2, TG]), -1.0, MASKED, ALU.add, ALU.mult
                                    ).then_inc(*C["mask_ready"].up())
            nc.vector.tensor_copy(ctx_g, ctx_T[:, bass.ds(g * TG, TG)]).then_inc(*C["mask_ready"].up())
            dve.wait_ge(C_nat_in, g * 16 + 16)
            for t in range(TILES):
                nc.vector.tensor_scalar(ctx_n[:, t, :], ctx_n[:, t, :], mask_n[:, bass.ds(g * TILES + t, 1)], None,
                                        ALU.mult).then_inc(*C["ctx_masked"].up())

            def shift(u):
                for s in range(2):
                    n = 2 * u + s
                    dve.wait_ge(*C["scores_done"].at(g, n + 1))
                    sc = ps[:, 3 + s, :].rearrange("p (k n) -> p k n", k=8)
                    nc.vector.tensor_reduce(mxC[:, n, :], sc, AX, ALU.max).then_inc(*C["maxed"].up())
                    dve.wait_ge(*C["maxed"].at(g, n + 1))
                    if u:
                        dve.wait_ge(*C["pT_done"].at(g, s + 1))
                    nc.vector.tensor_tensor(pC[:, s], sc, bc_last(mxC[:, n, :], S),
                                            ALU.subtract).then_inc(*C["shifted"].up())

            def sums(u):
                for s in range(2):
                    n = 2 * u + s
                    dve.wait_ge(*C["exp_ready"].at(g, n + 1))
                    nc.vector.tensor_reduce(smC[:, n, :], pC[:, s], AX, ALU.add).then_inc(*C["summed"].up())
                    dve.wait_ge(*C["summed"].at(g, n + 1))
                    nc.vector.reciprocal(rcC[:, n, :], smC[:, n, :]).then_inc(*C["recip_ready"].up())

            def lower_probs(u):
                for s in range(2):
                    dve.wait_ge(*C["pT_hi"].at(g, 2 * u + s + 1))
                    lo, hi = (v.rearrange("p t (j n) -> p t j n", j=PAIRS1)[:, :, 2 * s:2 * s + 2, :]
                              .rearrange("p t j n -> p j t n") for v in (pT_lo, pT_hi))
                    nc.vector.tensor_tensor(lo, ps[:, TURNED[s], :].rearrange("p (j t n) -> p j t n", j=2, t=2),
                                            hi.bitcast(F32), ALU.subtract).then_inc(*C["pT_lo"].up())

            def lower_z(u):
                for k in range(BG):
                    dve.wait_ge(*C["z_hi"].at(g, u * BG + k + 1))
                    nc.vector.tensor_tensor(z_lo[:, :, k * S:(k + 1) * S],
                                            z_of(u * BG + k).rearrange("p (h n) -> p h n", h=HALF),
                                            z_hi[:, :, k * S:(k + 1) * S].bitcast(F32),
                                            ALU.subtract).then_inc(*C["z_lo"].up())

            def add(u):
                dve.wait_ge(*C["out_done"].at(g, u + 1))
                if u:
                    dve.wait_ge(*C["x_done"].at(g, 1))
                xg = x[:, bass.ds(g * TILES, TILES), :]
                nc.vector.scalar_tensor_tensor(out=xg, in0=ps[:, 2, :].rearrange("p (t n) -> p t n", t=TILES),
                                               scalar=tg[:, 2:3], in1=xg, op0=ALU.mult,
                                               op1=ALU.add).then_inc(*C["x_done"].up())

            def take_bits(r):
                n, o = ROUNDS[r], sum(ROUNDS[:r])
                if r == 0:
                    dve.wait_ge(C_idx_in, g * 16 + 16)
                else:
                    dve.wait_ge(*C["level1"].at(g, 8 * r))
                    dve.wait_ge(*C["chosen"].last(g))
                for bit in range(4):
                    nc.vector.tensor_scalar(bits[:, bit, 0:n], idx[:, o:o + n], 1 << bit, None,
                                            ALU.bitwise_and).then_inc(*C["bits"].up())

            def choose(r):
                n = ROUNDS[r]
                dve.wait_ge(*C["level1"].at(g, 8 * r + 8))
                for i, step in enumerate((1, 2, 4)):
                    left, right = (lev[:, k::2 * step, 0:n] for k in (0, step))
                    m = bits[:, i + 1:i + 2, 0:n].broadcast_to([P, 4 // step, n])
                    if i:
                        dve.wait_ge(*C["chosen"].last(g))
                    else:
                        dve.wait_ge(*C["bits"].at(g, 4 * r + 4))
                    dve.sem_inc(waited, 1)
                    nc.vector.copy_predicated(left, m, right).then_inc(*C["chosen"].up())

            take_bits(0)
            front_norm(dve, 9 + g, after(g))
            dve.wait_ge(*C["cx_hi"].at(g, 1))
            nc.vector.tensor_tensor(split_tokens(cx_lo), split_tokens(ctx_n), split_tokens(cx_hi).bitcast(F32),
                                    ALU.subtract).then_inc(*C["cx_lo"].up())
            shift(0)
            sums(0)
            choose(0)
            take_bits(1)
            lower_probs(0)
            shift(1)
            sums(1)
            lower_z(0)
            choose(1)
            take_bits(2)
            lower_probs(1)
            add(0)
            front_lower(dve, 9 + g, 3)
            lower_z(1)
            choose(2)
            add(1)
            dve.wait_ge(*C["x_done"].at(g, 2))

        def pool_C(pool, g):
            front_pool(pool, 9 + g)

            def scale(u):
                for s in range(2):
                    n = 2 * u + s
                    pool.wait_ge(*C["recip_ready"].at(g, n + 1))
                    nc.gpsimd.tensor_tensor(pC[:, s], pC[:, s], bc_last(rcC[:, n, :], S),
                                            ALU.mult).then_inc(*C["probs_ready"].up())

            def level1(r):
                n = ROUNDS[r]
                pool.wait_ge(*C["bits"].at(g, 4 * r + 1))
                if r:
                    pool.wait_ge(*C["dec_lo"].at(g, r))
                pool.sem_inc(waited, 1)
                for j in range(POOL_LEVEL1):
                    nc.gpsimd.tensor_scalar(lev[:, j, 0:n], bits[:, 0, 0:n], lut_step[:, j:j + 1],
                                            lut[:, 2 * j:2 * j + 1], ALU.mult, ALU.add).then_inc(*C["level1"].up())

            def lower(r):
                pool.wait_ge(*C["dec_hi"].at(g, r + 1))
                nc.gpsimd.tensor_tensor(decoded((fg_lo, fu_lo, fd_lo), g, r), shape_r(lev[:, 0, 0:ROUNDS[r]], r),
                                        decoded((fg_hi, fu_hi, fd_hi), g, r).bitcast(F32),
                                        ALU.subtract).then_inc(*C["dec_lo"].up())

            level1(0)
            scale(0)
            lower(0)
            level1(1)
            scale(1)
            lower(1)
            level1(2)
            lower(2)
            pool.wait_ge(*C["dec_lo"].at(g, 3))
            pool.wait_ge(*C["x_done"].at(g, 2))

        def sp_C(sp, g):
            sp.dma_start(ctx_n, a["ctx_n"][bass.ds(g * TILES, TILES)].rearrange("t p n -> p t n")).then_inc(C_nat_in, 16)
            sp.dma_start(idx, a["idx"][bass.ds(g, 1)].rearrange("o p n -> p (o n)")).then_inc(C_idx_in, 16)
            sp.wait_ge(C_nat_in, g * 16 + 16)
            sp.sem_inc(waited, 1)
            sp.wait_ge(C_idx_in, g * 16 + 16)
            sp.sem_inc(waited, 1)
            sp.wait_ge(*C["cx_lo"].at(g, 1))
            sp.sem_inc(waited, 1)
            sp.wait_ge(*C["bits"].at(g, 4 * 3))
            sp.sem_inc(waited, 1)

        take = carver(work)
        fth, fh1, fh3 = ([take(TG) for _ in range(3)] for _ in range(3))
        take_r = carver(workr)
        fh_hi, fh_lo = ([take_r(TG) for _ in range(3)] for _ in range(2))

        def rows_D(k):
            return P if k < FC - 1 else FLAST

        def pe_D(pe, g, more):
            x_split(pe, 12 + g)

            def gate_up(k):
                if k >= 3:
                    pe.wait_ge(*Dp["h3"].at(g, k - 2))
                for o, w_hi, w_lo in ((gate_of(k), fg_hi, fg_lo), (up_of(k), fu_hi, fu_lo)):
                    for c in range(DC):
                        last = mm3(o, w_hi[:, c, k * P:(k + 1) * P],
                                   w_lo[:, c, k * P:(k + 1) * P], xT_hi[:, c, :], xT_lo[:, c, :], c == 0, c == DC - 1)
                last.then_inc(*Dp["gu_done"].up())

            def down(k):
                n = rows_D(k)
                pe.wait_ge(*Dp["h_hi"].at(g, k + 1))
                pe.wait_ge(*Dp["h_lo"].at(g, k + 1))
                for t in range(TILES):
                    last = mm3(ps[:, 6 + t, 0:D], fh_hi[k % 3][0:n, t * P:(t + 1) * P],
                               fh_lo[k % 3][0:n, t * P:(t + 1) * P], fd_hi[0:n, k, :], fd_lo[0:n, k, :],
                               k == 0, k == FC - 1)
                return last

            gate_up(0)
            gate_up(1)
            for k in range(2, FC):
                gate_up(k)
                down(k - 2)
            if more:
                front_pe(pe, 13 + g, 0)
            down(FC - 2)
            down(FC - 1).then_inc(*Dp["out_done"].up())
            pe.wait_ge(*Dp["x_done"].at(g, TILES))

        def act_D(act, g, more):

            def tanh(k):
                n = rows_D(k)
                act.wait_ge(*Dp["gu_done"].at(g, k + 1))
                nc.scalar.activation(fth[k % 3][0:n], gate_of(k)[0:n], ACT.Tanh,
                                     scale=0.5).then_inc(*Dp["tanh_ready"].up())

            def upper(k):
                n = rows_D(k)
                act.wait_ge(*Dp["h3"].at(g, k + 1))
                nc.scalar.copy(fh_hi[k % 3][0:n], fh3[k % 3][0:n]).then_inc(*Dp["h_hi"].up())

            tanh(0)
            for k in range(1, FC):
                tanh(k)
                upper(k - 1)
            upper(FC - 1)
            if more:
                front_upper(act, 13 + g, 0)
            act.wait_ge(*Dp["x_done"].at(g, TILES))

        def dve_D(dve, g, more):
            if more:
                front_dve(dve, 13 + g, g + 1)
            for k in range(FC):
                n = rows_D(k)
                dve.wait_ge(*Dp["tanh_ready"].at(g, k + 1))
                nc.vector.scalar_tensor_tensor(out=fh1[k % 3][0:n], in0=fth[k % 3][0:n], scalar=1.0,
                                               in1=gate_of(k)[0:n], op0=ALU.add,
                                               op1=ALU.mult).then_inc(*Dp["h1"].up())
                dve.wait_ge(*Dp["h1"].at(g, k + 1))
                nc.vector.scalar_tensor_tensor(out=fh3[k % 3][0:n], in0=fh1[k % 3][0:n], scalar=0.5,
                                               in1=up_of(k)[0:n], op0=ALU.mult,
                                               op1=ALU.mult).then_inc(*Dp["h3"].up())
            if more:
                front_lower(dve, 13 + g, 0)
            dve.wait_ge(*Dp["out_done"].at(g, 1))
            for t in range(TILES):
                xt = x[:, g * TILES + t, :]
                nc.vector.scalar_tensor_tensor(out=xt, in0=ps[:, 6 + t, 0:D], scalar=tg[:, 3:4], in1=xt,
                                               op0=ALU.mult, op1=ALU.add).then_inc(*Dp["x_done"].up())
            dve.wait_ge(*Dp["x_done"].at(g, TILES))

        def pool_D(pool, g, more):
            if more:
                front_pool(pool, 13 + g)
            for k in range(FC):
                n = rows_D(k)
                pool.wait_ge(*Dp["h_hi"].at(g, k + 1))
                nc.gpsimd.tensor_tensor(fh_lo[k % 3][0:n], fh3[k % 3][0:n], fh_hi[k % 3][0:n].bitcast(F32),
                                        ALU.subtract).then_inc(*Dp["h_lo"].up())
            pool.wait_ge(*Dp["x_done"].at(g, TILES))

        def sp_D(sp, g):
            sp.wait_ge(*Dp["x_done"].at(g, TILES))
            sp.dma_start(a["out"][bass.ds(g * TILES, TILES)].rearrange("t p n -> p t n"),
                         x[:, bass.ds(g * TILES, TILES), :]).then_inc(out_done, 16)

        block = ctx.enter_context(nc.Block())

        @block.sync
        def _(sp):
            sp.dma_start(x, a["x"].rearrange("t p n -> p t n")).then_inc(x_in, 16)
            sp.dma_start(stage[:, 0:NWA], a["wA"]).then_inc(wA_in, 16)
            sp.dma_start(ctx_T, a["ctx_T"]).then_inc(ctxT_in, 16)
            sp.dma_start(const, a["const"]).then_inc(const_in, 16)
            sp.dma_start(vec, a["vec"].partition_broadcast(P)).then_inc(vec_in, 16)
            for b in range(2):
                for (lo, hi), v in zip(PARTS, (a["vec_main"], a["vec_last"])):
                    sp.dma_start(veck[b * S + lo:b * S + hi, :], v.partition_broadcast(hi - lo)).then_inc(vec_in, 16)
            sp.dma_start(gates, a["gates"].partition_broadcast(P)).then_inc(gates_in, 16)
            sp.dma_start(lut, a["lut"].partition_broadcast(P)).then_inc(lut_in, 16)
            sp.dma_start(mask_row8, a["mask_row"]).then_inc(mask_in, 16)
            sp.dma_start(mask_n8, a["mask_n"]).then_inc(mask_in, 16)
            sp.wait_ge(setup_dve, 2)
            sp.dma_start(stage[:, GB:GB + NWS], a["wS"]).then_inc(wS_in, 16)
            sp.dma_start(stage[0:E + 1, 0:NSEL], a["sel"]).then_inc(sel_in, 16)
            sp.wait_ge(setup_act, 4)
            with sp.Fori(0, GROUPS) as g:
                sp_A(sp, g)
            sp.wait_ge(setup_dve, 5)
            with sp.Fori(0, GROUPS) as g:
                sp_B(sp, g)
            with sp.Fori(0, GROUPS) as g:
                sp_C(sp, g)
            with sp.Fori(0, GROUPS) as g:
                sp_D(sp, g)
            sp.wait_ge(out_done, 16 * GROUPS)

        @block.tensor
        def _(pe):
            pe.wait_ge(const_in, 16)
            pe.wait_ge(setup_dve, 2)
            pe_A_start(pe)
            with pe.Fori(0, GROUPS - 1) as g:
                pe_A(pe, g, True)
            pe_A(pe, GROUPS - 1, False)
            pe.wait_ge(setup_dve, 5)
            pe.wait_ge(setup_act, 4)
            with pe.Fori(0, GROUPS) as g:
                pe_B(pe, g)
            with pe.Fori(0, GROUPS) as g:
                pe_C(pe, g)
            pe.wait_ge(*C["dec_lo"].last(GROUPS - 1))
            with pe.Fori(0, GROUPS - 1) as g:
                pe_D(pe, g, True)
            pe_D(pe, GROUPS - 1, False)

        @block.scalar
        def _(act):
            act.wait_ge(wA_in, 16)
            nc.scalar.copy(wA_hi, stage[:, 0:NWA]).then_inc(setup_act, 1)
            act.wait_ge(gates_in, 16)
            nc.scalar.activation(tg, gates, ACT.Tanh).then_inc(setup_act, 1)
            act.wait_ge(wS_in, 16)
            nc.scalar.copy(wS_hi, stage[:, GB:GB + NWS]).then_inc(setup_act, 1)
            act.wait_ge(sel_in, 16)
            nc.scalar.copy(sel.rearrange("p k n -> p (k n)"), stage[0:E + 1, 0:NSEL]).then_inc(setup_act, 1)
            act.wait_ge(ctxT_in, 16)
            act.wait_ge(const_in, 16)
            act.wait_ge(setup_pool, 4)
            act_A_start(act)
            with act.Fori(0, GROUPS - 1) as g:
                act_A(act, g, True)
            act_A(act, GROUPS - 1, False)
            with act.Fori(0, GROUPS) as g:
                act_B(act, g)
            act.wait_ge(setup_dve, 2)
            with act.Fori(0, GROUPS) as g:
                act_C(act, g)
            with act.Fori(0, GROUPS - 1) as g:
                act_D(act, g, True)
            act_D(act, GROUPS - 1, False)

        @block.vector
        def _(dve):
            dve.wait_ge(setup_act, 1)
            nc.vector.tensor_tensor(wA_lo, stage[:, 0:NWA], wA_hi.bitcast(F32), ALU.subtract).then_inc(setup_dve, 1)
            dve.wait_ge(lut_in, 16)
            lp = lut.rearrange("p (j b) -> p j b", b=2)
            nc.vector.tensor_tensor(lut_step, lp[:, :, 1], lp[:, :, 0], ALU.subtract).then_inc(setup_dve, 1)
            dve.wait_ge(mask_in, 32)
            nc.vector.tensor_copy(mask_n, mask_n8).then_inc(setup_dve, 1)
            nc.vector.memset(ones_row, 1.0).then_inc(setup_dve, 1)
            dve.wait_ge(setup_act, 3)
            nc.vector.tensor_tensor(wS_lo, stage[:, GB:GB + NWS], wS_hi.bitcast(F32),
                                    ALU.subtract).then_inc(setup_dve, 1)
            dve.wait_ge(x_in, 16)
            dve.wait_ge(ctxT_in, 16)
            dve.wait_ge(vec_in, 16 * 5)
            dve.wait_ge(setup_pool, 4)
            dve_A_start(dve)
            with dve.Fori(0, GROUPS - 1) as g:
                dve_A(dve, g, True)
            dve_A(dve, GROUPS - 1, False)
            dve.wait_ge(const_in, 16)
            with dve.Fori(0, GROUPS) as g:
                dve_B(dve, g)
            pad = [w[:, :, INTER:FC * P].bitcast(F32) for w in (fg_hi, fg_lo, fu_hi, fu_lo)]
            for w in pad:
                nc.vector.memset(w, 0.0).then_inc(setup_dve, 1)
            with dve.Fori(0, GROUPS) as g:
                dve_C(dve, g)
            with dve.Fori(0, GROUPS - 1) as g:
                dve_D(dve, g, True)
            dve_D(dve, GROUPS - 1, False)

        @block.gpsimd
        def _(pool):
            nc.gpsimd.memset(expo, -0.5).then_inc(setup_pool, 1)
            nc.gpsimd.memset(workAr[:, 0:4 * TG].bitcast(F32), 0.0).then_inc(setup_pool, 1)
            nc.gpsimd.memset(kx.rearrange("p k a n -> p (k a n)"), 0.0).then_inc(setup_pool, 1)
            nc.gpsimd.memset(vz.rearrange("p t k b n -> p (t k b n)"), 0.0).then_inc(setup_pool, 1)
            pool.wait_ge(vec_in, 16 * 5)
            pool_A_start(pool)
            with pool.Fori(0, GROUPS - 1) as g:
                pool_A(pool, g, True)
            pool_A(pool, GROUPS - 1, False)
            with pool.Fori(0, GROUPS) as g:
                pool_B(pool, g)
            pool.wait_ge(setup_dve, 2)
            with pool.Fori(0, GROUPS) as g:
                pool_C(pool, g)
            with pool.Fori(0, GROUPS - 1) as g:
                pool_D(pool, g, True)
            pool_D(pool, GROUPS - 1, False)

        for name, phase, times in (("A", A, 2), ("B", Bp, 1), ("C", C, 1), ("D", Dp, 2)):
            for key, s in phase.items():
                assert s.n == times * s.per_group, (name, key, s.n, s.per_group)


def laid_out(i):
    f = {}
    f["x"] = i["x"].reshape(GROUPS * TILES, P, D)
    c = i["ctx_1024"].reshape(B * S, DV)
    f["ctx_T"] = c.T
    f["ctx_n"] = c.reshape(GROUPS * TILES, P, DV)

    def chunks(w):
        return w.reshape(-1, P, w.shape[1]).transpose(1, 0, 2).reshape(P, -1)

    def by_head(w):
        return w.reshape(w.shape[:-1] + (H0, 2, HD0)).swapaxes(-3, -2).reshape(w.shape)

    wkv = by_head(np.concatenate([i["L0_xattn_Wk"], i["L0_xattn_Wv"]], axis=1))
    f["wA"] = np.concatenate([chunks(i["L0_xattn_Wq"]), wkv, i["L0_xattn_Wkv_dca"], chunks(i["L0_xattn_Wo"])], axis=1)
    f["vec"] = np.concatenate([i["L0_xattn_bq"], i["L0_xattn_bo"], i["L0_xattn_qn_w"], i["L0_xattn_qn_b"]])
    bkv = by_head(np.concatenate([i["L0_xattn_bk"], i["L0_xattn_bv"]]))
    f["vec_main"] = np.concatenate([bkv, i["L0_xattn_kn_w"], i["L0_xattn_kn_b"]])
    f["vec_last"] = np.concatenate([i["L0_xattn_bkv_dca"], i["L0_xattn_kn_dca_w"], i["L0_xattn_kn_dca_b"]])
    f["gates"] = np.stack([i["g_xattn"], i["g_ffn"]], axis=1).reshape(-1)
    parts = []
    for w in (i["L0_ffn_Wg"], i["L0_ffn_Wu"]):
        parts.append(w.reshape(GROUPS, 4, DC, P, F).transpose(0, 3, 2, 1, 4).reshape(GROUPS, P, -1))
    parts.append(i["L0_ffn_Wd"].reshape(GROUPS, 2, P, D).transpose(0, 2, 1, 3).reshape(GROUPS, P, -1))
    f["wB"] = np.concatenate(parts, axis=2)
    sgu = chunks(np.concatenate([i["L0_ffn_sWg"], i["L0_ffn_sWu"]], axis=1))
    sd = np.concatenate([i["L0_ffn_sWd"], np.zeros_like(i["L0_ffn_sWd"])])
    router = np.concatenate([i["L0_ffn_gate_w"].T, i["L0_ffn_shared_gate_w"],
                             np.zeros_like(i["L0_ffn_shared_gate_w"])], axis=1)
    f["wS"] = np.concatenate([sgu, sd, chunks(router)], axis=1)
    q = i["L1_xattn_Wq"].reshape(D, GROUPS, HG, HD1).transpose(1, 3, 2, 0).reshape(GROUPS, P, -1)
    k, v = (i[n].reshape(DV, GROUPS, HG // 2, HD1).transpose(1, 3, 2, 0).reshape(GROUPS, P, -1)
            for n in ("L1_xattn_Wk", "L1_xattn_Wv"))
    o = i["L1_xattn_Wo"].reshape(GROUPS, HG, HD1, D).transpose(0, 2, 1, 3).reshape(GROUPS, P, -1)
    f["wC"] = np.concatenate([q, k, v, o], axis=2)
    up = [i[n].T.reshape(DC, P, GROUPS, IG).transpose(2, 1, 0, 3).reshape(GROUPS, P, -1)
          for n in ("L1_ffn_gate_idx", "L1_ffn_up_idx")]
    d = i["L1_ffn_down_idx"].T
    d = np.concatenate([d, np.zeros((FC * P - INTER, D), d.dtype)]).reshape(FC, P, GROUPS, DG)
    f["idx"] = np.concatenate(up + [d.transpose(2, 1, 0, 3).reshape(GROUPS, P, -1)], axis=2)
    f["lut"] = i["L1_ffn_lut"]
    m = i["mask_BxS2_bf1"].view(np.uint8)
    f["mask_row"] = m.reshape(1, B * S)
    f["mask_n"] = m.reshape(GROUPS * TILES, P).T
    const = np.zeros((P, NCONST), np.float32)
    const[:, 0:P] = np.eye(P)
    const[:, P] = np.arange(P) // HD0 % 2 == 0
    const[:, P + 1] = np.arange(P) // HD0 % 2 == 1
    const[:, P + 2:P + 2 + E] = np.arange(E)
    f["const"] = const
    sel = np.zeros((E + 1, EC + 1, P), np.float32)
    for k_ in range(EC):
        for e in range(2):
            sel[2 * k_ + e, k_, e * F:(e + 1) * F] = 1
    sel[E, EC, :] = 1
    f["sel"] = sel.reshape(E + 1, NSEL)
    return {k_: np.ascontiguousarray(v_) for k_, v_ in f.items()}


def kernel(**inputs):
    import concourse.bacc as bacc
    from concourse.bass_utils import run_bass_kernel_spmd

    arrays = laid_out({k: np.asarray(v) for k, v in inputs.items()})
    nc = bacc.Bacc("TRN2", target_bir_lowering=False, num_devices=1)
    a = {k: nc.dram_tensor(f"in_{k}", v.shape, mybir.dt.from_np(v.dtype), kind="ExternalInput").ap()
         for k, v in arrays.items()}
    a["out"] = nc.dram_tensor("out", (GROUPS * TILES, P, D), F32, kind="ExternalOutput").ap()
    build(nc, a)
    r = run_bass_kernel_spmd(nc, [{f"in_{k}": v for k, v in arrays.items()}], core_ids=[0])
    return r.results[0]["out"].reshape(B, S, D)
```

```python
from contextlib import ExitStack

import numpy as np

import concourse.bass as bass
from concourse import mybir

ALU = mybir.AluOpType
ACT = mybir.ActivationFunctionType
F32 = mybir.dt.float32
F32R = mybir.dt.float32r
BF16 = mybir.dt.bfloat16
I32 = mybir.dt.int32
U32 = mybir.dt.uint32
U8 = mybir.dt.uint8
AX = mybir.AxisListType.X

P = 128
B, S, D = 16, 64, 256
DV = 128
GROUPS = 4
TG = B * S // GROUPS
BG = TG // S
TILES = TG // P
DC = D // P
H0, HD0 = 16, 16
DCA = 16
MAIN = S - DCA
PARTS = ((0, MAIN), (MAIN, S))
PAIRS0 = 4
E, F, TOPK = 16, 64, 4
EC = E * F // P
NL = E + 2
H1, HD1, KV1 = 16, 128, 8
HALF = H1 // 2
PAIRS1 = HALF // 2
HG = H1 // GROUPS
INTER, LUT = 688, 16
FC = -(-INTER // P)
FLAST = INTER - (FC - 1) * P
IG = INTER // GROUPS
DG = D // GROUPS
ROUNDS = (DC * IG, DC * IG, FC * DG)
RMAX = max(ROUNDS)
MASKED = 1e30

NVEC = D + D
NVK = 2 * D
NCOL = 6
NWA = 2 * DC * D + 4 * D
NWC = DC * D + 2 * D
GB = 2 * DC * 4 * F + 2 * D
NWS = DC * 2 * F + D + DC * NL
GCW = HG * D + HG // 2 * 2 * DV + HG * D
NCONST = P + 2 + E
NSEL = (EC + 1) * P


class Signal:

    def __init__(self, sem, per_group):
        self.sem, self.per_group, self.n, self.base = sem, per_group, 0, 0

    def start_at(self, base):
        self.base = base
        return self.sem, base

    def up(self):
        self.n += 1
        return self.sem, 1

    def at(self, g, n):
        return self.sem, g * self.per_group + (n + self.base)

    def last(self, g):
        return self.at(g, self.n)


def build(nc, a):
    ctx = ExitStack()
    with ctx:
        def sb(name, shape, dt=F32):
            return ctx.enter_context(nc.sbuf_tensor(name, shape, dt))[:]

        def sem(name):
            return ctx.enter_context(nc.semaphore(name))

        def signals(phase, **per_group):
            return {k: Signal(sem(f"{phase}_{k}"), n) for k, n in per_group.items()}

        ps = ctx.enter_context(nc.psum_tensor("ps", [P, 8, 512], F32))[:]

        x = sb("x", [P, GROUPS * TILES, D])
        ctx_T = sb("ctx_T", [P, B * S])
        ctx_n = sb("ctx_n", [P, TILES, DV])
        const = sb("const", [P, NCONST])
        ident, parity = const[:, 0:P], const[:, P:P + 2]
        iota = const[:, P + 2:P + 2 + E]
        gates = sb("gates", [P, 4])
        tg = sb("tg", [P, 4])
        expo = sb("expo", [P, TILES])
        lut = sb("lut", [P, LUT])
        lut_step = sb("lut_step", [P, LUT // 2])
        mask_row8 = sb("mask_row8", [1, B * S], U8)
        mask_rows = sb("mask_rows", [1, 2, TG], BF16)
        ones_row = sb("ones_row", [1, P], BF16)
        mask_n8 = sb("mask_n8", [P, GROUPS * TILES], U8)
        mask_n = sb("mask_n", [P, GROUPS * TILES])
        xn = sb("xn", [P, TILES, D])
        stats = sb("stats", [P, TILES, 6])
        mv = sb("mv", [P, TILES, 2])
        ve = sb("ve", [P, TILES])
        rstd = sb("rstd", [P, TILES])
        xT_hi = sb("xT_hi", [P, DC, TG], F32R)
        xT_lo = sb("xT_lo", [P, DC, TG], F32R)
        shared_r = sb("shared_r", [P, 2 * NWA], F32R)
        wB_hi = sb("wB_hi", [P, GROUPS * GB], F32R)
        wB_lo = sb("wB_lo", [P, GROUPS * GB], F32R)
        wS_hi = sb("wS_hi", [P, NWS], F32R)
        wS_lo = sb("wS_lo", [P, NWS], F32R)
        stage = sb("stage", [P, GCW])
        with nc.sbuf_tensor("workA", [P, 13248], F32) as early, \
                nc.sbuf_tensor("workAr", [P, 4 * TG + 2 * DC * TG], F32R) as early_r:
            workA, workAr = early[:], early_r[:]
        wM_hi = sb("wM_hi", [P, H1, D], F32R)
        wM_lo = sb("wM_lo", [P, H1, D], F32R)
        wN_hi = sb("wN_hi", [P, H1, D], F32R)
        wN_lo = sb("wN_lo", [P, H1, D], F32R)
        work = sb("work", [P, 7800])
        workr = sb("workr", [P, 8 * TG + NSEL], F32R)

        def carver(pool):
            at = [0]

            def carve(n):
                at[0] += n
                assert at[0] <= pool.shape[1], at
                return pool[:, at[0] - n:at[0]]
            return carve

        def split_tokens(v):
            return v.rearrange("p c n -> p (c n)")

        def bc_last(v, n):
            return v.unsqueeze(2).broadcast_to([v.shape[0], v.shape[1], n])

        def bc_mid(v, n):
            return v.unsqueeze(1).broadcast_to([v.shape[0], n, v.shape[1]])

        def wA(w):
            kv = w[:, DC * D:DC * D + 4 * D].rearrange("p (j i n) -> p i j n", i=2, j=2)
            return (w[:, 0:DC * D].rearrange("p (c n) -> p c n", c=DC), kv[:, 0], kv[:, 1],
                    w[:, DC * D + 4 * D:NWA].rearrange("p (c n) -> p c n", c=DC))

        wA_hi, wA_lo = shared_r[:, 0:NWA], shared_r[:, NWA:2 * NWA]
        wq_hi, wkv_hi, wkvd_hi, wo_hi = wA(wA_hi)
        wq_lo, wkv_lo, wkvd_lo, wo_lo = wA(wA_lo)

        def wB(w):
            v, n = w.rearrange("p (g n) -> p g n", g=GROUPS), DC * 4 * F
            return (v[:, :, 0:n].rearrange("p g (c n) -> p g c n", c=DC),
                    v[:, :, n:2 * n].rearrange("p g (c n) -> p g c n", c=DC),
                    v[:, :, 2 * n:].rearrange("p g (k n) -> p g k n", k=2))

        eg_hi, eu_hi, ed_hi = wB(wB_hi)
        eg_lo, eu_lo, ed_lo = wB(wB_lo)

        def wS(w):
            n = DC * 2 * F
            return (w[:, 0:n].rearrange("p (c n) -> p c n", c=DC), w[0:F, n:n + D],
                    w[:, n + D:].rearrange("p (c n) -> p c n", c=DC))

        sgu_hi, sd_hi, wr_hi = wS(wS_hi)
        sgu_lo, sd_lo, wr_lo = wS(wS_lo)

        def wF(w):
            n = DC * FC * P
            return (w[:, 0:n].rearrange("p (c n) -> p c n", c=DC), w[:, n:2 * n].rearrange("p (c n) -> p c n", c=DC),
                    w[:, 2 * n:2 * n + FC * D].rearrange("p (c n) -> p c n", c=FC))

        fg_hi, fu_hi, fd_hi = wF(wB_hi)
        fg_lo, fu_lo, fd_lo = wF(wB_lo)

        waited = sem("waited")
        const_in, gates_in, x0_in, x_in, ctxT_in, vec_in, lut_in, mask_in = (
            sem(n) for n in ("const_in", "gates_in", "x0_in", "x_in", "ctxT_in", "vec_in", "lut_in", "mask_in"))
        wA1_in, wA2_in, wS_in, sel_in, setup_pool, setup_act, setup_dve, out_done = (
            sem(n) for n in ("wA1_in", "wA2_in", "wS_in", "sel_in", "setup_pool", "setup_act", "setup_dve", "out_done"))

        front = signals("front", stat=4, var_ready=1, rstd_ready=1, xn_ready=2, xT_done=1, hi_ready=1, lo_ready=1)
        A = signals("A", dve=4, act=1, ctx_hi=2, ctx_lo=2, kv_done=2, q_done=1, kv_ready=6, q_ready=1,
                    squared=1, grp_var=1, grp_guess=1, scaled=1, qT_done=2, kT_ready=2 * PAIRS0,
                    qx_ready=2, scores_done=2, maxed=4, shifted=4, exp_ready=2, summed=4, recip_ready=2,
                    probs_ready=4, pT_done=2, pT_ready=2, pv_done=1, an_ready=4, anT_done=1, an_hi=1, an_lo=1,
                    o_done=1, o_biased=1, x_done=1, prep_hi=1, prep_lo=1)
        centred, wA_hi_ready, wA_lo_ready = sem("centred"), sem("wA_hi_ready"), sem("wA_lo_ready")
        A_prep_in = sem("A_prep_in")
        CH = EC + 1
        Bp = signals("B", dve=12, logits_done=1, shifted=1, exp_ready=1, gate_ready=1, comb_ready=2,
                     combT_done=1, combT_hi=1, combT_lo=1, gu_done=CH, tanh_ready=CH, h1=CH, h2=CH, bc_done=CH,
                     h3=CH, h_hi=CH, h_lo=CH, out_done=1, x_done=TILES, join_done=4, join_hi=4, join_lo=4)
        B_prep_in = sem("B_prep_in")
        C = signals("C", mask_ready=2, ctx_masked=TILES, cx_hi=1, cx_lo=1, q_done=2 * PAIRS1, q_ready=2 * PAIRS1,
                    scores_done=4, maxed=4, shifted=4, exp_ready=4, summed=4, recip_ready=4, probs_ready=4,
                    pT_done=4, pT_hi=4, pT_lo=4, z_done=2 * BG, z_hi=2 * BG, z_lo=2 * BG, out_done=2, x_done=2,
                    bits=4 * 3, level1=8 * 3, chosen=3 * 3, dec_hi=3, dec_lo=3)
        C_nat_in, C_idx_in = sem("C_nat_in"), sem("C_idx_in")
        Dp = signals("D", gu_done=FC, tanh_ready=FC, h1=FC, h3=FC, h_hi=FC, h_lo=FC, out_done=1,
                     x_done=TILES)

        free_at_start = [s.start_at(n) for s, n in ((A["x_done"], 1), (Bp["x_done"], 1), (C["x_done"], 1),
                                                    (Dp["x_done"], 1), (Bp["join_lo"], 1), (Bp["h2"], 3), (Dp["h3"], 3))]

        def front_stats(dve, f, g):
            for t in range(TILES):
                nc.vector.bn_stats(stats[:, t, :], x[:, g * TILES + t, :]).then_inc(*front["stat"].up())
            for t in range(TILES):
                dve.wait_ge(*front["stat"].at(f, t + 1))
                dve.sem_inc(waited, 1)
                nc.vector.bn_aggr(mv[:, t, :], stats[:, t, :]).then_inc(*front["stat"].up())
            dve.wait_ge(*front["stat"].at(f, 4))
            nc.vector.tensor_scalar(ve, mv[:, :, 1], 1e-5, None, ALU.add).then_inc(*front["var_ready"].up())

        def front_norm(dve, f, g):
            dve.wait_ge(*front["rstd_ready"].at(f, 1))
            for t in range(TILES):
                nc.vector.tensor_scalar(xn[:, t, :], x[:, g * TILES + t, :], mv[:, t, 0:1], rstd[:, t:t + 1],
                                        ALU.subtract, ALU.mult).then_inc(*front["xn_ready"].up())

        def front_dve(dve, f, g):
            front_stats(dve, f, g)
            front_norm(dve, f, g)

        def front_pool(pool, f):
            pool.wait_ge(*front["var_ready"].at(f, 1))
            nc.gpsimd.tensor_tensor(rstd, ve, expo, ALU.pow).then_inc(*front["rstd_ready"].up())

        def turn(src, to):
            for c in range(DC):
                for t in range(TILES):
                    last = nc.tensor.transpose(ps[:, to, c * TG + t * P:c * TG + (t + 1) * P],
                                               src[:, t, c * P:(c + 1) * P], ident)
            return last

        def front_pe(pe, f, to):
            pe.wait_ge(*front["xn_ready"].at(f, TILES))
            turn(xn, to).then_inc(*front["xT_done"].up())

        def front_upper(act, f, to):
            act.wait_ge(*front["xT_done"].at(f, 1))
            nc.scalar.copy(split_tokens(xT_hi), ps[:, to, :]).then_inc(*front["hi_ready"].up())

        def front_lower(dve, f, to):
            dve.wait_ge(*front["hi_ready"].at(f, 1))
            nc.vector.tensor_tensor(split_tokens(xT_lo), ps[:, to, :], split_tokens(xT_hi).bitcast(F32),
                                    ALU.subtract).then_inc(*front["lo_ready"].up())

        def x_split(pe, f):
            pe.wait_ge(*front["hi_ready"].at(f, 1))
            pe.wait_ge(*front["lo_ready"].at(f, 1))

        def after(g):
            return (g + 1) % GROUPS

        def mm3(out, l_hi, l_lo, r_hi, r_lo, start, stop, loose=False):
            for i, (l, r) in enumerate(((l_hi, r_hi), (l_hi, r_lo), (l_lo, r_hi))):
                last = nc.tensor.matmul(out, l, r, start=start and i == 0, stop=stop and i == 2)
            return last

        take = carver(workA)
        qk = take(TILES * 2 * D)
        qk4 = qk.rearrange("p (t k n) -> p t k n", t=TILES, k=2)
        heads = qk.rearrange("p (h n) -> p h n", n=HD0)
        sq = take(TILES * 2 * D)
        probs = take(TILES * 1024).rearrange("p (t k n) -> p t k n", t=TILES, n=S)
        pT = take(TILES * 1024).rearrange("p (t k n) -> p t k n", t=TILES, n=P)
        vz = take(TILES * 8 * 2 * 32).rearrange("p (t k b n) -> p t k b n", t=TILES, k=8, b=2)
        vec, veck = take(NVEC), take(NVK)
        bq, bo, bkv = vec[:, 0:D], vec[:, D:2 * D], veck
        cols = take(NCOL)
        q_scale, q_shift = take(2), take(2)
        vnext = take(TILES * D).rearrange("p (t n) -> p t n", t=TILES)
        kx = take(DC * BG * PAIRS0 * S).rearrange("p (k a n) -> p k a n", a=PAIRS0, n=S)
        qx = take(2 * DC * TG).rearrange("p (k h n) -> p k h n", h=2, n=S)
        an = take(TILES * D).rearrange("p (t n) -> p t n", t=TILES)
        gsum, gssq, gvar, gln, guess, gsq, gfix, grs = (take(64) for _ in range(8))
        mxA, smA, rcA = (take(64).rearrange("p (t n) -> p t n", t=TILES) for _ in range(3))
        take_r = carver(workAr)
        ctxm = [take_r(TG).rearrange("p (b n) -> p b n", b=BG) for _ in range(4)]
        aT_hi, aT_lo = (take_r(DC * TG).rearrange("p (c n) -> p c n", c=DC) for _ in range(2))

        def ctx_rows(g, lo, hi):
            return ctx_T[:, bass.ds(g * TG, TG)].rearrange("p (b n) -> p b n", b=BG)[:, :, lo:hi]

        def pe_A_kv(pe, n):
            pe.wait_ge(*A["ctx_hi"].at(n, 2))
            pe.wait_ge(*A["ctx_lo"].at(n, 2))
            for t in range(TILES):
                m = [c.rearrange("p b n -> p (b n)")[:, t * P:(t + 1) * P] for c in ctxm]
                mm3(ps[:, 4 + t, :], m[0], m[1], wkv_hi, wkv_lo, True, False)
                mm3(ps[:, 4 + t, :], m[2], m[3], wkvd_hi, wkvd_lo, False, True).then_inc(*A["kv_done"].up())

        def pe_A_q(pe, n):
            x_split(pe, n)
            for t in range(TILES):
                for c in range(DC):
                    last = mm3(ps[:, 6, t * D:(t + 1) * D], xT_hi[:, c, t * P:(t + 1) * P],
                               xT_lo[:, c, t * P:(t + 1) * P], wq_hi[:, c, :], wq_lo[:, c, :], c == 0, c == DC - 1)
            last.then_inc(*A["q_done"].up())

        def pe_A_turn(pe, n):
            pe.wait_ge(*A["scaled"].at(n, 1))
            for k in range(2):
                for c in range(DC):
                    for t in range(TILES):
                        last = nc.tensor.transpose(ps[:, 4 + k, c * TG + t * P:c * TG + (t + 1) * P],
                                                   qk4[:, t, k, c * P:(c + 1) * P], ident)
                last.then_inc(*A["qT_done"].up())

        def pe_A_scores(pe, n, t):
            pe.wait_ge(*A["kT_ready"].at(n, 2 * PAIRS0))
            pe.wait_ge(*A["qx_ready"].at(n, 2))
            for c in range(DC):
                o = ps[:, 2 * t + c, :].rearrange("p (a b n) -> p a b n", a=PAIRS0, b=2)
                for b in range(2):
                    k = c * BG + 2 * t + b
                    last = nc.tensor.matmul(o[:, :, b, :], qx[:, k].rearrange("p h n -> p (h n)"),
                                            kx[:, k], start=True, stop=True)
            last.then_inc(*A["scores_done"].up())

        def act_A_ctx(act, n):
            for i, (lo, hi) in enumerate(PARTS):
                nc.scalar.copy(ctxm[2 * i][:, :, lo:hi], ctx_rows(n, lo, hi)).then_inc(*A["ctx_hi"].up())

        def act_A_square(act, n):
            act.wait_ge(*A["kv_ready"].at(n, 4))
            act.wait_ge(*A["q_ready"].at(n, 1))
            nc.scalar.activation(sq, qk, ACT.Square).then_inc(*A["squared"].up())

        def act_A_guess(act, n):
            act.wait_ge(*A["grp_var"].at(n, 1))
            nc.scalar.activation(gln, gvar, ACT.Ln).then_inc(*A["act"].up())
            act.wait_ge(*A["act"].at(n, 1))
            nc.scalar.activation(guess, gln, ACT.Exp, scale=-0.5).then_inc(*A["grp_guess"].up())

        def act_A_qk(act, n):
            act.wait_ge(*A["qT_done"].at(n, 1))
            for h in range(2):
                nc.scalar.activation(qx[:, :, h, :], ps[:, 4, :].rearrange("p (k n) -> p k n", n=S), ACT.Identity,
                                     scale=q_scale[:, h:h + 1], bias=q_shift[:, h:h + 1]
                                     ).then_inc(*A["qx_ready"].up())

        def dve_A_ctx(dve, n):
            for i, (lo, hi) in enumerate(PARTS):
                dve.wait_ge(*A["ctx_hi"].at(n, i + 1))
                nc.vector.tensor_tensor(ctxm[2 * i + 1][:, :, lo:hi], ctx_rows(n, lo, hi),
                                        ctxm[2 * i][:, :, lo:hi].bitcast(F32), ALU.subtract
                                        ).then_inc(*A["ctx_lo"].up())

        def dve_A_kv(dve, n):
            for t in range(TILES):
                dve.wait_ge(*A["kv_done"].at(n, t + 1))
                nc.vector.tensor_tensor(qk4[:, t, 1, :], ps[:, 4 + t, 0:D], bkv[:, 0:D],
                                        ALU.add).then_inc(*A["kv_ready"].up())
                nc.vector.tensor_tensor(vnext[:, t, :], ps[:, 4 + t, D:2 * D], bkv[:, D:2 * D],
                                        ALU.add).then_inc(*A["kv_ready"].up())

        def dve_A_q(dve, n):
            dve.wait_ge(*A["q_done"].at(n, 1))
            nc.vector.tensor_tensor(qk4[:, :, 0, :], ps[:, 6, :].rearrange("p (t n) -> p t n", t=TILES),
                                    bc_mid(bq, TILES), ALU.add).then_inc(*A["q_ready"].up())

        def dve_A_var(dve, n):
            dve.wait_ge(*A["squared"].at(n, 1))
            nc.vector.tensor_reduce(gssq, sq.rearrange("p (h n) -> p h n", n=HD0), AX, ALU.add
                                    ).then_inc(*A["dve"].up())
            dve.wait_ge(*A["dve"].at(n, 1))
            nc.vector.tensor_scalar(gvar, gssq, 1.0 / HD0, 1e-6, ALU.mult, ALU.add).then_inc(*A["grp_var"].up())

        def dve_A_scale(dve, n):
            dve.wait_ge(*A["grp_guess"].at(n, 1))
            nc.vector.tensor_tensor(gsq, guess, guess, ALU.mult).then_inc(*A["dve"].up())
            dve.wait_ge(*A["dve"].at(n, 2))
            nc.vector.scalar_tensor_tensor(out=gfix, in0=gsq, scalar=-0.5, in1=gvar, op0=ALU.mult,
                                           op1=ALU.mult).then_inc(*A["dve"].up())
            dve.wait_ge(*A["dve"].at(n, 3))
            nc.vector.scalar_tensor_tensor(out=grs, in0=gfix, scalar=1.5, in1=guess, op0=ALU.add,
                                           op1=ALU.mult).then_inc(*A["dve"].up())
            dve.wait_ge(*A["dve"].at(n, 4))
            nc.vector.tensor_tensor(heads, heads, bc_last(grs, HD0), ALU.mult).then_inc(*A["scaled"].up())

        def dve_A_values(dve, n):
            dve.wait_ge(*A["kv_ready"].at(n, 4))
            for b in range(2):
                r = slice(S * b, S * b + S)
                nc.vector.tensor_copy(vz[r, :, :, b, :], vnext[r].rearrange("p t (k n) -> p t k n", n=32)
                                      ).then_inc(*A["kv_ready"].up())

        def act_A_k(act, n):
            act.wait_ge(*A["qT_done"].at(n, 2))
            p = PAIRS0 - 1
            for i, (lo, hi) in enumerate(PARTS):
                r = slice(32 * p, 32 * p + 32)
                nc.scalar.activation(kx[r, :, p, lo:hi],
                                     ps[r, 5, :].rearrange("p (k n) -> p k n", n=S)[:, :, lo:hi], ACT.Identity,
                                     scale=cols[r, 2 + 2 * i:3 + 2 * i], bias=cols[r, 3 + 2 * i:4 + 2 * i]
                                     ).then_inc(*A["kT_ready"].up())

        def dve_A_k(dve, n):
            dve.wait_ge(*A["qT_done"].at(n, 2))
            for p in range(PAIRS0 - 1):
                for i, (lo, hi) in enumerate(PARTS):
                    r = slice(32 * p, 32 * p + 32)
                    nc.vector.tensor_scalar(kx[r, :, p, lo:hi],
                                            ps[r, 5, :].rearrange("p (k n) -> p k n", n=S)[:, :, lo:hi],
                                            cols[r, 2 + 2 * i:3 + 2 * i], cols[r, 3 + 2 * i:4 + 2 * i],
                                            ALU.mult, ALU.add).then_inc(*A["kT_ready"].up())

        def pe_A_probs(pe, g, t):
            pe.wait_ge(*A["probs_ready"].at(g, 2 * t + 2))
            for k in range(8):
                last = nc.tensor.transpose(ps[:, 2 * t + k // 4, k % 4 * P:(k % 4 + 1) * P],
                                           probs[:, t, 2 * k:2 * k + 2, :].rearrange("p a b -> p (a b)"), ident)
            last.then_inc(*A["pT_done"].up())

        def pe_A_values(pe, g, t):
            pe.wait_ge(*A["pT_ready"].at(g, t + 1))
            if t == 0:
                pe.wait_ge(*A["kv_ready"].at(g, 6))
            for k in range(8):
                last = nc.tensor.matmul(ps[:, 6 + t, k * 64:(k + 1) * 64], pT[:, t, k, :],
                                        vz[:, t, k].rearrange("p b n -> p (b n)"), start=True, stop=True)
            if t == TILES - 1:
                last.then_inc(*A["pv_done"].up())

        def pe_A_turn_out(pe, g):
            pe.wait_ge(*A["an_ready"].at(g, 4))
            turn(an, 6).then_inc(*A["anT_done"].up())

        def pe_A_out(pe, g):
            pe.wait_ge(*A["an_hi"].at(g, 1))
            pe.wait_ge(*A["an_lo"].at(g, 1))
            for t in range(TILES):
                for c in range(DC):
                    last = mm3(ps[:, 7, t * D:(t + 1) * D], aT_hi[:, c, t * P:(t + 1) * P],
                               aT_lo[:, c, t * P:(t + 1) * P], wo_hi[:, c, :], wo_lo[:, c, :], c == 0, c == DC - 1)
            last.then_inc(*A["o_done"].up())

        def act_A_exp(act, g, t):
            act.wait_ge(*A["shifted"].at(g, 2 * t + 2))
            v = split_tokens(probs[:, t])
            nc.scalar.activation(v, v, ACT.Exp, scale=HD0 ** -0.5).then_inc(*A["exp_ready"].up())

        def act_A_probs(act, g, t):
            act.wait_ge(*A["pT_done"].at(g, t + 1))
            nc.scalar.copy(split_tokens(pT[:, t]), split_tokens(ps[:, 2 * t:2 * t + 2, :])
                           ).then_inc(*A["pT_ready"].up())

        def act_A_an(act, g):
            act.wait_ge(*A["pv_done"].at(g, 1))
            for b in range(2):
                for h in range(2):
                    src = ps[S * h:S * h + S, 6:8, :].rearrange("p t (k b h n) -> p (t k) b h n", b=2, h=2, n=HD0)
                    dst = an[S * b:S * b + S].rearrange("p t (k h n) -> p (t k) h n", k=8, h=2)
                    nc.scalar.copy(dst[:, :, h, :], src[:, :, b, h, :]).then_inc(*A["an_ready"].up())

        def act_A_upper(act, g):
            act.wait_ge(*A["anT_done"].at(g, 1))
            nc.scalar.copy(split_tokens(aT_hi), ps[:, 6, :]).then_inc(*A["an_hi"].up())

        def act_A_prep(act, g):
            act.wait_ge(A_prep_in, g * 16 + 16)
            nc.scalar.copy(wB_hi[:, bass.ds(g * GB, GB)], stage[:, 0:GB]).then_inc(*A["prep_hi"].up())

        def dve_A_shift(dve, g, t):
            dve.wait_ge(*A["scores_done"].at(g, t + 1))
            s = split_tokens(ps[:, 2 * t:2 * t + 2, :]).rearrange("p (k n) -> p k n", n=S)
            for i, (lo, hi) in enumerate(PARTS):
                nc.vector.tensor_reduce(mxA[:, t, 16 * i:16 * i + 16], s[:, :, lo:hi], AX,
                                        ALU.max).then_inc(*A["maxed"].up())
            for i, (lo, hi) in enumerate(PARTS):
                dve.wait_ge(*A["maxed"].at(g, 2 * t + i + 1))
                nc.vector.tensor_tensor(probs[:, t, :, lo:hi], s[:, :, lo:hi],
                                        bc_last(mxA[:, t, 16 * i:16 * i + 16], hi - lo),
                                        ALU.subtract).then_inc(*A["shifted"].up())

        def dve_A_sum(dve, g, t):
            dve.wait_ge(*A["exp_ready"].at(g, t + 1))
            for i, (lo, hi) in enumerate(PARTS):
                nc.vector.tensor_reduce(smA[:, t, 16 * i:16 * i + 16], probs[:, t, :, lo:hi], AX,
                                        ALU.add).then_inc(*A["summed"].up())
            dve.wait_ge(*A["summed"].at(g, 2 * t + 2))
            nc.vector.reciprocal(rcA[:, t, :], smA[:, t, :]).then_inc(*A["recip_ready"].up())

        def dve_A_lower(dve, g):
            dve.wait_ge(*A["an_hi"].at(g, 1))
            nc.vector.tensor_tensor(split_tokens(aT_lo), ps[:, 6, :], split_tokens(aT_hi).bitcast(F32),
                                    ALU.subtract).then_inc(*A["an_lo"].up())

        def dve_A_add(dve, g):
            dve.wait_ge(*A["o_done"].at(g, 1))
            nc.vector.tensor_tensor(an, ps[:, 7, :].rearrange("p (t n) -> p t n", t=TILES), bc_mid(bo, TILES),
                                    ALU.add).then_inc(*A["o_biased"].up())
            dve.wait_ge(*A["o_biased"].at(g, 1))
            xg = x[:, bass.ds(g * TILES, TILES), :] if not isinstance(g, int) else x[:, g * TILES:(g + 1) * TILES, :]
            nc.vector.scalar_tensor_tensor(out=xg, in0=an, scalar=tg[:, 0:1], in1=xg, op0=ALU.mult,
                                           op1=ALU.add).then_inc(*A["x_done"].up())

        def pool_A_scale(pool, g, t):
            pool.wait_ge(*A["recip_ready"].at(g, t + 1))
            for i, (lo, hi) in enumerate(PARTS):
                v = probs[:, t, :, lo:hi]
                nc.gpsimd.tensor_tensor(v, v, bc_last(rcA[:, t, 16 * i:16 * i + 16], hi - lo),
                                        ALU.mult).then_inc(*A["probs_ready"].up())

        def pool_A_prep(pool, g):
            pool.wait_ge(*A["prep_hi"].at(g, 1))
            nc.gpsimd.tensor_tensor(wB_lo[:, bass.ds(g * GB, GB)], stage[:, 0:GB],
                                    wB_hi[:, bass.ds(g * GB, GB)].bitcast(F32), ALU.subtract
                                    ).then_inc(*A["prep_lo"].up())

        def pe_A_start(pe):
            front_pe(pe, 0, 7)
            pe_A_kv(pe, 0)
            pe_A_q(pe, 0)
            front_pe(pe, 1, 7)
            pe_A_turn(pe, 0)
            for t in range(TILES):
                pe_A_scores(pe, 0, t)
            pe_A_kv(pe, 1)

        def pe_A(pe, g, more, two_more):
            n = g + 1
            if more:
                pe_A_q(pe, n)
            pe_A_probs(pe, g, 0)
            if more:
                pe.wait_ge(*A["q_ready"].at(n, 1))
            pe_A_values(pe, g, 0)
            if more:
                pe_A_turn(pe, n)
            pe_A_probs(pe, g, 1)
            if more:
                front_pe(pe, g + 2, 1)
            pe.wait_ge(*A["x_done"].at(g, 0))
            pe_A_values(pe, g, 1)
            if more:
                pe.wait_ge(*front["lo_ready"].at(g + 2, 1))
                pe_A_scores(pe, n, 0)
            pe_A_turn_out(pe, g)
            if two_more:
                pe_A_kv(pe, g + 2)
            pe_A_out(pe, g)
            if more:
                pe_A_scores(pe, n, 1)

        def act_A_start(act):
            act_A_ctx(act, 0)
            front_upper(act, 0, 7)
            act_A_square(act, 0)
            act_A_guess(act, 0)
            front_upper(act, 1, 7)
            act_A_ctx(act, 1)
            act_A_qk(act, 0)
            act_A_k(act, 0)
            act.wait_ge(wS_in, 16)
            nc.scalar.copy(wS_hi, stage[:, GB:GB + NWS]).then_inc(setup_act, 1)
            act.wait_ge(sel_in, 16)
            nc.scalar.copy(sel.rearrange("p k n -> p (k n)"), stage[0:E + 1, 0:NSEL]).then_inc(setup_act, 1)

        def act_A(act, g, more, two_more):
            n = g + 1
            act_A_prep(act, g)
            act_A_exp(act, g, 0)
            if more:
                act_A_square(act, n)
                act_A_guess(act, n)
            else:
                act_A_exp(act, g, 1)
            if two_more:
                act_A_ctx(act, g + 2)
            act_A_probs(act, g, 0)
            if more:
                act_A_exp(act, g, 1)
                act_A_qk(act, n)
                act_A_k(act, n)
            act_A_probs(act, g, 1)
            if more:
                front_upper(act, g + 2, 1)
            act_A_an(act, g)
            act_A_upper(act, g)

        def dve_A_start(dve):
            def centre(v, first, n):
                h, mean = v.rearrange("p (h n) -> p h n", n=HD0), gsum[:, 0:n]
                nc.vector.tensor_reduce(mean, h, AX, ALU.add).then_inc(centred, 1)
                dve.wait_ge(centred, first + 1)
                nc.vector.tensor_scalar(mean, mean, 1.0 / HD0, None, ALU.mult).then_inc(centred, 1)
                dve.wait_ge(centred, first + 2)
                nc.vector.tensor_tensor(h, h, bc_last(mean, HD0), ALU.subtract).then_inc(centred, 1)
                dve.wait_ge(centred, first + 3)

            dve.wait_ge(wA1_in, 16)
            centre(stage[:, 0:NWC], 0, NWC // HD0)
            dve.wait_ge(x0_in, 16)
            front_dve(dve, 0, 0)
            dve.wait_ge(wA_hi_ready, 1)
            nc.vector.tensor_tensor(wA_lo[:, 0:NWC], stage[:, 0:NWC], wA_hi[:, 0:NWC].bitcast(F32),
                                    ALU.subtract).then_inc(wA_lo_ready, 1)
            dve.wait_ge(wA_hi_ready, 2)
            nc.vector.tensor_tensor(wA_lo[:, NWC:], stage[:, NWC:NWA], wA_hi[:, NWC:].bitcast(F32),
                                    ALU.subtract).then_inc(wA_lo_ready, 1)
            dve.wait_ge(ctxT_in, 16)
            dve.wait_ge(setup_pool, 4)
            dve_A_ctx(dve, 0)
            front_lower(dve, 0, 7)
            dve.wait_ge(vec_in, 16 * 6)
            centre(bq, 3, H0)
            centre(bkv[:, 0:D], 6, H0)
            dve.wait_ge(const_in, 16)
            nc.vector.tensor_scalar(q_scale, parity, cols[:, 0:1], None, ALU.mult).then_inc(setup_dve, 1)
            nc.vector.tensor_scalar(q_shift, parity, cols[:, 1:2], None, ALU.mult).then_inc(setup_dve, 1)
            dve_A_kv(dve, 0)
            dve_A_q(dve, 0)
            dve_A_values(dve, 0)
            dve_A_var(dve, 0)
            dve.wait_ge(x_in, 16)
            front_dve(dve, 1, 1)
            dve_A_scale(dve, 0)
            front_lower(dve, 1, 7)
            dve_A_ctx(dve, 1)
            dve_A_k(dve, 0)
            dve.wait_ge(lut_in, 16)
            lp = lut.rearrange("p (j b) -> p j b", b=2)
            nc.vector.tensor_tensor(lut_step, lp[:, :, 1], lp[:, :, 0], ALU.subtract).then_inc(setup_dve, 1)
            dve.wait_ge(mask_in, 32)
            nc.vector.tensor_copy(mask_n, mask_n8).then_inc(setup_dve, 1)
            nc.vector.memset(ones_row, 1.0).then_inc(setup_dve, 1)
            dve.wait_ge(setup_act, 1)
            nc.vector.tensor_tensor(wS_lo, stage[:, GB:GB + NWS], wS_hi.bitcast(F32),
                                    ALU.subtract).then_inc(setup_dve, 1)

        def dve_A(dve, g, more, two_more):
            n = g + 1
            dve_A_shift(dve, g, 0)
            if more:
                dve_A_kv(dve, n)
                dve_A_q(dve, n)
            dve_A_sum(dve, g, 0)
            if more:
                dve_A_var(dve, n)
            dve_A_shift(dve, g, 1)
            if more:
                front_stats(dve, g + 2, (g + 2) % GROUPS)
                dve_A_scale(dve, n)
            dve_A_sum(dve, g, 1)
            if more:
                front_norm(dve, g + 2, (g + 2) % GROUPS)
                dve_A_k(dve, n)
                front_lower(dve, g + 2, 1)
            if two_more:
                dve_A_ctx(dve, g + 2)
            dve_A_lower(dve, g)
            if more:
                dve_A_values(dve, n)
            dve_A_add(dve, g)
            dve.wait_ge(*A["x_done"].at(g, 1))

        def pool_A_start(pool):
            front_pool(pool, 0)
            front_pool(pool, 1)

        def pool_A(pool, g, more, two_more):
            pool_A_prep(pool, g)
            pool_A_scale(pool, g, 0)
            if more:
                front_pool(pool, g + 2)
            pool_A_scale(pool, g, 1)

        def sp_A(sp, g):
            sp.dma_start(stage[:, 0:GB], a["wB"][bass.ds(g, 1)].rearrange("o p n -> p (o n)")).then_inc(A_prep_in, 16)
            sp.wait_ge(A_prep_in, g * 16 + 16)
            sp.sem_inc(waited, 1)
            sp.wait_ge(*A["prep_lo"].at(g, 1))
            sp.sem_inc(waited, 1)

        take = carver(work)
        lgs = take(TILES * NL).rearrange("p (t n) -> p t n", t=TILES)
        m8, ixf = (take(TILES * 8).rearrange("p (t n) -> p t n", t=TILES) for _ in range(2))
        ix = take(TILES * 8).bitcast(U32).rearrange("p (t n) -> p t n", t=TILES)
        ex, chosen, wsel = (take(TILES * E).rearrange("p (t n) -> p t n", t=TILES) for _ in range(3))
        comb = take(TILES * (E + 1)).rearrange("p (t n) -> p t n", t=TILES)
        eq = take(TILES * E * TOPK).rearrange("p (t n k) -> p t n k", t=TILES, k=TOPK)
        wsum, wrec, whalf, sgate = (take(TILES) for _ in range(4))
        th, h1, h2, h3 = ([take(TG) for _ in range(3)] for _ in range(4))
        take_r = carver(workr)
        h_hi, h_lo = ([take_r(TG) for _ in range(3)] for _ in range(2))
        combT_hi, combT_lo = (take_r(TG)[0:E + 1] for _ in range(2))
        sel = take_r((EC + 1) * P)[0:E + 1].rearrange("p (k n) -> p k n", k=EC + 1)
        logits = ps[:, 2, 0:TILES * NL]
        combT = ps[0:E + 1, 6, TG:2 * TG]
        wqT, wkT = stage[:, 0:HG * D].rearrange("p (h n) -> p h n", h=HG), \
            stage[:, HG * D:HG * D + HG // 2 * DV].rearrange("p (h n) -> p h n", h=HG // 2)
        wvT = stage[:, HG * D + HG // 2 * DV:HG * D + HG * DV].rearrange("p (h n) -> p h n", h=HG // 2)
        wo1 = stage[:, HG * D + HG * DV:GCW].rearrange("p (h n) -> p h n", h=HG)
        JOIN = ((wM_hi, wM_lo), (wM_hi, wM_lo), (wN_hi, wN_lo), (wN_hi, wN_lo))

        def rows_B(k):
            return P if k < EC else F

        def gate_of(k):
            return ps[:, (3, 4, 1)[k % 3], 0:TG]

        def up_of(k):
            return ps[:, (3, 4, 1)[k % 3], TG:2 * TG]

        def up_B(k):
            return up_of(k) if k < EC else gate_of(k)[F:2 * F]

        def spread_of(k):
            return ps[:, (5, 2)[k % 2], 0:TG]

        def pe_B(pe, g):
            x_split(pe, 4 + g)
            for t in range(TILES):
                for c in range(DC):
                    last = mm3(logits[:, t * NL:(t + 1) * NL], xT_hi[:, c, t * P:(t + 1) * P],
                               xT_lo[:, c, t * P:(t + 1) * P], wr_hi[:, c, :], wr_lo[:, c, :], c == 0, c == DC - 1)
            last.then_inc(*Bp["logits_done"].up())

            def gate_up(k):
                pe.wait_ge(*Bp["h2"].at(g, k - 2))
                if k < EC:
                    col = slice(k % 2 * P, k % 2 * P + P)
                    for o, w_hi, w_lo in ((gate_of(k), eg_hi, eg_lo), (up_of(k), eu_hi, eu_lo)):
                        for c in range(DC):
                            last = mm3(o, w_hi[:, k // 2, c, col],
                                       w_lo[:, k // 2, c, col], xT_hi[:, c, :], xT_lo[:, c, :], c == 0, c == DC - 1)
                else:
                    for c in range(DC):
                        last = mm3(gate_of(k), sgu_hi[:, c, :], sgu_lo[:, c, :], xT_hi[:, c, :],
                                   xT_lo[:, c, :], c == 0, c == DC - 1)
                last.then_inc(*Bp["gu_done"].up())

            def spread(k):
                if k >= 2:
                    pe.wait_ge(*Bp["h3"].at(g, k - 1))
                o = spread_of(k)
                nc.tensor.matmul(o, sel[:, k, :], combT_hi, start=True, stop=False)
                nc.tensor.matmul(o, sel[:, k, :], combT_lo, start=False, stop=True).then_inc(*Bp["bc_done"].up())

            def down(k):
                pe.wait_ge(*Bp["h_hi"].at(g, k + 1))
                pe.wait_ge(*Bp["h_lo"].at(g, k + 1))
                n = rows_B(k)
                d_hi, d_lo = (ed_hi[:, k // 2, k % 2, :], ed_lo[:, k // 2, k % 2, :]) if k < EC else (sd_hi, sd_lo)
                for t in range(TILES):
                    last = mm3(ps[:, 6 + t, 0:D], h_hi[k % 3][0:n, t * P:(t + 1) * P],
                               h_lo[k % 3][0:n, t * P:(t + 1) * P], d_hi, d_lo, k == 0, k == EC)
                return last

            def join(r):
                if r == 0:
                    pe.wait_ge(B_prep_in, g * 16 + 16)
                pe.wait_ge(*Bp["join_lo"].at(g, r))
                for i in range(2):
                    h = 2 * (r % 2) + i
                    for c in range(DC) if r < 2 else ():
                        last = nc.tensor.matmul(ps[:, 0, i * D + c * DV:i * D + (c + 1) * DV],
                                                wqT[:, h, c * P:(c + 1) * P], wkT[:, h // 2, :], start=True, stop=True)
                    if r >= 2:
                        last = nc.tensor.matmul(ps[:, 0, i * D:(i + 1) * D], wvT[:, h // 2, :],
                                                wo1[:, h, :], start=True, stop=True)
                last.then_inc(*Bp["join_done"].up())

            gate_up(0)
            gate_up(1)
            join(0)
            gate_up(2)
            pe.wait_ge(*Bp["x_done"].at(g, 0))
            pe.wait_ge(*Bp["comb_ready"].at(g, 2))
            for t in range(TILES):
                last = nc.tensor.transpose(combT[:, t * P:(t + 1) * P], comb[:, t, :], ident)
            last.then_inc(*Bp["combT_done"].up())
            gate_up(3)
            pe.wait_ge(*Bp["combT_hi"].at(g, 1))
            pe.wait_ge(*Bp["combT_lo"].at(g, 1))
            spread(0)
            spread(1)
            join(1)
            gate_up(4)
            down(0)
            spread(2)
            down(1)
            spread(3)
            for k in range(5, EC + 1):
                gate_up(k)
                if k == 5:
                    join(2)
                if k == EC:
                    pe.wait_ge(*Bp["join_lo"].at(g, 3))
                    front_pe(pe, 5 + g, 0)
                down(k - 3)
                spread(k - 1)
            down(EC - 2)
            spread(EC)
            pe.wait_ge(*front["lo_ready"].at(5 + g, 1))
            join(3)
            down(EC - 1)
            down(EC).then_inc(*Bp["out_done"].up())

        def act_B(act, g):

            def tanh(k):
                act.wait_ge(*Bp["gu_done"].at(g, k + 1))
                n = rows_B(k)
                nc.scalar.activation(th[k % 3][0:n], gate_of(k)[0:n], ACT.Tanh,
                                     scale=0.5).then_inc(*Bp["tanh_ready"].up())

            def upper(k):
                act.wait_ge(*Bp["h3"].at(g, k + 1))
                n = rows_B(k)
                nc.scalar.copy(h_hi[k % 3][0:n], h3[k % 3][0:n]).then_inc(*Bp["h_hi"].up())

            def join(r):
                act.wait_ge(*Bp["join_done"].at(g, r + 1))
                w = JOIN[r][0][:, bass.ds(g * HG + 2 * (r % 2), 2), :]
                nc.scalar.copy(w, ps[:, 0, :].rearrange("p (h n) -> p h n", h=2)).then_inc(*Bp["join_hi"].up())

            tanh(0)
            act.wait_ge(*Bp["shifted"].at(g, 1))
            nc.scalar.activation(ex, ex, ACT.Exp).then_inc(*Bp["exp_ready"].up())
            nc.scalar.activation(sgate, lgs[:, :, E], ACT.Tanh, scale=0.5).then_inc(*Bp["gate_ready"].up())
            tanh(1)
            join(0)
            tanh(2)
            act.wait_ge(*Bp["combT_done"].at(g, 1))
            nc.scalar.copy(combT_hi, combT).then_inc(*Bp["combT_hi"].up())
            upper(0)
            for k in range(3, EC + 1):
                tanh(k)
                upper(k - 2)
                if k in (3, 5):
                    join(k // 2)
            front_upper(act, 5 + g, 0)
            upper(EC - 1)
            upper(EC)
            join(3)

        def dve_B(dve, g):
            front_stats(dve, 5 + g, after(g))

            def gated(k):
                n = rows_B(k)
                dve.wait_ge(*Bp["tanh_ready"].at(g, k + 1))
                nc.vector.scalar_tensor_tensor(out=h1[k % 3][0:n], in0=th[k % 3][0:n], scalar=1.0,
                                               in1=gate_of(k)[0:n], op0=ALU.add,
                                               op1=ALU.mult).then_inc(*Bp["h1"].up())
                dve.wait_ge(*Bp["h1"].at(g, k + 1))
                nc.vector.tensor_tensor(h2[k % 3][0:n], h1[k % 3][0:n], up_B(k), ALU.mult).then_inc(*Bp["h2"].up())

            def weighted(k):
                n = rows_B(k)
                dve.wait_ge(*Bp["h2"].at(g, k + 1))
                dve.wait_ge(*Bp["bc_done"].at(g, k + 1))
                nc.vector.tensor_tensor(h3[k % 3][0:n], h2[k % 3][0:n], spread_of(k)[0:n],
                                        ALU.mult).then_inc(*Bp["h3"].up())

            def join(r):
                dve.wait_ge(*Bp["join_hi"].at(g, r + 1))
                hi, lo = (w[:, bass.ds(g * HG + 2 * (r % 2), 2), :] for w in JOIN[r])
                nc.vector.tensor_tensor(lo, ps[:, 0, :].rearrange("p (h n) -> p h n", h=2),
                                        hi.bitcast(F32), ALU.subtract).then_inc(*Bp["join_lo"].up())

            dve.wait_ge(*Bp["logits_done"].at(g, 1))
            nc.vector.tensor_copy(lgs, logits.rearrange("p (t n) -> p t n", t=TILES)
                                  ).then_inc(*Bp["dve"].up())
            dve.wait_ge(*Bp["dve"].last(g))
            dve.sem_inc(waited, 1)
            for t in range(TILES):
                nc.vector.max(m8[:, t, :], lgs[:, t, 0:E]).then_inc(*Bp["dve"].up())
            dve.wait_ge(*Bp["dve"].last(g))
            nc.vector.tensor_tensor(ex, lgs[:, :, 0:E], m8[:, :, 0:1].broadcast_to([P, TILES, E]),
                                    ALU.subtract).then_inc(*Bp["shifted"].up())
            for t in range(TILES):
                nc.vector.max_index(ix[:, t, :], m8[:, t, :], lgs[:, t, 0:E]).then_inc(*Bp["dve"].up())
            dve.wait_ge(*Bp["dve"].last(g))
            nc.vector.tensor_copy(ixf, ix).then_inc(*Bp["dve"].up())
            dve.wait_ge(*Bp["dve"].last(g))
            nc.vector.tensor_tensor(eq, iota.unsqueeze(1).unsqueeze(3).broadcast_to([P, TILES, E, TOPK]),
                                    ixf[:, :, 0:TOPK].unsqueeze(2).broadcast_to([P, TILES, E, TOPK]),
                                    ALU.is_equal).then_inc(*Bp["dve"].up())
            dve.wait_ge(*Bp["dve"].last(g))
            nc.vector.tensor_reduce(chosen, eq, AX, ALU.add).then_inc(*Bp["dve"].up())
            dve.wait_ge(*Bp["dve"].last(g))
            dve.wait_ge(*Bp["exp_ready"].at(g, 1))
            nc.vector.tensor_tensor(wsel, ex, chosen, ALU.mult).then_inc(*Bp["dve"].up())
            dve.wait_ge(*Bp["dve"].last(g))
            nc.vector.tensor_reduce(wsum, wsel, AX, ALU.add).then_inc(*Bp["dve"].up())
            dve.wait_ge(*Bp["dve"].last(g))
            nc.vector.reciprocal(wrec, wsum).then_inc(*Bp["dve"].up())
            dve.wait_ge(*Bp["dve"].last(g))
            nc.vector.tensor_scalar(whalf, wrec, 0.5, None, ALU.mult).then_inc(*Bp["dve"].up())
            dve.wait_ge(*Bp["dve"].last(g))
            nc.vector.tensor_tensor(comb[:, :, 0:E], wsel, bc_last(whalf, E), ALU.mult).then_inc(*Bp["comb_ready"].up())
            dve.wait_ge(*Bp["gate_ready"].at(g, 1))
            nc.vector.tensor_scalar(comb[:, :, E], sgate, 0.25, 0.25, ALU.mult, ALU.add).then_inc(*Bp["comb_ready"].up())
            gated(0)
            gated(1)
            join(0)
            dve.wait_ge(*Bp["combT_hi"].at(g, 1))
            nc.vector.tensor_tensor(combT_lo, combT, combT_hi.bitcast(F32),
                                    ALU.subtract).then_inc(*Bp["combT_lo"].up())
            gated(2)
            weighted(0)
            front_norm(dve, 5 + g, after(g))
            for k in range(3, EC + 1):
                weighted(k - 2)
                gated(k)
                if k in (3, 5):
                    join(k // 2)
            weighted(EC - 1)
            front_lower(dve, 5 + g, 0)
            weighted(EC)
            join(3)
            dve.wait_ge(*Bp["out_done"].at(g, 1))
            for t in range(TILES):
                xt = x[:, g * TILES + t, :]
                nc.vector.scalar_tensor_tensor(out=xt, in0=ps[:, 6 + t, 0:D], scalar=tg[:, 1:2], in1=xt,
                                               op0=ALU.mult, op1=ALU.add).then_inc(*Bp["x_done"].up())
            dve.wait_ge(*Bp["x_done"].at(g, TILES))

        def pool_B(pool, g):
            front_pool(pool, 5 + g)
            for k in range(EC + 1):
                n = rows_B(k)
                pool.wait_ge(*Bp["h_hi"].at(g, k + 1))
                nc.gpsimd.tensor_tensor(h_lo[k % 3][0:n], h3[k % 3][0:n], h_hi[k % 3][0:n].bitcast(F32),
                                        ALU.subtract).then_inc(*Bp["h_lo"].up())

        def sp_B(sp, g):
            sp.dma_start(stage, a["wC"][bass.ds(g, 1)].rearrange("o p n -> p (o n)")).then_inc(B_prep_in, 16)
            sp.wait_ge(B_prep_in, g * 16 + 16)
            sp.sem_inc(waited, 1)
            sp.wait_ge(*Bp["join_done"].at(g, 4))
            sp.sem_inc(waited, 1)

        take = carver(work)
        qt = take(PAIRS1 * 2 * TG).rearrange("p (j b h n) -> p j b h n", j=PAIRS1, b=BG, h=2)
        pC = take(2 * 512).rearrange("p (s k n) -> p s k n", s=2, k=8)
        mxC, smC, rcC = (take(4 * 8).rearrange("p (s n) -> p s n", s=4) for _ in range(3))
        bits = take(4 * RMAX).bitcast(I32).rearrange("p (b n) -> p b n", b=4)
        lev = take(8 * RMAX).rearrange("p (j n) -> p j n", j=8)
        take_r = carver(workr)
        pT_hi, pT_lo = (take_r(TILES * 512).rearrange("p (t n) -> p t n", t=TILES) for _ in range(2))
        cx_hi, cx_lo = (take_r(TILES * DV).rearrange("p (t n) -> p t n", t=TILES) for _ in range(2))
        z_hi, z_lo = (shared_r[:, i * HALF * TG:(i + 1) * HALF * TG].rearrange("p (h n) -> p h n", h=HALF)
                      for i in range(2))
        idx = stage[:, 0:sum(ROUNDS)].bitcast(I32)
        TURNED = (5, 0)

        def q_of(n):
            return ps[:, (1, 7)[n % 2], :]

        POOL_LEVEL1 = 6

        def z_of(n):
            return ps[:, (6, 7, 1)[n % 3], :]

        ctx_g = stage[:, sum(ROUNDS):sum(ROUNDS) + TG]

        def decoded(w, g, r):
            if r < 2:
                return w[r][:, :, bass.ds(g * IG, IG)]
            return w[2][:, :, bass.ds(g * DG, DG)]

        def shape_r(v, r):
            return v.rearrange("p (c n) -> p c n", c=DC if r < 2 else FC)

        def pe_C(pe, g):
            x_split(pe, 8 + g)

            def queries(u):
                for j in range(PAIRS1):
                    n = u * PAIRS1 + j
                    if n >= 2:
                        pe.wait_ge(*C["q_ready"].at(g, n - 1))
                    for h in range(2):
                        hh = 2 * n + h
                        for c in range(DC):
                            last = mm3(q_of(n)[:, h * TG:(h + 1) * TG], wM_hi[:, hh, c * DV:(c + 1) * DV],
                                       wM_lo[:, hh, c * DV:(c + 1) * DV], xT_hi[:, c, :], xT_lo[:, c, :],
                                       c == 0, c == DC - 1)
                    last.then_inc(*C["q_done"].up())

            def scores(u):
                if u == 0:
                    pe.wait_ge(*C["mask_ready"].at(g, 2))
                for s in range(2):
                    if u:
                        pe.wait_ge(*C["shifted"].at(g, s + 1))
                    nc.tensor.matmul(ps[:, 3 + s, :], ones_row, mask_rows.rearrange("p a n -> p (a n)"),
                                     start=True, stop=False)
                    pe.wait_ge(*C["q_ready"].at(g, u * PAIRS1 + 2 * s + 2))
                    for jj in range(2):
                        for b in range(BG):
                            k = jj * BG + b
                            last = nc.tensor.matmul(ps[:, 3 + s, k * S:(k + 1) * S],
                                                    qt[:, 2 * s + jj, b].rearrange("p h n -> p (h n)"),
                                                    ctx_g[:, b * S:(b + 1) * S], start=False, stop=k == 7)
                    last.then_inc(*C["scores_done"].up())

            def turn_probs(u, s):
                n = 2 * u + s
                pe.wait_ge(*C["probs_ready"].at(g, n + 1))
                if n >= 2:
                    pe.wait_ge(*C["pT_lo"].at(g, n - 1))
                for k in range(4):
                    last = nc.tensor.transpose(ps[:, TURNED[s], k * P:(k + 1) * P],
                                               pC[:, s, 2 * k:2 * k + 2, :].rearrange("p a b -> p (a b)"), ident)
                last.then_inc(*C["pT_done"].up())

            def mix(u):
                if u == 0:
                    pe.wait_ge(*C["cx_lo"].at(g, 1))
                    pe.wait_ge(*C["q_ready"].at(g, 2 * PAIRS1))
                pe.wait_ge(*C["pT_lo"].at(g, 2 * u + 2))
                for t in range(TILES):
                    for b in range(2):
                        n = u * BG + 2 * t + b
                        if n >= 3:
                            pe.wait_ge(*C["z_lo"].at(g, n - 2))
                        r = slice(S * b, S * b + S)
                        mm3(z_of(n), cx_hi[r, t, :], cx_lo[r, t, :], pT_hi[r, t, :], pT_lo[r, t, :],
                            True, True).then_inc(*C["z_done"].up())

            def output(u, t):
                pe.wait_ge(*C["z_lo"].at(g, u * BG + 2 * t + 2))
                if t == 0:
                    pe.wait_ge(*C["x_done"].at(g, u))
                for h in range(HALF):
                    hh = u * HALF + h
                    last = mm3(ps[:, 2, t * D:(t + 1) * D], z_hi[:, h, t * P:(t + 1) * P],
                               z_lo[:, h, t * P:(t + 1) * P], wN_hi[:, hh, :], wN_lo[:, hh, :],
                               h == 0, h == HALF - 1)
                if t == TILES - 1:
                    last.then_inc(*C["out_done"].up())

            queries(0)
            scores(0)
            queries(1)
            turn_probs(0, 0)
            turn_probs(0, 1)
            scores(1)
            mix(0)
            turn_probs(1, 0)
            output(0, 0)
            turn_probs(1, 1)
            output(0, 1)
            front_pe(pe, 9 + g, 3)
            mix(1)
            output(1, 0)
            output(1, 1)

        def act_C(act, g):

            def queries(u):
                for j in range(PAIRS1):
                    n = u * PAIRS1 + j
                    act.wait_ge(*C["q_done"].at(g, n + 1))
                    if u:
                        act.wait_ge(*C["scores_done"].at(g, j // 2 + 1))
                    nc.scalar.copy(qt[:, j].rearrange("p b h n -> p h b n"),
                                   q_of(n).rearrange("p (h b n) -> p h b n", h=2, b=BG)
                                   ).then_inc(*C["q_ready"].up())

            def exps(u, s):
                act.wait_ge(*C["shifted"].at(g, 2 * u + s + 1))
                v = split_tokens(pC[:, s])
                nc.scalar.activation(v, v, ACT.Exp, scale=HD1 ** -0.5).then_inc(*C["exp_ready"].up())

            def upper_probs(u):
                for s in range(2):
                    act.wait_ge(*C["pT_done"].at(g, 2 * u + s + 1))
                    dst = pT_hi.rearrange("p t (j n) -> p t j n", j=PAIRS1)[:, :, 2 * s:2 * s + 2, :]
                    nc.scalar.copy(dst.rearrange("p t j n -> p j t n"),
                                   ps[:, TURNED[s], :].rearrange("p (j t n) -> p j t n", j=2, t=2)
                                   ).then_inc(*C["pT_hi"].up())

            def upper_z(u, k):
                act.wait_ge(*C["z_done"].at(g, u * BG + k + 1))
                if u and k == 0:
                    act.wait_ge(*C["out_done"].at(g, 1))
                nc.scalar.copy(z_hi[:, :, k * S:(k + 1) * S],
                               z_of(u * BG + k).rearrange("p (h n) -> p h n", h=HALF)).then_inc(*C["z_hi"].up())

            def level1(r):
                n = ROUNDS[r]
                act.wait_ge(*C["bits"].at(g, 4 * r + 1))
                for j in range(POOL_LEVEL1, 8):
                    nc.scalar.activation(lev[:, j, 0:n], bits[:, 0, 0:n], ACT.Identity, scale=lut_step[:, j:j + 1],
                                         bias=lut[:, 2 * j:2 * j + 1]).then_inc(*C["level1"].up())

            def upper_decoded(r):
                act.wait_ge(*C["chosen"].at(g, 3 * r + 3))
                nc.scalar.copy(decoded((fg_hi, fu_hi, fd_hi), g, r), shape_r(lev[:, 0, 0:ROUNDS[r]], r)
                               ).then_inc(*C["dec_hi"].up())

            queries(0)
            act.wait_ge(*C["ctx_masked"].at(g, TILES))
            nc.scalar.copy(split_tokens(cx_hi), split_tokens(ctx_n)).then_inc(*C["cx_hi"].up())
            level1(0)
            exps(0, 0)
            exps(0, 1)
            queries(1)
            upper_probs(0)
            upper_decoded(0)
            level1(1)
            exps(1, 0)
            upper_z(0, 0)
            upper_z(0, 1)
            exps(1, 1)
            upper_z(0, 2)
            upper_z(0, 3)
            upper_decoded(1)
            upper_probs(1)
            level1(2)
            front_upper(act, 9 + g, 3)
            upper_z(1, 0)
            upper_z(1, 1)
            upper_z(1, 2)
            upper_z(1, 3)
            upper_decoded(2)

        def dve_C(dve, g):
            front_stats(dve, 9 + g, after(g))
            nc.vector.tensor_scalar(mask_rows, mask_row8[:, bass.ds(g * TG, TG)].unsqueeze(1)
                                    .broadcast_to([1, 2, TG]), -1.0, MASKED, ALU.add, ALU.mult
                                    ).then_inc(*C["mask_ready"].up())
            nc.vector.tensor_copy(ctx_g, ctx_T[:, bass.ds(g * TG, TG)]).then_inc(*C["mask_ready"].up())
            dve.wait_ge(C_nat_in, g * 16 + 16)
            for t in range(TILES):
                nc.vector.tensor_scalar(ctx_n[:, t, :], ctx_n[:, t, :], mask_n[:, bass.ds(g * TILES + t, 1)], None,
                                        ALU.mult).then_inc(*C["ctx_masked"].up())

            def shift(u, s):
                n = 2 * u + s
                dve.wait_ge(*C["scores_done"].at(g, n + 1))
                sc = ps[:, 3 + s, :].rearrange("p (k n) -> p k n", k=8)
                nc.vector.tensor_reduce(mxC[:, n, :], sc, AX, ALU.max).then_inc(*C["maxed"].up())
                dve.wait_ge(*C["maxed"].at(g, n + 1))
                if u:
                    dve.wait_ge(*C["pT_done"].at(g, s + 1))
                nc.vector.tensor_tensor(pC[:, s], sc, bc_last(mxC[:, n, :], S),
                                        ALU.subtract).then_inc(*C["shifted"].up())

            def sums(u, s):
                n = 2 * u + s
                dve.wait_ge(*C["exp_ready"].at(g, n + 1))
                nc.vector.tensor_reduce(smC[:, n, :], pC[:, s], AX, ALU.add).then_inc(*C["summed"].up())
                dve.wait_ge(*C["summed"].at(g, n + 1))
                nc.vector.reciprocal(rcC[:, n, :], smC[:, n, :]).then_inc(*C["recip_ready"].up())

            def lower_probs(u):
                for s in range(2):
                    dve.wait_ge(*C["pT_hi"].at(g, 2 * u + s + 1))
                    lo, hi = (v.rearrange("p t (j n) -> p t j n", j=PAIRS1)[:, :, 2 * s:2 * s + 2, :]
                              .rearrange("p t j n -> p j t n") for v in (pT_lo, pT_hi))
                    nc.vector.tensor_tensor(lo, ps[:, TURNED[s], :].rearrange("p (j t n) -> p j t n", j=2, t=2),
                                            hi.bitcast(F32), ALU.subtract).then_inc(*C["pT_lo"].up())

            def lower_z(u, k):
                dve.wait_ge(*C["z_hi"].at(g, u * BG + k + 1))
                nc.vector.tensor_tensor(z_lo[:, :, k * S:(k + 1) * S],
                                        z_of(u * BG + k).rearrange("p (h n) -> p h n", h=HALF),
                                        z_hi[:, :, k * S:(k + 1) * S].bitcast(F32),
                                        ALU.subtract).then_inc(*C["z_lo"].up())

            def add(u):
                dve.wait_ge(*C["out_done"].at(g, u + 1))
                if u:
                    dve.wait_ge(*C["x_done"].at(g, 1))
                xg = x[:, bass.ds(g * TILES, TILES), :]
                nc.vector.scalar_tensor_tensor(out=xg, in0=ps[:, 2, :].rearrange("p (t n) -> p t n", t=TILES),
                                               scalar=tg[:, 2:3], in1=xg, op0=ALU.mult,
                                               op1=ALU.add).then_inc(*C["x_done"].up())

            def take_bits(r):
                n, o = ROUNDS[r], sum(ROUNDS[:r])
                if r == 0:
                    dve.wait_ge(C_idx_in, g * 16 + 16)
                else:
                    dve.wait_ge(*C["level1"].at(g, 8 * r))
                    dve.wait_ge(*C["chosen"].last(g))
                for bit in range(4):
                    nc.vector.tensor_scalar(bits[:, bit, 0:n], idx[:, o:o + n], 1 << bit, None,
                                            ALU.bitwise_and).then_inc(*C["bits"].up())

            def choose(r):
                n = ROUNDS[r]
                dve.wait_ge(*C["level1"].at(g, 8 * r + 8))
                for i, step in enumerate((1, 2, 4)):
                    left, right = (lev[:, k::2 * step, 0:n] for k in (0, step))
                    m = bits[:, i + 1:i + 2, 0:n].broadcast_to([P, 4 // step, n])
                    if i:
                        dve.wait_ge(*C["chosen"].last(g))
                    else:
                        dve.wait_ge(*C["bits"].at(g, 4 * r + 4))
                    dve.sem_inc(waited, 1)
                    nc.vector.copy_predicated(left, m, right).then_inc(*C["chosen"].up())

            take_bits(0)
            front_norm(dve, 9 + g, after(g))
            shift(0, 0)
            shift(0, 1)
            sums(0, 0)
            sums(0, 1)
            choose(0)
            take_bits(1)
            dve.wait_ge(*C["cx_hi"].at(g, 1))
            nc.vector.tensor_tensor(split_tokens(cx_lo), split_tokens(ctx_n), split_tokens(cx_hi).bitcast(F32),
                                    ALU.subtract).then_inc(*C["cx_lo"].up())
            lower_probs(0)
            shift(1, 0)
            shift(1, 1)
            lower_z(0, 0)
            sums(1, 0)
            lower_z(0, 1)
            sums(1, 1)
            lower_z(0, 2)
            lower_z(0, 3)
            choose(1)
            take_bits(2)
            lower_probs(1)
            add(0)
            front_lower(dve, 9 + g, 3)
            lower_z(1, 0)
            lower_z(1, 1)
            lower_z(1, 2)
            lower_z(1, 3)
            choose(2)
            add(1)
            dve.wait_ge(*C["x_done"].at(g, 2))

        def pool_C(pool, g):
            front_pool(pool, 9 + g)

            def scale(u):
                for s in range(2):
                    n = 2 * u + s
                    pool.wait_ge(*C["recip_ready"].at(g, n + 1))
                    nc.gpsimd.tensor_tensor(pC[:, s], pC[:, s], bc_last(rcC[:, n, :], S),
                                            ALU.mult).then_inc(*C["probs_ready"].up())

            def level1(r):
                n = ROUNDS[r]
                pool.wait_ge(*C["bits"].at(g, 4 * r + 1))
                if r:
                    pool.wait_ge(*C["dec_lo"].at(g, r))
                pool.sem_inc(waited, 1)
                for j in range(POOL_LEVEL1):
                    nc.gpsimd.tensor_scalar(lev[:, j, 0:n], bits[:, 0, 0:n], lut_step[:, j:j + 1],
                                            lut[:, 2 * j:2 * j + 1], ALU.mult, ALU.add).then_inc(*C["level1"].up())

            def lower(r):
                pool.wait_ge(*C["dec_hi"].at(g, r + 1))
                nc.gpsimd.tensor_tensor(decoded((fg_lo, fu_lo, fd_lo), g, r), shape_r(lev[:, 0, 0:ROUNDS[r]], r),
                                        decoded((fg_hi, fu_hi, fd_hi), g, r).bitcast(F32),
                                        ALU.subtract).then_inc(*C["dec_lo"].up())

            level1(0)
            scale(0)
            lower(0)
            level1(1)
            scale(1)
            lower(1)
            level1(2)
            lower(2)
            pool.wait_ge(*C["dec_lo"].at(g, 3))

        def sp_C(sp, g):
            sp.dma_start(ctx_n, a["ctx_n"][bass.ds(g * TILES, TILES)].rearrange("t p n -> p t n")).then_inc(C_nat_in, 16)
            sp.dma_start(idx, a["idx"][bass.ds(g, 1)].rearrange("o p n -> p (o n)")).then_inc(C_idx_in, 16)
            sp.wait_ge(C_nat_in, g * 16 + 16)
            sp.sem_inc(waited, 1)
            sp.wait_ge(C_idx_in, g * 16 + 16)
            sp.sem_inc(waited, 1)
            sp.wait_ge(*C["cx_lo"].at(g, 1))
            sp.sem_inc(waited, 1)
            sp.wait_ge(*C["bits"].at(g, 4 * 3))
            sp.sem_inc(waited, 1)

        take = carver(work)
        fth, fh1, fh3 = ([take(TG) for _ in range(3)] for _ in range(3))
        take_r = carver(workr)
        fh_hi, fh_lo = ([take_r(TG) for _ in range(3)] for _ in range(2))

        def rows_D(k):
            return P if k < FC - 1 else FLAST

        def pe_D(pe, g, more):
            x_split(pe, 12 + g)

            def gate_up(k):
                pe.wait_ge(*Dp["h3"].at(g, k - 2))
                for o, w_hi, w_lo in ((gate_of(k), fg_hi, fg_lo), (up_of(k), fu_hi, fu_lo)):
                    for c in range(DC):
                        last = mm3(o, w_hi[:, c, k * P:(k + 1) * P],
                                   w_lo[:, c, k * P:(k + 1) * P], xT_hi[:, c, :], xT_lo[:, c, :], c == 0, c == DC - 1)
                last.then_inc(*Dp["gu_done"].up())

            def down(k):
                n = rows_D(k)
                if k == 0:
                    pe.wait_ge(*Dp["x_done"].at(g, 0))
                pe.wait_ge(*Dp["h_hi"].at(g, k + 1))
                pe.wait_ge(*Dp["h_lo"].at(g, k + 1))
                for t in range(TILES):
                    last = mm3(ps[:, 6 + t, 0:D], fh_hi[k % 3][0:n, t * P:(t + 1) * P],
                               fh_lo[k % 3][0:n, t * P:(t + 1) * P], fd_hi[0:n, k, :], fd_lo[0:n, k, :],
                               k == 0, k == FC - 1)
                return last

            gate_up(0)
            gate_up(1)
            for k in range(2, FC):
                gate_up(k)
                if more and k == FC - 1:
                    front_pe(pe, 13 + g, 0)
                down(k - 2)
            down(FC - 2)
            down(FC - 1).then_inc(*Dp["out_done"].up())

        def act_D(act, g, more):

            def tanh(k):
                n = rows_D(k)
                act.wait_ge(*Dp["gu_done"].at(g, k + 1))
                nc.scalar.activation(fth[k % 3][0:n], gate_of(k)[0:n], ACT.Tanh,
                                     scale=0.5).then_inc(*Dp["tanh_ready"].up())

            def upper(k):
                n = rows_D(k)
                act.wait_ge(*Dp["h3"].at(g, k + 1))
                nc.scalar.copy(fh_hi[k % 3][0:n], fh3[k % 3][0:n]).then_inc(*Dp["h_hi"].up())

            tanh(0)
            for k in range(1, FC):
                tanh(k)
                upper(k - 1)
            if more:
                front_upper(act, 13 + g, 0)
            upper(FC - 1)

        def dve_D(dve, g, more):
            for k in range(FC):
                if more and k == 2:
                    front_stats(dve, 13 + g, g + 1)
                if more and k == 3:
                    front_norm(dve, 13 + g, g + 1)
                n = rows_D(k)
                dve.wait_ge(*Dp["tanh_ready"].at(g, k + 1))
                nc.vector.scalar_tensor_tensor(out=fh1[k % 3][0:n], in0=fth[k % 3][0:n], scalar=1.0,
                                               in1=gate_of(k)[0:n], op0=ALU.add,
                                               op1=ALU.mult).then_inc(*Dp["h1"].up())
                dve.wait_ge(*Dp["h1"].at(g, k + 1))
                nc.vector.scalar_tensor_tensor(out=fh3[k % 3][0:n], in0=fh1[k % 3][0:n], scalar=0.5,
                                               in1=up_of(k)[0:n], op0=ALU.mult,
                                               op1=ALU.mult).then_inc(*Dp["h3"].up())
            if more:
                front_lower(dve, 13 + g, 0)
            dve.wait_ge(*Dp["out_done"].at(g, 1))
            for t in range(TILES):
                xt = x[:, g * TILES + t, :]
                nc.vector.scalar_tensor_tensor(out=xt, in0=ps[:, 6 + t, 0:D], scalar=tg[:, 3:4], in1=xt,
                                               op0=ALU.mult, op1=ALU.add).then_inc(*Dp["x_done"].up())
            dve.wait_ge(*Dp["x_done"].at(g, TILES))

        def pool_D(pool, g, more):
            for k in range(FC):
                if more and k == 2:
                    front_pool(pool, 13 + g)
                n = rows_D(k)
                pool.wait_ge(*Dp["h_hi"].at(g, k + 1))
                nc.gpsimd.tensor_tensor(fh_lo[k % 3][0:n], fh3[k % 3][0:n], fh_hi[k % 3][0:n].bitcast(F32),
                                        ALU.subtract).then_inc(*Dp["h_lo"].up())

        def sp_D(sp, g):
            sp.wait_ge(*Dp["x_done"].at(g, TILES))
            sp.dma_start(a["out"][bass.ds(g * TILES, TILES)].rearrange("t p n -> p t n"),
                         x[:, bass.ds(g * TILES, TILES), :]).then_inc(out_done, 16)

        block = ctx.enter_context(nc.Block())

        @block.sync
        def _(sp):
            xr = a["x"].rearrange("t p n -> p t n")
            sp.dma_start(stage[:, 0:NWC], a["wA"][:, 0:NWC]).then_inc(wA1_in, 16)
            sp.dma_start(x[:, 0:TILES, :], xr[:, 0:TILES, :]).then_inc(x0_in, 16)
            sp.dma_start(stage[:, NWC:NWA], a["wA"][:, NWC:NWA]).then_inc(wA2_in, 16)
            sp.dma_start(const, a["const"]).then_inc(const_in, 16)
            sp.dma_start(ctx_T, a["ctx_T"]).then_inc(ctxT_in, 16)
            sp.dma_start(vec, a["vec"].partition_broadcast(P)).then_inc(vec_in, 16)
            for b in range(2):
                for (lo, hi), v in zip(PARTS, (a["vec_main"], a["vec_last"])):
                    sp.dma_start(veck[b * S + lo:b * S + hi, :], v.partition_broadcast(hi - lo)).then_inc(vec_in, 16)
            sp.dma_start(cols, a["cols"]).then_inc(vec_in, 16)
            sp.dma_start(x[:, TILES:, :], xr[:, TILES:, :]).then_inc(x_in, 16)
            sp.dma_start(gates, a["gates"].partition_broadcast(P)).then_inc(gates_in, 16)
            sp.dma_start(lut, a["lut"].partition_broadcast(P)).then_inc(lut_in, 16)
            sp.dma_start(mask_row8, a["mask_row"]).then_inc(mask_in, 16)
            sp.dma_start(mask_n8, a["mask_n"]).then_inc(mask_in, 16)
            sp.wait_ge(wA_lo_ready, 2)
            sp.dma_start(stage[:, GB:GB + NWS], a["wS"]).then_inc(wS_in, 16)
            sp.dma_start(stage[0:E + 1, 0:NSEL], a["sel"]).then_inc(sel_in, 16)
            sp.wait_ge(setup_act, 2)
            with sp.Fori(0, GROUPS) as g:
                sp_A(sp, g)
            sp.wait_ge(setup_dve, 6)
            with sp.Fori(0, GROUPS) as g:
                sp_B(sp, g)
            with sp.Fori(0, GROUPS) as g:
                sp_C(sp, g)
            with sp.Fori(0, GROUPS) as g:
                sp_D(sp, g)
            sp.wait_ge(out_done, 16 * GROUPS)

        @block.tensor
        def _(pe):
            pe.wait_ge(const_in, 16)
            pe.wait_ge(wA_lo_ready, 2)
            pe_A_start(pe)
            with pe.Fori(0, GROUPS - 2) as g:
                pe_A(pe, g, True, True)
            pe_A(pe, GROUPS - 2, True, False)
            pe_A(pe, GROUPS - 1, False, False)
            pe.wait_ge(setup_dve, 6)
            pe.wait_ge(setup_act, 2)
            pe.wait_ge(*A["x_done"].at(GROUPS, 0))
            with pe.Fori(0, GROUPS) as g:
                pe_B(pe, g)
            pe.wait_ge(*Bp["x_done"].at(GROUPS, 0))
            with pe.Fori(0, GROUPS) as g:
                pe_C(pe, g)
            pe.wait_ge(*C["dec_lo"].at(GROUPS, 0))
            pe.wait_ge(*C["x_done"].at(GROUPS, 0))
            with pe.Fori(0, GROUPS - 1) as g:
                pe_D(pe, g, True)
            pe_D(pe, GROUPS - 1, False)

        @block.scalar
        def _(act):
            act.wait_ge(centred, 3)
            nc.scalar.copy(wA_hi[:, 0:NWC], stage[:, 0:NWC]).then_inc(wA_hi_ready, 1)
            act.wait_ge(wA2_in, 16)
            nc.scalar.copy(wA_hi[:, NWC:], stage[:, NWC:NWA]).then_inc(wA_hi_ready, 1)
            act.wait_ge(ctxT_in, 16)
            act.wait_ge(const_in, 16)
            act.wait_ge(setup_pool, 4)
            act_A_start(act)
            act.wait_ge(gates_in, 16)
            nc.scalar.activation(tg, gates, ACT.Tanh).then_inc(setup_act, 1)
            with act.Fori(0, GROUPS - 2) as g:
                act_A(act, g, True, True)
            act_A(act, GROUPS - 2, True, False)
            act_A(act, GROUPS - 1, False, False)
            act.wait_ge(*A["x_done"].at(GROUPS, 0))
            with act.Fori(0, GROUPS) as g:
                act_B(act, g)
            act.wait_ge(setup_dve, 6)
            act.wait_ge(*Bp["x_done"].at(GROUPS, 0))
            with act.Fori(0, GROUPS) as g:
                act_C(act, g)
            act.wait_ge(*C["x_done"].at(GROUPS, 0))
            with act.Fori(0, GROUPS - 1) as g:
                act_D(act, g, True)
            act_D(act, GROUPS - 1, False)

        @block.vector
        def _(dve):
            for signal, n in free_at_start:
                dve.sem_inc(signal, n)
            dve_A_start(dve)
            with dve.Fori(0, GROUPS - 2) as g:
                dve_A(dve, g, True, True)
            dve_A(dve, GROUPS - 2, True, False)
            dve_A(dve, GROUPS - 1, False, False)
            dve.wait_ge(const_in, 16)
            with dve.Fori(0, GROUPS) as g:
                dve_B(dve, g)
            pad = [w[:, :, INTER:FC * P].bitcast(F32) for w in (fg_hi, fg_lo, fu_hi, fu_lo)]
            for w in pad:
                nc.vector.memset(w, 0.0).then_inc(setup_dve, 1)
            with dve.Fori(0, GROUPS) as g:
                dve_C(dve, g)
            with dve.Fori(0, GROUPS - 1) as g:
                dve_D(dve, g, True)
            dve_D(dve, GROUPS - 1, False)

        @block.gpsimd
        def _(pool):
            nc.gpsimd.memset(expo, -0.5).then_inc(setup_pool, 1)
            nc.gpsimd.memset(workAr[:, 0:4 * TG].bitcast(F32), 0.0).then_inc(setup_pool, 1)
            nc.gpsimd.memset(kx.rearrange("p k a n -> p (k a n)"), 0.0).then_inc(setup_pool, 1)
            nc.gpsimd.memset(vz.rearrange("p t k b n -> p (t k b n)"), 0.0).then_inc(setup_pool, 1)
            pool.wait_ge(setup_pool, 4)
            pool_A_start(pool)
            with pool.Fori(0, GROUPS - 2) as g:
                pool_A(pool, g, True, True)
            pool_A(pool, GROUPS - 2, True, False)
            pool_A(pool, GROUPS - 1, False, False)
            pool.wait_ge(*A["x_done"].at(GROUPS, 0))
            with pool.Fori(0, GROUPS) as g:
                pool_B(pool, g)
            pool.wait_ge(setup_dve, 6)
            pool.wait_ge(*Bp["x_done"].at(GROUPS, 0))
            with pool.Fori(0, GROUPS) as g:
                pool_C(pool, g)
            pool.wait_ge(*C["x_done"].at(GROUPS, 0))
            with pool.Fori(0, GROUPS - 1) as g:
                pool_D(pool, g, True)
            pool_D(pool, GROUPS - 1, False)

        for name, phase, times in (("A", A, 3), ("B", Bp, 1), ("C", C, 1), ("D", Dp, 2)):
            for key, s in phase.items():
                assert s.n == times * s.per_group, (name, key, s.n, s.per_group)


def laid_out(i):
    f = {}
    f["x"] = i["x"].reshape(GROUPS * TILES, P, D)
    c = i["ctx_1024"].reshape(B * S, DV)
    f["ctx_T"] = c.T
    f["ctx_n"] = c.reshape(GROUPS * TILES, P, DV)

    def chunks(w):
        return w.reshape(-1, P, w.shape[1]).transpose(1, 0, 2).reshape(P, -1)

    def by_head(w):
        return w.reshape(w.shape[:-1] + (H0, 2, HD0)).swapaxes(-3, -2).reshape(w.shape)

    wkv = by_head(np.concatenate([i["L0_xattn_Wk"], i["L0_xattn_Wv"]], axis=1))
    wkv = np.stack([wkv.reshape(DV, 2, D), i["L0_xattn_Wkv_dca"].reshape(DV, 2, D)], axis=2).reshape(DV, -1)
    f["wA"] = np.concatenate([chunks(i["L0_xattn_Wq"]), wkv, chunks(i["L0_xattn_Wo"])], axis=1)
    f["vec"] = np.concatenate([i["L0_xattn_bq"], i["L0_xattn_bo"]])
    bkv = by_head(np.concatenate([i["L0_xattn_bk"], i["L0_xattn_bv"]]))
    f["vec_main"], f["vec_last"] = bkv, i["L0_xattn_bkv_dca"]
    f["cols"] = np.stack([np.tile(i[f"L0_xattn_{n}"], P // HD0)
                          for n in ("qn_w", "qn_b", "kn_w", "kn_b", "kn_dca_w", "kn_dca_b")], axis=1)
    f["gates"] = np.stack([i["g_xattn"], i["g_ffn"]], axis=1).reshape(-1)
    parts = []
    for w in (i["L0_ffn_Wg"], i["L0_ffn_Wu"]):
        parts.append(w.reshape(GROUPS, 4, DC, P, F).transpose(0, 3, 2, 1, 4).reshape(GROUPS, P, -1))
    parts.append(i["L0_ffn_Wd"].reshape(GROUPS, 2, P, D).transpose(0, 2, 1, 3).reshape(GROUPS, P, -1))
    f["wB"] = np.concatenate(parts, axis=2)
    sgu = chunks(np.concatenate([i["L0_ffn_sWg"], i["L0_ffn_sWu"]], axis=1))
    sd = np.concatenate([i["L0_ffn_sWd"], np.zeros_like(i["L0_ffn_sWd"])])
    router = np.concatenate([i["L0_ffn_gate_w"].T, i["L0_ffn_shared_gate_w"],
                             np.zeros_like(i["L0_ffn_shared_gate_w"])], axis=1)
    f["wS"] = np.concatenate([sgu, sd, chunks(router)], axis=1)
    q = i["L1_xattn_Wq"].reshape(D, GROUPS, HG, HD1).transpose(1, 3, 2, 0).reshape(GROUPS, P, -1)
    k, v = (i[n].reshape(DV, GROUPS, HG // 2, HD1).transpose(1, 3, 2, 0).reshape(GROUPS, P, -1)
            for n in ("L1_xattn_Wk", "L1_xattn_Wv"))
    o = i["L1_xattn_Wo"].reshape(GROUPS, HG, HD1, D).transpose(0, 2, 1, 3).reshape(GROUPS, P, -1)
    f["wC"] = np.concatenate([q, k, v, o], axis=2)
    up = [i[n].T.reshape(DC, P, GROUPS, IG).transpose(2, 1, 0, 3).reshape(GROUPS, P, -1)
          for n in ("L1_ffn_gate_idx", "L1_ffn_up_idx")]
    d = i["L1_ffn_down_idx"].T
    d = np.concatenate([d, np.zeros((FC * P - INTER, D), d.dtype)]).reshape(FC, P, GROUPS, DG)
    f["idx"] = np.concatenate(up + [d.transpose(2, 1, 0, 3).reshape(GROUPS, P, -1)], axis=2)
    f["lut"] = i["L1_ffn_lut"]
    m = i["mask_BxS2_bf1"].view(np.uint8)
    f["mask_row"] = m.reshape(1, B * S)
    f["mask_n"] = m.reshape(GROUPS * TILES, P).T
    const = np.zeros((P, NCONST), np.float32)
    const[:, 0:P] = np.eye(P)
    const[:, P] = np.arange(P) // HD0 % 2 == 0
    const[:, P + 1] = np.arange(P) // HD0 % 2 == 1
    const[:, P + 2:P + 2 + E] = np.arange(E)
    f["const"] = const
    sel = np.zeros((E + 1, EC + 1, P), np.float32)
    for k_ in range(EC):
        for e in range(2):
            sel[2 * k_ + e, k_, e * F:(e + 1) * F] = 1
    sel[E, EC, :] = 1
    f["sel"] = sel.reshape(E + 1, NSEL)
    return {k_: np.ascontiguousarray(v_) for k_, v_ in f.items()}


def kernel(**inputs):
    import concourse.bacc as bacc
    from concourse.bass_utils import run_bass_kernel_spmd

    arrays = laid_out({k: np.asarray(v) for k, v in inputs.items()})
    nc = bacc.Bacc("TRN2", target_bir_lowering=False, num_devices=1)
    a = {k: nc.dram_tensor(f"in_{k}", v.shape, mybir.dt.from_np(v.dtype), kind="ExternalInput").ap()
         for k, v in arrays.items()}
    a["out"] = nc.dram_tensor("out", (GROUPS * TILES, P, D), F32, kind="ExternalOutput").ap()
    build(nc, a)
    r = run_bass_kernel_spmd(nc, [{f"in_{k}": v for k, v in arrays.items()}], core_ids=[0])
    return r.results[0]["out"].reshape(B, S, D)
```
